# Optimizing a Trainium2 kernel written in Bass

```python
import numpy as np
import jax
import jax.numpy as jnp

def _softmax(x, axis=-1):
    return jax.nn.softmax(x, axis=axis)

def _gelu(x):
    return jax.nn.gelu(x, approximate=True)

def _silu(x):
    return jax.nn.silu(x)

def _sigmoid(x):
    return jax.nn.sigmoid(x)

def _layernorm(x, axis=-1, eps=1e-05):
    m = jnp.mean(x, axis=axis, keepdims=True)
    v = jnp.var(x, axis=axis, keepdims=True)
    return (x - m) / jnp.sqrt(v + eps)

def _scatter_add(tgt, idx, src, axis=0):
    return tgt.at[idx].add(src)

def _segment_sum(src, seg, n):
    return jax.ops.segment_sum(src, seg, n)
kernel_name = 'mk_gnn_preln_d2_gnn_r32_b37773'

def setup_inputs(seed: int=0):
    np.random.seed(seed)
    _w = jnp.asarray

    def _rec_inputs():
        import jax
        import jax.numpy as jnp
        _gk = jax.random.key(seed)
        x = -0.0003713 + 1 * jax.random.normal(jax.random.fold_in(_gk, 1), (3125, 256), jnp.float32)
        src = jax.random.randint(jax.random.fold_in(_gk, 2), (50000,), 0, 3125, jnp.int32)
        dst = jnp.minimum((3125 * jax.random.uniform(jax.random.fold_in(_gk, 3), (50000,)) ** 2.0).astype(jnp.int32), 99999)
        _o = jnp.argsort(dst, stable=True)
        src = src[_o]
        dst = dst[_o]
        edge_weight = jax.random.uniform(jax.random.fold_in(_gk, 12), (50000,), jnp.float32, 0.0, 0.999998)
        edge_weight_n2 = jax.random.uniform(jax.random.fold_in(_gk, 13), (50000,), jnp.float32, 0.0, 0.999998)
        return (x, src, dst, edge_weight, edge_weight_n2)
    x, src, dst, edge_weight, edge_weight_n2 = _rec_inputs()

    def _L0_gnn_setup():
        import jax, jax.numpy as jnp
        import numpy as np
        N = 50000
        E_RAND = 25000
        IN_DIM = 256
        HID = 64
        HEADS = 4
        OUT_DIM = 256
        NEG_SLOPE = 0.01

        def _xavier(key, shape, fan_in, fan_out):
            gain = np.sqrt(2.0)
            std = gain * np.sqrt(2.0 / (fan_in + fan_out))
            return jax.random.normal(key, shape, dtype=jnp.float32) * std

        def _leaky(x):
            return jnp.where(x > 0, x, NEG_SLOPE * x)

        def _segment_softmax(e, dst, n):
            m = jax.ops.segment_max(e, dst, num_segments=n)
            m = jnp.where(jnp.isfinite(m), m, 0.0)
            ex = jnp.exp(e - m[dst])
            s = jax.ops.segment_sum(ex, dst, num_segments=n)
            return ex / s[dst]
        key = jax.random.key(seed)
        k = jax.random.split(key, 8)
        h = jax.random.normal(k[0], (N, IN_DIM), dtype=jnp.float32)
        src = jnp.concatenate([jax.random.randint(k[1], (E_RAND,), 0, N), jnp.arange(N)]).astype(jnp.int32)
        dst = jnp.concatenate([jax.random.randint(k[2], (E_RAND,), 0, N), jnp.arange(N)]).astype(jnp.int32)
        W1 = _xavier(k[3], (HEADS, HID, IN_DIM), IN_DIM, HID)
        a1 = _xavier(k[4], (HEADS, 2 * HID), 2 * HID, 1)
        W2 = _xavier(k[5], (OUT_DIM, HID * HEADS), HID * HEADS, OUT_DIM)
        a2 = _xavier(k[6], (2 * OUT_DIM,), 2 * OUT_DIM, 1)
        return {'h': h, 'W1': W1, 'a1': a1, 'W2': W2, 'a2': a2, 'src': src, 'dst': dst}
    _L0_gnn_all = _L0_gnn_setup()
    _L0_gnn_in = {k: v for k, v in _L0_gnn_all.items() if k in ('W1', 'a1', 'W2', 'a2')}
    del _L0_gnn_all

    def _L1_gnn_setup():
        import jax, jax.numpy as jnp
        import numpy as np
        N_NODES = 3125
        N_EDGES = 25000
        DIM = 256
        EPS = 1e-05
        key = jax.random.key(seed)
        ks = jax.random.split(key, 12)
        H = DIM
        s = 1.0 / np.sqrt(H)
        s2 = 1.0 / np.sqrt(2 * H)
        return {'feat': jax.random.normal(ks[0], (N_NODES, DIM), dtype=jnp.float32), 'src': jax.random.randint(ks[1], (N_EDGES,), 0, N_NODES, dtype=jnp.int32), 'dst': jax.random.randint(ks[2], (N_EDGES,), 0, N_NODES, dtype=jnp.int32), 'iw': jax.random.uniform(ks[3], (N_EDGES,), dtype=jnp.float32), 'ow': jax.random.uniform(ks[4], (N_EDGES,), dtype=jnp.float32), 'gamma': jnp.ones((DIM,), jnp.float32), 'beta': jnp.zeros((DIM,), jnp.float32), 'W_in': jax.random.uniform(ks[5], (H, H), jnp.float32, -s, s), 'b_in': jax.random.uniform(ks[6], (H,), jnp.float32, -s, s), 'W_out': jax.random.uniform(ks[7], (H, H), jnp.float32, -s, s), 'b_out': jax.random.uniform(ks[8], (H,), jnp.float32, -s, s), 'W_x2i': jax.random.uniform(ks[9], (2 * H, 2 * H), jnp.float32, -s2, s2), 'b_x2i': jax.random.uniform(ks[10], (2 * H,), jnp.float32, -s2, s2), 'W_h2h': jax.random.uniform(ks[11], (H, 2 * H), jnp.float32, -s, s)}
    _L1_gnn_all = _L1_gnn_setup()
    _L1_gnn_in = {k: v for k, v in _L1_gnn_all.items() if k in ('gamma', 'beta', 'W_in', 'b_in', 'W_out', 'b_out', 'W_x2i', 'b_x2i', 'W_h2h')}
    del _L1_gnn_all
    return {'x': x, 'src': src, 'dst': dst, 'edge_weight': edge_weight, 'edge_weight_n2': edge_weight_n2, 'L0_gnn_W1': _L0_gnn_in['W1'], 'L0_gnn_a1': _L0_gnn_in['a1'], 'L0_gnn_W2': _L0_gnn_in['W2'], 'L0_gnn_a2': _L0_gnn_in['a2'], 'L1_gnn_gamma': _L1_gnn_in['gamma'], 'L1_gnn_beta': _L1_gnn_in['beta'], 'L1_gnn_W_in': _L1_gnn_in['W_in'], 'L1_gnn_b_in': _L1_gnn_in['b_in'], 'L1_gnn_W_out': _L1_gnn_in['W_out'], 'L1_gnn_b_out': _L1_gnn_in['b_out'], 'L1_gnn_W_x2i': _L1_gnn_in['W_x2i'], 'L1_gnn_b_x2i': _L1_gnn_in['b_x2i'], 'L1_gnn_W_h2h': _L1_gnn_in['W_h2h']}

def reference(x, src, dst, edge_weight, edge_weight_n2, L0_gnn_W1, L0_gnn_a1, L0_gnn_W2, L0_gnn_a2, L1_gnn_gamma, L1_gnn_beta, L1_gnn_W_in, L1_gnn_b_in, L1_gnn_W_out, L1_gnn_b_out, L1_gnn_W_x2i, L1_gnn_b_x2i, L1_gnn_W_h2h):
    import jax
    import jax.numpy as jnp

    def _L0_gnn_ref(h, W1, a1, W2, a2, src, dst):
        import jax, jax.numpy as jnp
        import numpy as np
        N = 50000
        E_RAND = 25000
        IN_DIM = 256
        HID = 64
        HEADS = 4
        OUT_DIM = 256
        NEG_SLOPE = 0.01

        def _xavier(key, shape, fan_in, fan_out):
            gain = np.sqrt(2.0)
            std = gain * np.sqrt(2.0 / (fan_in + fan_out))
            return jax.random.normal(key, shape, dtype=jnp.float32) * std

        def _leaky(x):
            return jnp.where(x > 0, x, NEG_SLOPE * x)

        def _segment_softmax(e, dst, n):
            m = jax.ops.segment_max(e, dst, num_segments=n)
            m = jnp.where(jnp.isfinite(m), m, 0.0)
            ex = jnp.exp(e - m[dst])
            s = jax.ops.segment_sum(ex, dst, num_segments=n)
            return ex / s[dst]
        n = h.shape[0]
        z = jnp.einsum('ni,hoi->nho', h, W1)
        a_s, a_d = (a1[:, :HID], a1[:, HID:])
        es = jnp.einsum('nho,ho->nh', z, a_s)
        ed = jnp.einsum('nho,ho->nh', z, a_d)
        e = _leaky(es[src] + ed[dst])
        alpha = _segment_softmax(e, dst, n)
        m = jax.ops.segment_sum(alpha[:, :, None] * z[src], dst, num_segments=n)
        h1 = jax.nn.elu(m.reshape(n, HEADS * HID))
        z2 = h1 @ W2.T
        e2 = _leaky((z2 @ a2[:OUT_DIM])[src] + (z2 @ a2[OUT_DIM:])[dst])
        alpha2 = _segment_softmax(e2, dst, n)
        out = jax.ops.segment_sum(alpha2[:, None] * z2[src], dst, num_segments=n)
        return out

    def _L1_gnn_ref(feat, src, dst, iw, ow, gamma, beta, W_in, b_in, W_out, b_out, W_x2i, b_x2i, W_h2h):
        import jax, jax.numpy as jnp
        import numpy as np
        N_NODES = 3125
        N_EDGES = 25000
        DIM = 256
        EPS = 1e-05
        N = feat.shape[0]
        num_steps = 1
        mean = jnp.mean(feat, axis=0)
        var = jnp.var(feat, axis=0)
        h = (feat - mean) * jax.lax.rsqrt(var + EPS) * gamma + beta
        for _ in range(num_steps):
            feat_in = h @ W_in + b_in
            feat_out = h @ W_out + b_out
            a_in = jax.ops.segment_sum(feat_in[src] * iw[:, None], dst, num_segments=N)
            a_out = jax.ops.segment_sum(feat_out[dst] * ow[:, None], src, num_segments=N)
            a = jnp.concatenate((a_in, a_out), axis=1)
            xi = a @ W_x2i + b_x2i
            hh = h @ W_h2h
            i_i, i_n = jnp.split(xi, 2, axis=1)
            h_i, h_n = jnp.split(hh, 2, axis=1)
            input_gate = jax.nn.sigmoid(i_i + h_i)
            new_gate = jnp.tanh(i_n + h_n)
            h = new_gate + input_gate * (h - new_gate)
        return h
    h = jnp.maximum(_layernorm(x, axis=-1), 0.0)
    x = x + _L0_gnn_ref(h, L0_gnn_W1, L0_gnn_a1, L0_gnn_W2, L0_gnn_a2, src, dst)
    h = jnp.maximum(_layernorm(x, axis=-1), 0.0)
    x = x + _L1_gnn_ref(h, src, dst, edge_weight, edge_weight_n2, L1_gnn_gamma, L1_gnn_beta, L1_gnn_W_in, L1_gnn_b_in, L1_gnn_W_out, L1_gnn_b_out, L1_gnn_W_x2i, L1_gnn_b_x2i, L1_gnn_W_h2h)
    return x

_drawn_inputs = setup_inputs


def setup_inputs(seed=0):
    import zlib

    import numpy as np

    out = dict(_drawn_inputs(seed))
    spreads = {'L1_gnn_gamma': (1.0, 0.2), 'L1_gnn_beta': (0.0, 0.1)}
    factors = {'L1_gnn_b_x2i': 8.0}
    for name, (base, spread) in spreads.items():
        noise = np.random.default_rng([zlib.crc32(name.encode()), seed]).standard_normal(out[name].shape)
        drawn = base * np.exp(spread * noise) if base else spread * noise
        out[name] = jnp.asarray(drawn.astype(out[name].dtype))
    for name, factor in factors.items():
        out[name] = (out[name] * factor).astype(out[name].dtype)
    return out
```

```python
import concourse.bass as bass
from concourse import mybir
from contextlib import ExitStack, contextmanager

F32, I32, BF16, U32 = mybir.dt.float32, mybir.dt.int32, mybir.dt.bfloat16, mybir.dt.uint32
ALU, ACT, AX = mybir.AluOpType, mybir.ActivationFunctionType, mybir.AxisListType

N, D, E = 3125, 256, 50000
HEADS, HID = 4, 64
TN = 125
NT = N // TN
CH = 128
SH = 14
EC = 392
EP = EC * CH
IQ, IP = 4, 104
NI = IQ * IP
G = 8
NG = NI // G
PAD_KEY = 4000.0
BIG = 1e30
ROUND = 12582912.0
EPS = 1e-5
assert NI >= EC + NT - 1 and EC % (2 * SH) == 0 and EP >= E


class Chain:

    def __init__(self, eng, sem):
        self.eng, self.sem, self.done, self.here, self.turn, self.per = eng, sem, 0, 0, None, 0

    def value(self):
        return self.done + self.here if self.turn is None else self.turn * self.per + (self.done + self.here)

    def __call__(self, ins):
        ins.then_inc(self.sem, 1)
        self.here += 1
        self.eng.wait_ge(self.sem, self.value())

    @contextmanager
    def loop(self, turns, per):
        self.done, self.here = self.done + self.here, 0
        with self.eng.Fori(0, turns) as i:
            self.turn, self.per = i, per
            yield i
            assert self.here == per, (self.here, per)
        self.turn, self.done, self.here = None, self.done + turns * per, 0


def build(nc, x, src, dst, edge_weight, edge_weight_n2, W1, a1, W2, a2, gamma, beta,
          W_in, b_in, W_out, b_out, W_x2i, b_x2i, W_h2h, out):
    ctx = ExitStack()
    with ctx:
        held = []

        def sem(name):
            held.append(nc.alloc_semaphore(name=name))
            return held[-1]

        def end_stage():
            with nc.Block() as block:
                @block.gpsimd
                def _(pool):
                    nc.clear_and_free_semaphores(held)
            held.clear()

        def sb(name, shape, dt=F32, scope=ctx):
            return scope.enter_context(nc.sbuf_tensor(name, shape, dt))

        def dram(name, shape, dt=F32):
            return nc.dram_tensor(name, shape, dt, kind="Internal").ap()

        rec_half = dram("rec_half", (EC * CH, 4))
        rec_src = dram("rec_src", (EC * CH, 4))
        rec_dst = dram("rec_dst", (EC * CH, 4))
        row_local = dram("row_local", (NI * CH,), BF16)
        row_other = dram("row_other", (NI * CH,), BF16)
        tile_tab = [dram(f"tile_tab{i}", (NI,), I32) for i in range(2)]
        edge_tab = [dram(f"edge_tab{i}", (4, IP)) for i in range(2)]
        z_tab, z2_tab = dram("z_tab", (N, D)), dram("z2_tab", (N, D))
        fin_tab, fout_tab = dram("fin_tab", (N, D)), dram("fout_tab", (N, D))

        bank = [ctx.enter_context(nc.psum_tensor(f"bank{i}", [128, 512], F32)) for i in range(8)]

        part = sb("part", [128, 1])
        col = sb("col", [128, 128])
        item_no = sb("item_no", [128, IQ])
        ident = sb("ident", [128, 128])
        below = sb("below", [128, 128])
        ones = sb("ones", [128, 128])
        eps = sb("eps", [128, 1])
        x_sb = sb("x_sb", [TN, NT, D])
        acc = sb("acc", [TN, NT * (D + HEADS)])
        s_iota, s_const, s_x = sem("s_iota"), sem("s_const"), sem("s_x")
        with nc.Block() as block:
            @block.sync
            def _(sp):
                sp.dma_start(x_sb[:], x.rearrange("(t p) d -> p t d", p=TN)).then_inc(s_x, 16)
                sp.wait_ge(s_x, 16)

            @block.gpsimd
            def _(pool):
                nc.gpsimd.iota(part[:], [[0, 1]], base=0, channel_multiplier=1,
                               allow_small_or_imprecise_dtypes=True).then_inc(s_iota, 1)
                nc.gpsimd.iota(col[:], [[1, 128]], base=0, channel_multiplier=0,
                               allow_small_or_imprecise_dtypes=True).then_inc(s_iota, 1)
                nc.gpsimd.iota(item_no[:], [[1, IQ]], base=0, channel_multiplier=IQ,
                               allow_small_or_imprecise_dtypes=True).then_inc(s_iota, 1)

            @block.vector
            def _(dve):
                nc.vector.memset(ones[:], 1.0)
                nc.vector.memset(eps[:], EPS)
                dve.wait_ge(s_iota, 3)
                nc.vector.tensor_scalar(ident[:], col[:], part[:], None, ALU.is_equal)
                nc.vector.tensor_scalar(below[:], col[:], part[:], None, ALU.is_gt)

        cnt_s = sb("cnt_s", [128, NT])
        cnt_d = sb("cnt_d", [128, NT])
        with ExitStack() as scope:
            rec = sb("rec", [128, EC, 4], scope=scope)
            key_i = sb("key_i", [128, EC], I32, scope)
            oth_i = sb("oth_i", [128, EC], I32, scope)
            wgt = sb("wgt", [128, EC], F32, scope)
            digit = sb("digit", [128, EC], F32, scope)
            equal = sb("equal", [128, EC], F32, scope)
            rank = sb("rank", [128, EC], F32, scope)
            place = sb("place", [128, EC], F32, scope)
            place_i = sb("place_i", [128, EC], I32, scope)
            stage_p = sb("stage_p", [128, 2, SH], I32, scope)
            stage_r = sb("stage_r", [128, 2, SH, 4], F32, scope)
            tot = sb("tot", [128, 128], F32, scope)
            cnt = sb("cnt", [128, 128], F32, scope)
            incl = sb("incl", [128, 128], F32, scope)
            off = sb("off", [128, 128], F32, scope)

            def load_edges(name, key, other, weight):
                s_pad, s_in, s_c = sem(name + "_pad"), sem(name + "_in"), sem(name + "_c")
                full = E // EC
                rest = E - full * EC
                with nc.Block() as block:
                    @block.sync
                    def _(sp):
                        sp.wait_ge(s_pad, 3)
                        for t, a in ((key_i, key), (oth_i, other), (wgt, weight)):
                            sp.dma_start(t[0:full, :], a[0:full * EC].rearrange("(p j) -> p j", j=EC)).then_inc(s_in, 16)
                            sp.dma_start(t[full:full + 1, 0:rest],
                                         a[full * EC:E].rearrange("(o j) -> o j", o=1)).then_inc(s_in, 16)
                        sp.wait_ge(s_in, 96)

                    @block.vector
                    def _(dve):
                        nc.vector.memset(key_i[:], int(PAD_KEY)).then_inc(s_pad, 1)
                        nc.vector.memset(oth_i[:], 0).then_inc(s_pad, 1)
                        nc.vector.memset(wgt[:], 0.0).then_inc(s_pad, 1)
                        nc.vector.memset(rec[:], 0.0).then_inc(s_c, 1)
                        dve.wait_ge(s_c, 1)
                        dve.wait_ge(s_in, 96)
                        nc.vector.tensor_copy(rec[:, :, 0], key_i[:])
                        nc.vector.tensor_copy(rec[:, :, 1], oth_i[:])
                        nc.vector.tensor_copy(rec[:, :, 2], wgt[:])

            def radix(name, low, buckets, to, reload=None):
                s_c, s_in, s_tot, s_sum, s_off = (sem(name + k) for k in ("_c", "_in", "_tot", "_sum", "_off"))
                s_turn = sem(name + "_turn")
                s_place, s_stage, s_free = sem(name + "_place"), sem(name + "_stage"), [sem(name + f"_free{h}") for h in range(2)]
                with nc.Block() as block:
                    @block.sync
                    def _(sp):
                        if reload is not None:
                            sp.dma_start(rec[:], reload.rearrange("(p j) f -> p j f", p=128)).then_inc(s_in, 16)
                            sp.wait_ge(s_in, 16)

                    @block.vector
                    def _(dve):
                        c = Chain(dve, s_c)
                        if reload is not None:
                            dve.wait_ge(s_in, 16)
                        c(nc.vector.tensor_scalar(digit[:], rec[:, :, 0], 1.0 / TN, -0.496, ALU.mult, ALU.add))
                        c(nc.vector.tensor_scalar(digit[:], digit[:], ROUND, ROUND, ALU.add, ALU.subtract))
                        c(nc.vector.tensor_scalar(digit[:], digit[:], float(NT - 1), None, ALU.min))
                        if low:
                            c(nc.vector.scalar_tensor_tensor(digit[:], digit[:], -float(TN), rec[:, :, 0], ALU.mult, ALU.add))
                            c(nc.vector.tensor_scalar(digit[:], digit[:], float(TN - 1), None, ALU.min))
                        with c.loop(buckets, 1) as b:
                            c(nc.vector.tensor_scalar(equal[:], digit[:], col[:, bass.ds(b, 1)], 0.0, ALU.is_equal, ALU.add,
                                                      accum_out=tot[:, bass.ds(b, 1)]))
                        c(nc.vector.tensor_copy(cnt[:, 0:1], tot[:, 0:1]))
                        dve.drain().then_inc(s_tot, 1)
                        dve.wait_ge(s_sum, 1)
                        ps = bank[0]
                        c(nc.vector.tensor_copy(cnt[:, 0:buckets], ps[:, 128:128 + buckets]))
                        c(nc.vector.tensor_tensor_scan(incl[:, 0:buckets], cnt[:, 0:buckets], cnt[:, 0:buckets], 0.0, ALU.add, ALU.bypass))
                        c(nc.vector.tensor_tensor(off[:, 0:buckets], incl[:, 0:buckets], cnt[:, 0:buckets], ALU.subtract))
                        c(nc.vector.scalar_tensor_tensor(off[:, 0:buckets], off[:, 0:buckets], -1.0, ps[:, 0:buckets], ALU.add, ALU.add))
                        c(nc.vector.memset(place[:], 0.0))
                        with c.loop(buckets, 3) as b:
                            c(nc.vector.tensor_scalar(equal[:], digit[:], col[:, bass.ds(b, 1)], None, ALU.is_equal))
                            c(nc.vector.tensor_tensor_scan(rank[:], equal[:], equal[:], off[:, bass.ds(b, 1)], ALU.add, ALU.bypass))
                            dve.sem_inc(s_turn, 1)
                            c(nc.vector.copy_predicated(place[:], equal[:].bitcast(U32), rank[:]))
                        c(nc.vector.tensor_copy(place_i[:], place[:]))
                        dve.drain().then_inc(s_place, 1)

                    @block.tensor
                    def _(pe):
                        pe.wait_ge(s_tot, 1)
                        nc.tensor.matmul(bank[0][:, 0:buckets], below[:], tot[:, 0:buckets], start=True, stop=True)
                        nc.tensor.matmul(bank[0][:, 128:128 + buckets], ones[:], tot[:, 0:buckets], start=True, stop=True)
                        pe.drain().then_inc(s_sum, 1)

                    @block.gpsimd
                    def _(pool):
                        pool.wait_ge(s_place, 1)

                        def round_(g, h, first):
                            if not first:
                                pool.wait_ge(s_free[h], (g // 2 if isinstance(g, int) else g) * 16 * SH)
                            at = (g * 2 + h) * SH if not isinstance(g, int) else h * SH
                            nc.gpsimd.tensor_copy(stage_p[:, h, :], place_i[:, bass.ds(at, SH)]).then_inc(s_stage, 1)
                            nc.gpsimd.tensor_copy(stage_r[:, h, :, :].rearrange("p a f -> p (a f)"),
                                                  rec[:].rearrange("p j f -> p (j f)")[:, bass.ds(at * 4, SH * 4)]).then_inc(s_stage, 1)
                            pool.wait_ge(s_stage, g * 4 + 2 * h + 2)
                            pool.sem_inc(s_turn, 1)
                            for k in range(SH):
                                nc.gpsimd.indirect_dma_start(to, bass.IndirectOffsetOnAxis(ap=stage_p[:, h, k:k + 1], axis=0),
                                                             stage_r[:, h, k, :], None).then_inc(s_free[h], 16)

                        for h in range(2):
                            round_(0, h, True)
                        with pool.Fori(1, EC // (2 * SH)) as g:
                            for h in range(2):
                                round_(g, h, False)
                        for h in range(2):
                            pool.wait_ge(s_free[h], EC // 2 * 16)

            load_edges("ls", src, dst, edge_weight_n2)
            end_stage()
            radix("rs", False, NT, rec_src)
            end_stage()
            with nc.Block() as block:
                @block.vector
                def _(dve):
                    nc.vector.tensor_copy(cnt_s[:], cnt[:, 0:NT])
            load_edges("ld", dst, src, edge_weight)
            end_stage()
            radix("rl", True, TN, rec_half)
            end_stage()
            radix("rh", False, NT, rec_dst, reload=rec_half)
            end_stage()
            with nc.Block() as block:
                @block.vector
                def _(dve):
                    nc.vector.tensor_copy(cnt_d[:], cnt[:, 0:NT])

        def item_arrays(name):
            return {"local": sb(name + "_local", [128, NI]), "index": sb(name + "_index", [128, NI], I32),
                    "weight": sb(name + "_weight", [128, NI]), "tiles": sb(name + "_tiles", [1, NI], I32)}

        it_s, it_d = item_arrays("src"), item_arrays("dst")
        high = sb("high", [128, NI])
        same_f = sb("same_f", [IP, IQ * CH])
        same_b = sb("same_b", [IP, IQ * CH])
        link = sb("link", [IP, 4])

        def items(name, which, recs, counts, it, attention):
            with ExitStack() as scope:
                t25 = [sb(f"{name}_b{i}", [128, NT], F32, scope) for i in range(8)]
                start, end, sc, ec, n, ib, dl, tmp = t25
                ge = sb(name + "_ge", [IP, IQ, NT], F32, scope)
                gd = sb(name + "_gd", [IP, IQ, NT], F32, scope)
                tcol = sb(name + "_tcol", [IP, IQ], F32, scope)
                jcol = sb(name + "_jcol", [IP, IQ], F32, scope)
                tcol_i = sb(name + "_tcol_i", [IP, IQ], I32, scope)
                jcol_i = sb(name + "_jcol_i", [IP, IQ], I32, scope)
                rows = sb(name + "_rows", [IP, IQ, CH * 4], F32, scope)
                loc = sb(name + "_loc", [IP, IQ, CH], F32, scope)
                oth = sb(name + "_oth", [IP, IQ, CH], F32, scope)
                wg = sb(name + "_wg", [IP, IQ, CH], F32, scope)
                hi = sb(name + "_hi", [IP, IQ, CH], F32, scope)
                lo = sb(name + "_lo", [IP, IQ, CH], F32, scope)
                loc_b = sb(name + "_loc_b", [IP, IQ, CH], BF16, scope)
                lo_b = sb(name + "_lo_b", [IP, IQ, CH], BF16, scope)
                prev = sb(name + "_prev", [IP, 2], F32, scope)
                whole = sb(name + "_whole", [IP, 2], F32, scope)
                s_c, s_j, s_rows, s_t, s_tl, s_rw, s_tr, s_ed, s_b = (sem(name + k) for k in (
                    "_c", "_j", "_rows", "_t", "_tl", "_rw", "_tr", "_ed", "_b"))
                f = rows[:].rearrange("p q (s f) -> p q s f", f=4)
                key = f[:, :, :, 0]

                with nc.Block() as block:
                    @block.vector
                    def _(dve):
                        c = Chain(dve, s_c)
                        v = nc.vector

                        def floor128(o, i):
                            c(v.tensor_scalar(o[:], i[:], 1.0 / CH, -0.498, ALU.mult, ALU.add))
                            c(v.tensor_scalar(o[:], o[:], ROUND, ROUND, ALU.add, ALU.subtract))

                        c(v.tensor_tensor_scan(end[:], counts[:], counts[:], 0.0, ALU.add, ALU.bypass))
                        c(v.tensor_tensor(start[:], end[:], counts[:], ALU.subtract))
                        c(v.tensor_scalar(end[:], end[:], -1.0, None, ALU.add))
                        floor128(sc, start)
                        floor128(ec, end)
                        c(v.tensor_tensor(n[:], ec[:], sc[:], ALU.subtract))
                        c(v.tensor_scalar(tmp[:], counts[:], 0.0, None, ALU.is_gt))
                        c(v.scalar_tensor_tensor(n[:], n[:], 1.0, tmp[:], ALU.add, ALU.mult))
                        c(v.tensor_tensor_scan(ib[:], n[:], n[:], 0.0, ALU.add, ALU.bypass))
                        c(v.tensor_tensor(ib[:], ib[:], n[:], ALU.subtract))
                        c(v.tensor_tensor(tmp[:], sc[:], ib[:], ALU.subtract))
                        c(v.tensor_copy(dl[:], tmp[:]))
                        c(v.tensor_tensor(dl[:, 1:NT], tmp[:, 1:NT], tmp[:, 0:NT - 1], ALU.subtract))
                        c(v.tensor_tensor(ge[:], item_no[0:IP, :].unsqueeze(2).to_broadcast([IP, IQ, NT]),
                                          ib[0:IP, :].unsqueeze(1).to_broadcast([IP, IQ, NT]), ALU.is_ge))
                        c(v.tensor_reduce(tcol[:], ge[:], AX.X, ALU.add))
                        c(v.tensor_scalar(tcol[:], tcol[:], -1.0, None, ALU.add))
                        c(v.tensor_tensor(gd[:], ge[:], dl[0:IP, :].unsqueeze(1).to_broadcast([IP, IQ, NT]), ALU.mult))
                        c(v.tensor_reduce(jcol[:], gd[:], AX.X, ALU.add))
                        c(v.tensor_tensor(jcol[:], jcol[:], item_no[0:IP, :], ALU.add))
                        c(v.tensor_scalar(jcol[:], jcol[:], float(EC - 1), None, ALU.min))
                        c(v.tensor_copy(jcol_i[:], jcol[:]))
                        c(v.tensor_copy(tcol_i[:], tcol[:]))
                        dve.drain().then_inc(s_j, 1)
                        for q in range(IQ):
                            dve.wait_ge(s_rows, 16 * IQ)
                        c(v.scalar_tensor_tensor(loc[:], tcol[:].unsqueeze(2).to_broadcast([IP, IQ, CH]), -float(TN), key, ALU.mult, ALU.add))
                        c(v.tensor_scalar(oth[:], f[:, :, :, 1], float(N - 1), None, ALU.min))
                        c(v.tensor_scalar(hi[:], oth[:], 1.0 / TN, -0.496, ALU.mult, ALU.add))
                        c(v.tensor_scalar(hi[:], hi[:], ROUND, ROUND, ALU.add, ALU.subtract))
                        c(v.scalar_tensor_tensor(lo[:], hi[:], -float(TN), oth[:], ALU.mult, ALU.add))
                        c(v.tensor_copy(wg[:], f[:, :, :, 2]))
                        c(v.tensor_copy(loc_b[:], loc[:]))
                        c(v.tensor_copy(lo_b[:], lo[:]))
                        dve.drain().then_inc(s_rw, 1)
                        if attention:
                            k2 = key.rearrange("p q s -> p (q s)") if False else rows[:].rearrange("p q (s f) -> p (q s) f", f=4)[:, :, 0]
                            L = IQ * CH
                            c(v.memset(same_f[:], 1.0))
                            c(v.memset(same_b[:], 1.0))
                            c(v.tensor_tensor(same_f[:, 1:L], k2[:, 1:L], k2[:, 0:L - 1], ALU.not_equal))
                            c(v.tensor_tensor(same_b[:, 0:L - 1], k2[:, 1:L], k2[:, 0:L - 1], ALU.not_equal))
                            c(v.tensor_scalar(same_f[:], same_f[:], -BIG, None, ALU.mult))
                            c(v.tensor_scalar(same_b[:], same_b[:], -BIG, None, ALU.mult))
                            c(v.memset(prev[:], -5.0))
                            dve.drain().then_inc(s_b, 1)
                            dve.wait_ge(s_ed, 32 + 32)
                            c(v.tensor_tensor(link[:, 0:1], prev[:, 0:1], k2[:, 0:1], ALU.not_equal))
                            c(v.tensor_tensor(link[:, 1:2], prev[:, 1:2], k2[:, L - 1:L], ALU.not_equal))
                            c(v.tensor_tensor(whole[:, 0:1], k2[:, 0:1], k2[:, L - 1:L], ALU.not_equal))
                            c(v.tensor_scalar(link[:, 2:4], link[:, 0:2], whole[:, 0:1], None, ALU.max))
                            c(v.tensor_scalar(link[:], link[:], -BIG, None, ALU.mult))
                        dve.wait_ge(s_tr, 1)
                        for b, to in ((0, it["local"]), (1, it["index"]), (2, it["weight"]), (3, high)):
                            if b == 3 and not attention:
                                continue
                            v.tensor_copy(to[:].rearrange("e (p q) -> e q p", q=IQ),
                                          bank[b][:, 0:NI].rearrange("e (q p) -> e q p", q=IQ))

                    @block.gpsimd
                    def _(pool):
                        pool.wait_ge(s_j, 1)
                        for q in range(IQ):
                            nc.gpsimd.indirect_dma_start(rows[:, q, :], None, recs.rearrange("(c s) f -> c (s f)", s=CH),
                                                         bass.IndirectOffsetOnAxis(ap=jcol_i[:, q:q + 1], axis=0)).then_inc(s_rows, 16)

                    @block.sync
                    def _(sp):
                        sp.wait_ge(s_j, 1)
                        sp.dma_start(tile_tab[which].rearrange("(p q) -> p q", q=IQ), tcol_i[:]).then_inc(s_t, 16)
                        sp.wait_ge(s_t, 16)
                        sp.dma_start(it["tiles"][:], tile_tab[which].rearrange("(o n) -> o n", o=1)).then_inc(s_tl, 16)
                        if attention:
                            sp.wait_ge(s_rw, 1)
                            sp.dma_start(row_local.rearrange("(p n) -> p n", p=IP), loc_b[:].rearrange("p q s -> p (q s)")).then_inc(s_tl, 16)
                            sp.dma_start(row_other.rearrange("(p n) -> p n", p=IP), lo_b[:].rearrange("p q s -> p (q s)")).then_inc(s_tl, 16)
                            sp.wait_ge(s_b, 1)
                            for i, q, s in ((0, IQ - 1, CH - 1), (1, 0, 0)):
                                sp.dma_start(edge_tab[which][i:i + 1, :].rearrange("o p -> p o"), f[:, q, s, 0:1]).then_inc(s_ed, 16)
                            sp.wait_ge(s_ed, 32)
                            sp.dma_start(prev[1:IP, 0:1], edge_tab[which][0:1, 0:IP - 1].rearrange("o p -> p o")).then_inc(s_ed, 16)
                            sp.dma_start(prev[0:IP - 1, 1:2], edge_tab[which][1:2, 1:IP].rearrange("o p -> p o")).then_inc(s_ed, 16)
                            sp.wait_ge(s_ed, 64)
                        sp.wait_ge(s_tl, 48 if attention else 16)

                    @block.tensor
                    def _(pe):
                        pe.wait_ge(s_rw, 1)
                        for b, t in enumerate((loc, oth, wg, hi)):
                            for q in range(IQ):
                                nc.tensor.transpose(bank[b][:, q * IP:(q + 1) * IP], t[:, q, :], ident[0:IP, 0:IP])
                        pe.drain().then_inc(s_tr, 1)

        items("is", 0, rec_src, cnt_s, it_s, False)
        end_stage()
        items("id", 1, rec_dst, cnt_d, it_d, True)
        end_stage()

        KD = D // 128
        w_nat = sb("w_nat", [128, KD, D])
        w_aug = sb("w_aug", [128, KD, D + 2 * HEADS])
        a_blk = sb("a_blk", [128, KD, 2 * HEADS])
        s_tab = sb("s_tab", [TN, HEADS * NT])
        d_tab = sb("d_tab", [TN, NT * HEADS])
        s_part = sb("s_part", [TN, 3, HEADS * NT], BF16)
        d_part = sb("d_part", [TN, 3, NT * HEADS], BF16)

        def attention_weights(name, W, a, heads):
            s_z, s_in, s_tr, s_cp, s_m = (sem(name + k) for k in ("_z", "_in", "_tr", "_cp", "_m"))
            with nc.Block() as block:
                @block.sync
                def _(sp):
                    sp.dma_start(w_nat[:], W.rearrange("(k p) i -> p k i", p=128)).then_inc(s_in, 16)
                    sp.wait_ge(s_z, 1)
                    hid = D // heads
                    loads = 1
                    with nc.allow_non_contiguous_dma(reason="a few hundred words"):
                        for part_ in range(2):
                            for h in range(heads):
                                for k in range(KD):
                                    lo_, hi_ = max(h * hid, k * 128), min((h + 1) * hid, (k + 1) * 128)
                                    if lo_ < hi_:
                                        sp.dma_start(a_blk[lo_ - k * 128:hi_ - k * 128, k, part_ * heads + h:part_ * heads + h + 1],
                                                     a[h:h + 1, part_ * hid + lo_ - h * hid:part_ * hid + hi_ - h * hid].rearrange("o n -> n o")).then_inc(s_in, 16)
                                        loads += 1
                    sp.wait_ge(s_in, 16 * loads)
                    sp.sem_inc(s_z, 1)

                @block.vector
                def _(dve):
                    nc.vector.memset(a_blk[:], 0.0).then_inc(s_z, 1)
                    dve.wait_ge(s_tr, 1)
                    for k in range(KD):
                        nc.vector.tensor_copy(w_aug[:, k, 0:D], bank[k][:, 0:D])
                        nc.vector.tensor_copy(w_aug[:, k, D:D + 2 * heads], bank[2 + k][:, 0:2 * heads])

                @block.tensor
                def _(pe):
                    pe.wait_ge(s_z, 2)
                    for k in range(KD):
                        for m in range(KD):
                            nc.tensor.transpose(bank[k][:, m * 128:(m + 1) * 128], w_nat[:, m, k * 128:(k + 1) * 128], ident[:])
                    for k in range(KD):
                        for m in range(KD):
                            nc.tensor.matmul(bank[2 + k][:, 0:2 * heads], w_nat[:, m, k * 128:(k + 1) * 128], a_blk[:, m, 0:2 * heads],
                                             start=(m == 0), stop=(m == KD - 1))
                    pe.drain().then_inc(s_tr, 1)

        stats = sb("stats", [TN, NT * 6])
        mean = sb("mean", [TN, NT])
        rstd = sb("rstd", [TN, NT])
        spread = sb("spread", [TN, NT])

        def row_stats(name):
            s_c, s_v, s_q = sem(name + "_c"), sem(name + "_v"), sem(name + "_q")
            st = stats[:].rearrange("p (t s) -> p t s", s=6)
            with nc.Block() as block:
                @block.vector
                def _(dve):
                    c = Chain(dve, s_c)
                    v = nc.vector
                    with dve.Fori(0, NT) as t:
                        v.bn_stats(stats[:, bass.ds(t * 6, 6)], x_sb[:].rearrange("p t d -> p (t d)")[:, bass.ds(t * D, D)])
                    dve.drain().then_inc(s_c, 1)
                    c.here += 1
                    dve.wait_ge(s_c, 1)
                    c(v.tensor_tensor(mean[:], st[:, :, 1], st[:, :, 4], ALU.add))
                    c(v.tensor_scalar(mean[:], mean[:], 0.5, None, ALU.mult))
                    c(v.tensor_tensor(spread[:], st[:, :, 1], st[:, :, 4], ALU.subtract))
                    c(v.scalar_tensor_tensor(spread[:], spread[:], 0.25, spread[:], ALU.mult, ALU.mult))
                    c(v.tensor_tensor(rstd[:], st[:, :, 2], st[:, :, 5], ALU.add))
                    c(v.scalar_tensor_tensor(rstd[:], rstd[:], 1.0 / D, spread[:], ALU.mult, ALU.add))
                    dve.drain().then_inc(s_v, 1)
                    dve.wait_ge(s_q, 1)
                    v.reciprocal(rstd[:], rstd[:])

                @block.scalar
                def _(act):
                    act.wait_ge(s_v, 1)
                    nc.scalar.activation(rstd[:], rstd[:], ACT.Sqrt, bias=eps[0:TN, :]).then_inc(s_q, 1)

        def project(name, heads, table, prepare, func, act_step=None):
            s_h, s_tr, s_ht, s_z, s_zc, s_ac, s_w, s_c = (sem(name + k) for k in ("_h", "_tr", "_ht", "_z", "_zc", "_ac", "_w", "_c"))
            with ExitStack() as scope:
                hbuf = sb(name + "_hbuf", [TN, D], F32, scope)
                h_t = sb(name + "_h_t", [128, KD, TN], F32, scope)
                zst = sb(name + "_zst", [TN, D + 2 * HEADS], F32, scope)
                pt = bank[0][:, 0:KD * TN].rearrange("p (k n) -> p k n", k=KD)
                pz = bank[1]
                with nc.Block() as block:
                    @block.vector
                    def _(dve):
                        c = Chain(dve, s_c)
                        before, per, tile_ = prepare(dve, c, scope, name)
                        before()
                        with c.loop(NT, per + 2) as t:
                            dve.wait_ge(s_tr, t + 1)
                            tile_(t, hbuf)
                            dve.sem_inc(s_h, 1)
                            dve.wait_ge(s_zc, t + 2)
                            c(nc.vector.tensor_copy(s_tab[:, 0:heads * NT].rearrange("p (h t) -> p h t", h=heads)[:, :, bass.ds(t, 1)],
                                                    zst[:, D:D + heads].unsqueeze(2)))
                            c(nc.vector.tensor_copy(d_tab[:, bass.ds(t * heads, heads)], zst[:, D + heads:D + 2 * heads]))
                            dve.sem_inc(s_ac, 1)
                        for tab, parts in ((s_tab[:, 0:heads * NT], s_part),
                                           (d_tab[:, 0:heads * NT], d_part)):
                            for k in range(3):
                                c(nc.vector.tensor_copy(parts[:, k, 0:heads * NT], tab))
                                if k < 2:
                                    c(nc.vector.tensor_tensor(tab, tab, parts[:, k, 0:heads * NT], ALU.subtract))

                    @block.tensor
                    def _(pe):
                        pe.sem_inc(s_tr, 1)
                        with pe.Fori(0, NT) as t:
                            pe.wait_ge(s_h, t + 1)
                            for k in range(KD):
                                last = nc.tensor.transpose(pt[:, k, :], hbuf[:, k * 128:(k + 1) * 128], ident[0:TN, 0:TN])
                            last.then_inc(s_tr, 1)
                            pe.wait_ge(s_ht, t + 1)
                            pe.wait_ge(s_zc, t + 1)
                            for k in range(KD):
                                last = nc.tensor.matmul(pz[0:TN, 0:D + 2 * heads], h_t[:, k, :], w_aug[:, k, 0:D + 2 * heads],
                                                        start=(k == 0), stop=(k == KD - 1))
                            last.then_inc(s_z, 1)

                    @block.scalar
                    def _(act):
                        act.sem_inc(s_zc, 1)
                        act.sem_inc(s_ac, 1)
                        with act.Fori(0, NT) as t:
                            if act_step is not None:
                                act_step(act, t)
                            act.wait_ge(s_tr, t + 2)
                            nc.scalar.activation(h_t[:], pt, func).then_inc(s_ht, 1)
                            act.wait_ge(s_z, t + 1)
                            act.wait_ge(s_w, t * 16 + 16)
                            act.wait_ge(s_ac, t + 1)
                            nc.scalar.activation(zst[:, 0:D + 2 * heads], pz[0:TN, 0:D + 2 * heads], ACT.Copy).then_inc(s_zc, 1)

                    @block.sync
                    def _(sp):
                        sp.sem_inc(s_w, 16)
                        with sp.Fori(0, NT) as t:
                            sp.wait_ge(s_zc, t + 2)
                            sp.dma_start(table[bass.ds(t * TN, TN), :], zst[:, 0:D]).then_inc(s_w, 16)
                        sp.wait_ge(s_w, NT * 16 + 16)

        def prep_norm(dve, c, scope, name):
            def tile_(t, hbuf):
                c(nc.vector.tensor_scalar(hbuf[:], x_sb[:].rearrange("p t d -> p (t d)")[:, bass.ds(t * D, D)],
                                          mean[:, bass.ds(t, 1)], rstd[:, bass.ds(t, 1)],
                                          ALU.subtract, ALU.mult))
            return (lambda: None), 1, tile_

        w_all = sb("w_all", [128, NI * HEADS])

        def edge_softmax(name, H):
            s_r, s_rf, s_lo, s_lof, s_l, s_lf, s_c, s_pd = (sem(name + k) for k in ("_r", "_rf", "_lo", "_lof", "_l", "_lf", "_c", "_pd"))
            s_ra, s_rb = sem(name + "_ra"), sem(name + "_rb")
            with ExitStack() as scope:
                rows_l = sb(name + "_rows_l", [128, 2, G * CH], BF16, scope)
                rows_o = sb(name + "_rows_o", [128, 2, G * CH], BF16, scope)
                sel_l = sb(name + "_sel_l", [128, 2, G * CH], BF16, scope)
                sel_o = sb(name + "_sel_o", [128, 2, G * CH], BF16, scope)
                hot = sb(name + "_hot", [128, G, NT], F32, scope)
                prod = sb(name + "_prod", [128, G, H, NT], F32, scope)
                es = sb(name + "_es", [128, G, H], F32, scope)
                e_all = sb(name + "_e", [128, H, NI], F32, scope)
                hg = G // 2

                def look(g2, b):
                    return bank[g2 * 2 + b][:, 0:hg * H * NT].rearrange("e (g h t) -> e g h t", g=hg, h=H)

                with nc.Block() as block:
                    @block.sync
                    def _(sp):
                        def rows_of(row, n):
                            return row.rearrange("(o n) -> o n", o=1)[:, bass.ds(n * (G * CH), G * CH)].to_broadcast([128, G * CH])

                        def fetch(n, b, s, first):
                            if not first:
                                sp.wait_ge(s_lo, n - 1)
                            sp.dma_start(rows_l[:, b, :], rows_of(row_local, n)).then_inc(s, 16)
                            sp.dma_start(rows_o[:, b, :], rows_of(row_other, n)).then_inc(s, 16)

                        fetch(0, 0, s_ra, True)
                        fetch(1, 1, s_rb, True)
                        with sp.Fori(1, NG // 2) as i:
                            fetch(i * 2, 0, s_ra, False)
                            fetch(i * 2 + 1, 1, s_rb, False)

                    @block.vector
                    def _(dve):
                        c = Chain(dve, s_c)

                        def select(n, b, s):
                            dve.wait_ge(s, (n - b) * 16 + 32)
                            c(nc.vector.tensor_scalar(sel_l[:, b, :], rows_l[:, b, :], part[:], None, ALU.is_equal))
                            c(nc.vector.tensor_scalar(sel_o[:, b, :], rows_o[:, b, :], part[:], None, ALU.is_equal))
                            dve.sem_inc(s_lo, 1)

                        def sums(n, b):
                            c(nc.vector.tensor_tensor(hot[:], high[:, bass.ds(n * G, G)].unsqueeze(2).to_broadcast([128, G, NT]),
                                                      col[:, 0:NT].unsqueeze(1).to_broadcast([128, G, NT]), ALU.is_equal))
                            dve.wait_ge(s_l, n + 1)
                            for k in range(2):
                                c(nc.vector.tensor_tensor(prod[:, k * hg:(k + 1) * hg], look(b, k),
                                                          hot[:, k * hg:(k + 1) * hg].unsqueeze(2).to_broadcast([128, hg, H, NT]), ALU.mult))
                            c(nc.vector.tensor_reduce(es[:], prod[:], AX.X, ALU.add))
                            pd = bank[4 + b][:, 0:G * H].rearrange("e (g h) -> e h g", h=H)
                            c(nc.vector.tensor_tensor(e_all[:, :, bass.ds(n * G, G)], es[:].rearrange("e g h -> e h g"), pd, ALU.add))
                            dve.sem_inc(s_lf, 1)

                        select(0, 0, s_ra)
                        with c.loop(NG // 2 - 1, 14) as i:
                            select(i * 2 + 1, 1, s_rb)
                            sums(i * 2, 0)
                            select(i * 2 + 2, 0, s_ra)
                            sums(i * 2 + 1, 1)
                        select(NG - 1, 1, s_rb)
                        sums(NG - 2, 0)
                        sums(NG - 1, 1)
                        c(nc.vector.scalar_tensor_tensor(e_all[:], e_all[:], 0.01, e_all[:], ALU.mult, ALU.max))

                    @block.tensor
                    def _(pe):
                        def lookups(n, b, first):
                            pe.wait_ge(s_lo, n + 1)
                            if not first:
                                pe.wait_ge(s_lf, n - 1)
                            for k in range(G):
                                o = bank[b * 2 + k // hg][:, (k % hg) * H * NT:(k % hg + 1) * H * NT]
                                for m in range(3):
                                    nc.tensor.matmul(o, sel_o[0:TN, b, k * CH:(k + 1) * CH], s_part[:, m, 0:H * NT],
                                                     start=(m == 0), stop=(m == 2))
                                t = pe.value_load(it_d["tiles"][0:1, bass.ds(n * G + k, 1)], min_val=0, max_val=NT - 1)
                                for m in range(3):
                                    last = nc.tensor.matmul(bank[4 + b][:, k * H:(k + 1) * H], sel_l[0:TN, b, k * CH:(k + 1) * CH],
                                                            d_part[:, m, bass.ds(t * H, H)], start=(m == 0), stop=(m == 2))
                            last.then_inc(s_l, 1)

                        lookups(0, 0, True)
                        lookups(1, 1, True)
                        with pe.Fori(1, NG // 2) as i:
                            lookups(i * 2, 0, False)
                            lookups(i * 2 + 1, 1, False)

                L = IQ * CH
                e_t = sb(name + "_e_t", [IP, H, L], F32, scope)
                fwd = sb(name + "_fwd", [IP, H, L], F32, scope)
                bwd = sb(name + "_bwd", [IP, H, L], F32, scope)
                res = sb(name + "_res", [IP, H, L], F32, scope)
                ends = sb(name + "_ends", [IP, 4, H], F32, scope)
                c_row = sb(name + "_c_row", [H, 4, IP], F32, scope)
                c_run = sb(name + "_c_run", [H, 2, IP], F32, scope)
                c_in = sb(name + "_c_in", [H, 2, IP], F32, scope)
                c_col = sb(name + "_c_col", [IP, 2, H], F32, scope)
                s_1, s_2, s_3, s_4, s_5, s_6, s_7, s_8 = (sem(name + f"_s{i}") for i in range(8))

                def scan(c, o, e, same, forward):
                    r = res[:].rearrange("p h l -> p (h l)")
                    c(nc.vector.tensor_copy(res[:], same[:].unsqueeze(1).to_broadcast([IP, H, L])))
                    o, e = o[:].rearrange("p h l -> p (h l)"), e[:].rearrange("p h l -> p (h l)")
                    if not forward:
                        o, e, r = o[:, ::-1], e[:, ::-1], r[:, ::-1]
                    c(nc.vector.tensor_tensor_scan(o, r, e, -BIG, ALU.add, ALU.max))

                with nc.Block() as block:
                    @block.tensor
                    def _(pe):
                        for h in range(H):
                            for q in range(IQ):
                                nc.tensor.transpose(bank[h][0:IP, q * CH:(q + 1) * CH],
                                                    e_all[:, h, :].rearrange("e (p q) -> e q p", q=IQ)[:, q, :], ident[:])
                        pe.drain().then_inc(s_1, 1)
                        pe.wait_ge(s_3, 1)
                        for k in range(4):
                            nc.tensor.transpose(bank[4][0:H, k * IP:(k + 1) * IP], ends[:, k, :], ident[0:IP, 0:IP])
                        pe.drain().then_inc(s_4, 1)
                        pe.wait_ge(s_5, 1)
                        for k in range(2):
                            nc.tensor.transpose(bank[5][0:IP, k * H:(k + 1) * H], c_in[:, k, :], ident[0:H, 0:H])
                        pe.drain().then_inc(s_6, 1)
                        pe.wait_ge(s_7, 1)
                        for h in range(H):
                            for q in range(IQ):
                                nc.tensor.transpose(bank[h][:, q * IP:(q + 1) * IP], fwd[:, h, q * CH:(q + 1) * CH], ident[0:IP, 0:IP])
                        pe.drain().then_inc(s_8, 1)

                    @block.scalar
                    def _(act):
                        act.wait_ge(s_1, 1)
                        for h in range(H):
                            nc.scalar.activation(e_t[:, h, :], bank[h][0:IP, :], ACT.Copy)
                        act.drain().then_inc(s_2, 1)

                    @block.vector
                    def _(dve):
                        c = Chain(dve, sem(name + "_c2"))
                        v = nc.vector
                        dve.wait_ge(s_2, 1)
                        scan(c, fwd, e_t, same_f, True)
                        scan(c, bwd, e_t, same_b, False)
                        c(v.tensor_copy(ends[:, 0, :], fwd[:, :, L - 1]))
                        c(v.tensor_copy(ends[:, 1, :], bwd[:, :, 0]))
                        c(v.tensor_copy(ends[:, 2:4, :], link[:, 2:4].unsqueeze(2).to_broadcast([IP, 2, H])))
                        dve.drain().then_inc(s_3, 1)
                        dve.wait_ge(s_4, 1)
                        c(v.tensor_copy(c_row[:], bank[4][0:H, 0:4 * IP].rearrange("h (k p) -> h k p", k=4)))
                        c(v.tensor_tensor_scan(c_run[:, 0, :], c_row[:, 2, :], c_row[:, 0, :], -BIG, ALU.add, ALU.max))
                        c(v.tensor_tensor_scan(c_run[:, 1, ::-1], c_row[:, 3, ::-1], c_row[:, 1, ::-1], -BIG, ALU.add, ALU.max))
                        c(v.memset(c_in[:], -BIG))
                        c(v.tensor_copy(c_in[:, 0, 1:IP], c_run[:, 0, 0:IP - 1]))
                        c(v.tensor_copy(c_in[:, 1, 0:IP - 1], c_run[:, 1, 1:IP]))
                        dve.drain().then_inc(s_5, 1)
                        dve.wait_ge(s_6, 1)
                        for k, at in ((0, 0), (1, L - 1)):
                            c(v.tensor_scalar(c_col[:, k, :], bank[5][0:IP, k * H:(k + 1) * H], link[:, k:k + 1], None, ALU.add))
                            c(v.tensor_tensor(e_t[:, :, at], e_t[:, :, at], c_col[:, k, :], ALU.max))
                        scan(c, fwd, e_t, same_f, True)
                        scan(c, bwd, e_t, same_b, False)
                        c(v.tensor_tensor(fwd[:], fwd[:], bwd[:], ALU.max))
                        dve.drain().then_inc(s_7, 1)
                        dve.wait_ge(s_8, 1)
                        for h in range(H):
                            c(v.tensor_tensor(e_all[:, h, :].rearrange("e (p q) -> e q p", q=IQ),
                                              e_all[:, h, :].rearrange("e (p q) -> e q p", q=IQ),
                                              bank[h][:, 0:NI].rearrange("e (q p) -> e q p", q=IQ), ALU.subtract))

                with nc.Block() as block:
                    @block.scalar
                    def _(act):
                        nc.scalar.activation(w_all[:, 0:NI * H].rearrange("e (n h) -> e h n", h=H), e_all[:], ACT.Exp)

        def aggregate(name, table, it, W, into, weight=None, heads=1):
            s_g = [sem(name + f"_g{k}") for k in range(G)]
            s_ix, s_use, s_sel, s_mm, s_add, s_z, s_turn = (sem(name + k) for k in ("_ix", "_use", "_sel", "_mm", "_add", "_z", "_turn"))
            with ExitStack() as scope:
                ix = sb(name + "_ixb", [128, 2 * G], I32, scope)
                rows = sb(name + "_rowb", [128, G, D + 1], F32, scope)
                sel = sb(name + "_selb", [128, 4, TN], F32, scope)
                scaled = sb(name + "_scl", [128, 4, D], F32, scope) if heads > 1 else None
                with nc.Block() as block:
                    @block.gpsimd
                    def _(pool):
                        pool.wait_ge(s_z, 1)

                        def group(g, h, first):
                            pool.wait_ge(s_z, 1)
                            if not first:
                                for k in range(G):
                                    pool.wait_ge(s_g[k], g * 16 - 16)
                            nc.gpsimd.tensor_copy(ix[:, h * G:(h + 1) * G], it["index"][:, bass.ds(g * G, G)]).then_inc(s_ix, 1)
                            pool.wait_ge(s_ix, g + 1)
                            pool.sem_inc(s_turn, 1)
                            for k in range(G):
                                if h or not first:
                                    if heads == 1:
                                        pool.wait_ge(s_mm, g * G + (k + 1 + 4 - G))
                                    else:
                                        pool.wait_ge(s_use, g * G + (k + 1 - G))
                                    pool.sem_inc(s_turn, 1)
                                nc.gpsimd.indirect_dma_start(rows[:, k, 0:D], None, table,
                                                             bass.IndirectOffsetOnAxis(ap=ix[:, h * G + k:h * G + k + 1], axis=0)).then_inc(s_g[k], 16)
                        group(0, 0, True)
                        group(1, 1, True)
                        with pool.Fori(1, NG // 2) as j:
                            group(j * 2, 0, False)
                            group(j * 2 + 1, 1, False)

                    @block.vector
                    def _(dve):
                        nc.vector.memset(into, 0.0)
                        nc.vector.memset(rows[:, :, D:D + 1], 1.0)
                        dve.drain().then_inc(s_z, 1)
                        dve.wait_ge(s_z, 1)
                        dve.sem_inc(s_mm, 4)
                        dve.sem_inc(s_add, 4)

                        def make(g, k):
                            n = g * G + k
                            dve.wait_ge(s_mm, n + 1)
                            if heads == 1:
                                nc.vector.tensor_scalar(sel[:, k % 4, :], col[:, 0:TN], it["local"][:, bass.ds(n, 1)],
                                                        weight[:, bass.ds(n, 1)], ALU.is_equal, ALU.mult).then_inc(s_sel, 1)
                            else:
                                nc.vector.tensor_scalar(sel[:, k % 4, :], col[:, 0:TN], it["local"][:, bass.ds(n, 1)],
                                                        None, ALU.is_equal).then_inc(s_sel, 1)
                                dve.wait_ge(s_g[k], g * 16 + 16)
                                wv = w_all[:, bass.ds(n * HEADS, HEADS)]
                                nc.vector.tensor_tensor(scaled[:, k % 4, :].rearrange("e (h o) -> e h o", h=heads),
                                                        rows[:, k, 0:D].rearrange("e (h o) -> e h o", h=heads),
                                                        wv.unsqueeze(2).to_broadcast([128, heads, D // heads]), ALU.mult).then_inc(s_use, 1)

                        def add(g, k):
                            n = g * G + k
                            t = dve.value_load(it["tiles"][0:1, bass.ds(n, 1)], min_val=0, max_val=NT - 1)
                            dve.wait_ge(s_mm, n + 5)
                            dve.wait_ge(s_add, n + 4)
                            o = into[:, bass.ds(t * W, W)]
                            nc.vector.tensor_tensor(o, o, bank[k % 4][0:TN, 0:W], ALU.add).then_inc(s_add, 1)

                        with dve.Fori(0, NG) as g:
                            for k in range(G):
                                make(g, k)
                                if k >= 2:
                                    add(g, k - 2)
                            add(g, G - 2)
                            add(g, G - 1)

                    @block.tensor
                    def _(pe):
                        with pe.Fori(0, NG) as g:
                            for k in range(G):
                                n = g * G + k
                                pe.wait_ge(s_sel, n + 1)
                                pe.wait_ge(s_add, n + 1)
                                if heads == 1:
                                    pe.wait_ge(s_g[k], g * 16 + 16)
                                    nc.tensor.matmul(bank[k % 4][0:TN, 0:W], sel[:, k % 4, :], rows[:, k, 0:W], start=True, stop=True).then_inc(s_mm, 1)
                                else:
                                    nc.tensor.matmul(bank[k % 4][0:TN, D:W], sel[:, k % 4, :],
                                                     w_all[:, bass.ds(n * HEADS, HEADS)], start=True, stop=True)
                                    pe.wait_ge(s_use, n + 1)
                                    nc.tensor.matmul(bank[k % 4][0:TN, 0:D], sel[:, k % 4, :], scaled[:, k % 4, :], start=True, stop=True).then_inc(s_mm, 1)

        W1_r = W1.rearrange("h o i -> (h o) i")
        x_flat = x_sb[:].rearrange("p t d -> p (t d)")
        row_stats("st1")
        end_stage()
        attention_weights("aw1", W1_r, a1, HEADS)
        end_stage()
        project("pr1", HEADS, z_tab, prep_norm, ACT.Relu)
        end_stage()
        edge_softmax("es1", HEADS)
        end_stage()
        W = D + HEADS
        aggregate("ag1", z_tab, it_d, W, acc[:], heads=HEADS)
        end_stage()
        elu = [None, None]

        def prep_elu(dve, c, scope, name):
            inv = sb("inv", [TN, HEADS], F32, scope)
            neg, ex = elu

            def tile_(t, hbuf):
                c(nc.vector.tensor_scalar(inv[:], acc[:, bass.ds(t * W + D, HEADS)], 1e-30, None, ALU.max))
                c(nc.vector.reciprocal(inv[:], inv[:]))
                c(nc.vector.tensor_tensor(hbuf[:].rearrange("p (h o) -> p h o", h=HEADS),
                                          acc[:, bass.ds(t * W, D)].rearrange("p (h o) -> p h o", h=HEADS),
                                          inv[:].unsqueeze(2).to_broadcast([TN, HEADS, HID]), ALU.mult))
                c(nc.vector.tensor_scalar(neg[:], hbuf[:], 0.0, None, ALU.min))
                dve.sem_inc(s_mn, 1)
                dve.wait_ge(s_ex, t + 1)
                c(nc.vector.scalar_tensor_tensor(hbuf[:], hbuf[:], 0.0, ex[:], ALU.max, ALU.add))
                c(nc.vector.tensor_scalar(hbuf[:], hbuf[:], -1.0, None, ALU.add))
            return (lambda: None), 6, tile_

        def exp_step(act, t):
            act.wait_ge(s_mn, t + 1)
            nc.scalar.activation(elu[1][:], elu[0][:], ACT.Exp).then_inc(s_ex, 1)

        attention_weights("aw2", W2, a2.rearrange("(o n) -> o n", o=1), 1)
        end_stage()
        with ExitStack() as scope:
            elu[0], elu[1] = sb("neg", [TN, D], F32, scope), sb("expo", [TN, D], F32, scope)
            s_mn, s_ex = sem("s_mn"), sem("s_ex")
            project("pr2", 1, z2_tab, prep_elu, ACT.Copy, act_step=exp_step)
            end_stage()
        edge_softmax("es2", 1)
        end_stage()
        W_ = D + 1
        aggregate("ag2", z2_tab, it_d, W_, acc[:, 0:NT * W_], weight=w_all)
        end_stage()
        s_c = sem("res_c")
        with nc.Block() as block:
            @block.vector
            def _(dve):
                c = Chain(dve, s_c)
                a3 = acc[:, 0:NT * W_].rearrange("p (t w) -> p t w", w=W_)
                c(nc.vector.tensor_scalar(spread[:], a3[:, :, D], 1e-30, None, ALU.max))
                c(nc.vector.reciprocal(spread[:], spread[:]))
                c(nc.vector.tensor_tensor(a3[:, :, 0:D], a3[:, :, 0:D], spread[:].unsqueeze(2).to_broadcast([TN, NT, D]), ALU.mult))
                c(nc.vector.tensor_tensor(x_sb[:], x_sb[:], a3[:, :, 0:D], ALU.add))

        row_stats("st2")
        end_stage()
        hb = sb("hb", [TN, NT, D])
        a_out = sb("a_out", [TN, NT * D])
        sq = a_out[:].rearrange("p (t d) -> p t d", d=D)
        vec = sb("vec", [TN, 4, D])
        w_io = sb("w_io", [128, KD, 2 * D])
        w_g = sb("w_g", [128, 3 * KD, 2 * D])
        b_io = sb("b_io", [1, 2 * D])
        b_g = sb("b_g", [1, 2 * D])
        s_c, s_p, s_p2, s_v, s_q, s_w = (sem("bn" + k) for k in ("_c", "_p", "_p2", "_v", "_q", "_w"))
        with nc.Block() as block:
            @block.sync
            def _(sp):
                for dst_, src_ in ((vec[:, 0, :], gamma.rearrange("(o d) -> o d", o=1).to_broadcast([TN, D])),
                                   (vec[:, 1, :], beta.rearrange("(o d) -> o d", o=1).to_broadcast([TN, D])),
                                   (w_io[:, :, 0:D], W_in.rearrange("(k p) n -> p k n", p=128)),
                                   (w_io[:, :, D:2 * D], W_out.rearrange("(k p) n -> p k n", p=128)),
                                   (w_g[:, 0:2 * KD, :], W_x2i.rearrange("(k p) n -> p k n", p=128)),
                                   (w_g[:, 2 * KD:3 * KD, :], W_h2h.rearrange("(k p) n -> p k n", p=128)),
                                   (b_io[:, 0:D], b_in.rearrange("(o d) -> o d", o=1)),
                                   (b_io[:, D:2 * D], b_out.rearrange("(o d) -> o d", o=1)),
                                   (b_g[:], b_x2i.rearrange("(o d) -> o d", o=1))):
                    sp.dma_start(dst_, src_).then_inc(s_w, 16)
                sp.wait_ge(s_w, 16 * 9)

            @block.vector
            def _(dve):
                c = Chain(dve, s_c)
                v = nc.vector
                wide = lambda a: a.unsqueeze(2).to_broadcast([TN, NT, D])
                tall = lambda k: vec[:, k:k + 1, :].to_broadcast([TN, NT, D])
                c(v.tensor_tensor(hb[:], x_sb[:], wide(mean[:]), ALU.subtract))
                c(v.tensor_tensor(hb[:], hb[:], wide(rstd[:]), ALU.mult))
                c(v.tensor_scalar(hb[:], hb[:], 0.0, None, ALU.max))
                dve.drain().then_inc(s_v, 1)
                dve.wait_ge(s_p, 1)
                c(v.tensor_scalar(vec[:, 2, :], bank[0][0:TN, 0:D], 1.0 / N, None, ALU.mult))
                c(v.tensor_tensor(hb[:], hb[:], tall(2), ALU.subtract))
                c(v.tensor_tensor(sq, hb[:], hb[:], ALU.mult))
                dve.drain().then_inc(s_v, 1)
                dve.wait_ge(s_p2, 1)
                c(v.tensor_scalar(vec[:, 3, :], bank[1][0:TN, 0:D], 1.0 / N, None, ALU.mult))
                dve.drain().then_inc(s_v, 1)
                dve.wait_ge(s_q, 1)
                c(v.reciprocal(vec[:, 3, :], vec[:, 3, :]))
                dve.wait_ge(s_w, 16 * 9)
                c(v.tensor_tensor(vec[:, 3, :], vec[:, 3, :], vec[:, 0, :], ALU.mult))
                c(v.tensor_tensor(hb[:], hb[:], tall(3), ALU.mult))
                c(v.tensor_tensor(hb[:], hb[:], tall(1), ALU.add))

            @block.scalar
            def _(act):
                act.wait_ge(s_v, 3)
                nc.scalar.activation(vec[:, 3, :], vec[:, 3, :], ACT.Sqrt, bias=eps[0:TN, :]).then_inc(s_q, 1)

            @block.tensor
            def _(pe):
                for i, (t, s) in enumerate(((hb[:], s_p), (sq, s_p2))):
                    pe.wait_ge(s_v, i + 1)
                    for k in range(NT):
                        last = nc.tensor.matmul(bank[i][0:TN, 0:D], ones[0:TN, 0:TN], t[:, k, :], start=(k == 0), stop=(k == NT - 1))
                    last.then_inc(s, 1)

        def dense(name, srcs, weights, bias, after_act, after_dve, dve_per, store, nst):
            K = KD * len(srcs)
            s_h, s_tr, s_ht, s_z, s_a, s_o, s_w, s_c = (sem(name + k) for k in ("_h", "_tr", "_ht", "_z", "_a", "_o", "_w", "_c"))
            with ExitStack() as scope:
                hbuf = sb(name + "_hbuf", [TN, K * 128], F32, scope)
                h_t = sb(name + "_h_t", [128, K, TN], F32, scope)
                res = sb(name + "_res", [TN, 2 * D], F32, scope)
                outb = sb(name + "_outb", [TN, D], F32, scope)
                with nc.Block() as block:
                    @block.vector
                    def _(dve):
                        c = Chain(dve, s_c)
                        with c.loop(NT, len(srcs) + dve_per) as t:
                            dve.wait_ge(s_tr, t + 1)
                            for i, s in enumerate(srcs):
                                c(nc.vector.tensor_copy(hbuf[:, i * D:(i + 1) * D], s[:, bass.ds(t * D, D)]))
                            dve.sem_inc(s_h, 1)
                            if dve_per:
                                dve.wait_ge(s_a, t + 2)
                                dve.wait_ge(s_w, t * 16 + 16)
                                after_dve(c, t, res, outb)
                                dve.sem_inc(s_o, 1)

                    @block.tensor
                    def _(pe):
                        pe.sem_inc(s_tr, 1)
                        with pe.Fori(0, NT) as t:
                            pe.wait_ge(s_h, t + 1)
                            for k in range(K):
                                last = nc.tensor.transpose(bank[k // 4][:, (k % 4) * TN:(k % 4 + 1) * TN], hbuf[:, k * 128:(k + 1) * 128], ident[0:TN, 0:TN])
                            last.then_inc(s_tr, 1)
                            pe.wait_ge(s_ht, t + 1)
                            pe.wait_ge(s_a, t + 1)
                            for k in range(K):
                                nc.tensor.matmul(bank[2][0:TN, :], h_t[:, k, :], weights[:, k, :], start=(k == 0), stop=False)
                            nc.tensor.matmul(bank[2][0:TN, :], ones[0:1, 0:TN], bias[:], start=False, stop=True).then_inc(s_z, 1)

                    @block.scalar
                    def _(act):
                        act.sem_inc(s_a, 1)
                        act.sem_inc(s_o, 1)
                        with act.Fori(0, NT) as t:
                            act.wait_ge(s_tr, t + 2)
                            for b in range((K + 3) // 4):
                                n = min(4, K - 4 * b)
                                ins = nc.scalar.activation(h_t[:, 4 * b:4 * b + n, :], bank[b][:, 0:n * TN].rearrange("p (k n) -> p k n", k=n), ACT.Copy)
                            ins.then_inc(s_ht, 1)
                            act.wait_ge(s_z, t + 1)
                            act.wait_ge(s_o if dve_per else s_w, t + 1 if dve_per else t * 16 * nst + 16)
                            after_act(res).then_inc(s_a, 1)

                    @block.sync
                    def _(sp):
                        sp.sem_inc(s_w, 16)
                        with sp.Fori(0, NT) as t:
                            sp.wait_ge(s_o if dve_per else s_a, t + 2)
                            for o, i in store(t, res, outb):
                                sp.dma_start(o, i).then_inc(s_w, 16)
                        sp.wait_ge(s_w, NT * 16 * nst + 16)

        dense("fp", [hb[:].rearrange("p t d -> p (t d)")], w_io, b_io,
              lambda res: nc.scalar.activation(res[:], bank[2][0:TN, :], ACT.Copy), None, 0,
              lambda t, res, outb: [(fin_tab[bass.ds(t * TN, TN), :], res[:, 0:D]), (fout_tab[bass.ds(t * TN, TN), :], res[:, D:2 * D])], 2)
        end_stage()
        aggregate("ag3", fin_tab, it_d, D, acc[:, 0:NT * D], weight=it_d["weight"])
        end_stage()
        aggregate("ag4", fout_tab, it_s, D, a_out[:], weight=it_s["weight"])
        end_stage()

        def gates(res):
            nc.scalar.activation(res[:, 0:D], bank[2][0:TN, 0:D], ACT.Sigmoid)
            return nc.scalar.activation(res[:, D:2 * D], bank[2][0:TN, D:2 * D], ACT.Tanh)

        def gru(c, t, res, outb):
            v = nc.vector
            c(v.tensor_tensor(outb[:], hb[:].rearrange("p t d -> p (t d)")[:, bass.ds(t * D, D)], res[:, D:2 * D], ALU.subtract))
            c(v.tensor_tensor(outb[:], outb[:], res[:, 0:D], ALU.mult))
            c(v.tensor_tensor(outb[:], outb[:], res[:, D:2 * D], ALU.add))
            c(v.tensor_tensor(outb[:], outb[:], x_flat[:, bass.ds(t * D, D)], ALU.add))

        dense("gr", [acc[:, 0:NT * D], a_out[:], hb[:].rearrange("p t d -> p (t d)")], w_g, b_g, gates, gru, 4,
              lambda t, res, outb: [(out[bass.ds(t * TN, TN), :], outb[:])], 1)
        end_stage()


_INS = ["x", "src", "dst", "edge_weight", "edge_weight_n2", "L0_gnn_W1", "L0_gnn_a1", "L0_gnn_W2", "L0_gnn_a2",
        "L1_gnn_gamma", "L1_gnn_beta", "L1_gnn_W_in", "L1_gnn_b_in", "L1_gnn_W_out", "L1_gnn_b_out",
        "L1_gnn_W_x2i", "L1_gnn_b_x2i", "L1_gnn_W_h2h"]


def kernel(**inputs):
    import numpy as np
    import concourse.bacc as bacc
    from concourse.bass_utils import run_bass_kernel_spmd

    nc = bacc.Bacc("TRN2", target_bir_lowering=False, num_devices=1)
    arrays, args = {}, []
    for name in _INS:
        a = np.ascontiguousarray(inputs[name])
        arrays[f"in_{name}"] = a
        args.append(nc.dram_tensor(f"in_{name}", a.shape, mybir.dt.from_np(a.dtype), kind="ExternalInput").ap())
    out = nc.dram_tensor("out", (N, D), F32, kind="ExternalOutput").ap()
    build(nc, *args, out)
    r = run_bass_kernel_spmd(nc, [arrays], core_ids=[0])
    return r.results[0]["out"]
```

```python
import concourse.bass as bass
from concourse import mybir
from contextlib import ExitStack, contextmanager

F32, I32, BF16, U32 = mybir.dt.float32, mybir.dt.int32, mybir.dt.bfloat16, mybir.dt.uint32
ALU, ACT, AX = mybir.AluOpType, mybir.ActivationFunctionType, mybir.AxisListType

N, D, E = 3125, 256, 50000
HEADS, HID = 4, 64
TN = 125
NT = N // TN
CH = 128
SH = 14
EC = 392
EP = EC * CH
IQ, IP = 4, 104
NI = IQ * IP
G = 8
NG = NI // G
RB = 16
RING = 8
LEAD = 4
PAD_KEY = 4000.0
BIG = 1e30
ROUND = 12582912.0
EPS = 1e-5
assert NI >= EC + NT - 1 and EC % (2 * SH) == 0 and EP >= E


class Chain:

    def __init__(self, eng, sem):
        self.eng, self.sem, self.done, self.here, self.turn, self.per = eng, sem, 0, 0, None, 0

    def step(self, ins):
        ins.then_inc(self.sem, 1)
        self.here += 1

    def wait(self, back=0):
        n = self.done + self.here - back
        self.eng.wait_ge(self.sem, n if self.turn is None else self.turn * self.per + n)

    def __call__(self, ins):
        self.step(ins)
        self.wait()

    @contextmanager
    def loop(self, turns, per):
        self.done, self.here = self.done + self.here, 0
        with self.eng.Fori(0, turns) as i:
            self.turn, self.per = i, per
            yield i
            assert self.here == per, (self.here, per)
        self.turn, self.done, self.here = None, self.done + turns * per, 0


class Flow:

    def __init__(self, hbuf, res, s_tr, s_h, s_zc, s_w):
        self.hbuf, self.res, self.s_tr, self.s_h, self.s_zc, self.s_w = hbuf, res, s_tr, s_h, s_zc, s_w


@contextmanager
def turns_of(eng, turns, chain=None, per=0):
    if chain is None:
        with eng.Fori(0, turns) as i:
            yield i
    else:
        with chain.loop(turns, per) as i:
            yield i


def alternate(eng, count, step, chain=None, per=0):
    with turns_of(eng, count // 2, chain, 2 * per) as i:
        step(i * 2, 0, i)
        step(i * 2 + 1, 1, i)
    if count % 2:
        step(count - 1, 0, count // 2)


def skewed(eng, count, ahead, behind, chain=None, per=0):
    ahead(0, 0, 0)
    pairs = (count - 1) // 2
    with turns_of(eng, pairs, chain, 2 * per) as i:
        ahead(i * 2 + 1, 1, i)
        behind(i * 2, 0, i)
        ahead(i * 2 + 2, 0, i + 1)
        behind(i * 2 + 1, 1, i)
    n = 2 * pairs
    if count - 1 > n:
        ahead(n + 1, 1, pairs)
        behind(n, 0, pairs)
        behind(n + 1, 1, pairs)
    else:
        behind(n, 0, pairs)


def build(nc, x, src, dst, edge_weight, edge_weight_n2, W1, a1, W2, a2, gamma, beta,
          W_in, b_in, W_out, b_out, W_x2i, b_x2i, W_h2h, out):
    ctx = ExitStack()
    with ctx:
        held = []

        def sem(name):
            held.append(nc.alloc_semaphore(name=name))
            return held[-1]

        def end_stage():
            with nc.Block() as block:
                @block.gpsimd
                def _(pool):
                    nc.clear_and_free_semaphores(held)
            held.clear()

        def fence(block, name, engines=("sync", "scalar", "tensor", "vector")):
            s_here = sem(name)
            for which in engines:
                def program(eng):
                    eng.drain().then_inc(s_here, 1)
                    eng.wait_ge(s_here, len(engines))
                {"sync": block.sync, "scalar": block.scalar, "tensor": block.tensor,
                 "vector": block.vector, "gpsimd": block.gpsimd}[which](program)

        def sb(name, shape, dt=F32, scope=ctx):
            return scope.enter_context(nc.sbuf_tensor(name, shape, dt))

        def dram(name, shape, dt=F32):
            return nc.dram_tensor(name, shape, dt, kind="Internal").ap()

        rec_half = dram("rec_half", (EP, 4))
        rec_src = dram("rec_src", (EP, 4))
        rec_dst = dram("rec_dst", (EP, 4))
        row_local = dram("row_local", (NI * CH,), BF16)
        row_other = dram("row_other", (NI * CH,), BF16)
        tile_tab = [dram(f"tile_tab{i}", (NI,), I32) for i in range(2)]
        edge_tab = dram("edge_tab", (2, IP))
        z_tab, z2_tab = dram("z_tab", (N, D)), dram("z2_tab", (N, D))
        fin_tab, fout_tab = dram("fin_tab", (N, D)), dram("fout_tab", (N, D))

        bank = [ctx.enter_context(nc.psum_tensor(f"bank{i}", [128, 512], F32)) for i in range(8)]

        part = sb("part", [128, 1])
        col = sb("col", [128, 128])
        item_no = sb("item_no", [128, IQ])
        ident = sb("ident", [128, 128])
        below = sb("below", [128, 128])
        ones = sb("ones", [128, 128])
        eps = sb("eps", [128, 1])
        KD = D // 128
        x_sb = sb("x_sb", [TN, NT, D])
        x_flat = x_sb[:].rearrange("p t d -> p (t d)")
        acc = sb("acc", [TN, NT * (D + HEADS)])
        w_aug = [sb(f"w_aug{i}", [128, KD, D + 2 * HEADS]) for i in range(2)]
        cnt_s = sb("cnt_s", [128, NT])
        cnt_d = sb("cnt_d", [128, NT])
        place_i = sb("place_i", [128, EC], I32)
        rec_s = sb("rec_s", [128, EC, 4])
        stage_p = sb("stage_p", [128, 2, SH], I32)
        stage_r = sb("stage_r", [128, 2, SH, 4])
        disorder = sb("disorder", [1, 1], I32)

        def item_arrays(name):
            return {"local": sb(name + "_local", [128, NI]), "index": sb(name + "_index", [128, NI], I32),
                    "weight": sb(name + "_weight", [128, NI]), "tiles": sb(name + "_tiles", [1, NI], I32)}

        it_s, it_d = item_arrays("src"), item_arrays("dst")
        high = sb("high", [128, NI])
        same_f = sb("same_f", [IP, IQ * CH])
        same_b = sb("same_b", [IP, IQ * CH])
        link = sb("link", [IP, 4])
        s_tab = sb("s_tab", [TN, HEADS * NT])
        d_tab = sb("d_tab", [TN, NT * HEADS])
        s_part = sb("s_part", [TN, 3, HEADS * NT], BF16)
        d_part = sb("d_part", [TN, 3, NT * HEADS], BF16)
        stats = sb("stats", [TN, NT * 6])
        mean = sb("mean", [TN, NT])
        rstd = sb("rstd", [TN, NT])
        spread = sb("spread", [TN, NT])
        w_all = sb("w_all", [128, NI * HEADS])

        def scatter(name, pool, rec, to, first, last, ready=None):
            s_stage, s_turn = sem(name + "_stage"), sem(name + "_turn")
            s_free = [sem(name + f"_free{h}") for h in range(2)]
            flat = rec[:].rearrange("p j f -> p (j f)")

            def half(g, r, h, first_use):
                if not first_use:
                    pool.wait_ge(s_free[h], r * (16 * SH))
                at = (g * 2 + h) * SH
                nc.gpsimd.tensor_copy(stage_p[:, h, :], place_i[:, bass.ds(at, SH)]).then_inc(s_stage, 1)
                nc.gpsimd.tensor_copy(stage_r[:, h, :, :].rearrange("p a f -> p (a f)"),
                                      flat[:, bass.ds(at * 4, SH * 4)]).then_inc(s_stage, 1)
                pool.wait_ge(s_stage, r * 4 + (2 * h + 2))
                pool.sem_inc(s_turn, 1)
                for k in range(SH):
                    nc.gpsimd.indirect_dma_start(to, bass.IndirectOffsetOnAxis(ap=stage_p[:, h, k:k + 1], axis=0),
                                                 stage_r[:, h, k, :], None).then_inc(s_free[h], 16)

            for h in range(2):
                half(first, 0, h, True)
            with pool.Fori(1, last - first) as r:
                for h in range(2):
                    half(r + first, r, h, False)
            for h in range(2):
                pool.wait_ge(s_free[h], (last - first) * 16 * SH)

        def sort_digit(c, rec, digit, low):
            v = nc.vector
            c(v.tensor_scalar(digit[:], rec[:, :, 0], 1.0 / TN, -0.496, ALU.mult, ALU.add))
            c(v.tensor_scalar(digit[:], digit[:], ROUND, ROUND, ALU.add, ALU.subtract))
            c(v.tensor_scalar(digit[:], digit[:], float(NT - 1), None, ALU.min))
            if low:
                c(v.scalar_tensor_tensor(digit[:], digit[:], -float(TN), rec[:, :, 0], ALU.mult, ALU.add))
                c(v.tensor_scalar(digit[:], digit[:], float(TN - 1), None, ALU.min))

        def rank(name, tmp):
            digit, equal, run, place, tot, cnt, incl, off = tmp
            s_tot, s_sum, s_turn = sem(name + "_tot"), sem(name + "_sum"), sem(name + "_turn")

            def vector(dve, c, rec, low, buckets):
                v = nc.vector
                sort_digit(c, rec, digit, low)
                with c.loop(buckets, 1) as b:
                    c(v.tensor_scalar(equal[:, 0, :], digit[:], col[:, bass.ds(b, 1)], 0.0, ALU.is_equal, ALU.add,
                                             accum_out=tot[:, bass.ds(b, 1)]))
                c.wait()
                dve.drain().then_inc(s_tot, 1)
                dve.wait_ge(s_sum, 1)
                c(v.tensor_copy(cnt[:, 0:buckets], bank[0][:, 128:128 + buckets]))
                c(v.tensor_tensor_scan(incl[:, 0:buckets], cnt[:, 0:buckets], cnt[:, 0:buckets], 0.0, ALU.add, ALU.bypass))
                c(v.tensor_tensor(off[:, 0:buckets], incl[:, 0:buckets], cnt[:, 0:buckets], ALU.subtract))
                c(v.scalar_tensor_tensor(off[:, 0:buckets], off[:, 0:buckets], -1.0, bank[0][:, 0:buckets], ALU.add, ALU.add))
                c(v.memset(place[:], 0.0))

                def mark(b, i):
                    c.step(v.tensor_scalar(equal[:, i, :], digit[:], col[:, bass.ds(b, 1)], None, ALU.is_equal))

                def count(b, i):
                    c.step(v.tensor_tensor_scan(run[:, i, :], equal[:, i, :], equal[:, i, :], off[:, bass.ds(b, 1)], ALU.add, ALU.bypass))

                def take(i):
                    c.step(v.copy_predicated(place[:], equal[:, i, :].bitcast(U32), run[:, i, :]))

                with c.loop(buckets // 2, 6) as i:
                    mark(i * 2, 0)
                    c.wait(1)
                    mark(i * 2 + 1, 1)
                    c.wait(1)
                    count(i * 2, 0)
                    c.wait(1)
                    count(i * 2 + 1, 1)
                    c.wait(1)
                    dve.sem_inc(s_turn, 1)
                    take(0)
                    c.wait(0)
                    dve.sem_inc(s_turn, 1)
                    take(1)
                c.wait()
                mark(buckets - 1, 0)
                c.wait()
                count(buckets - 1, 0)
                c.wait()
                take(0)
                c.wait()
                c(v.tensor_copy(place_i[:], place[:]))

            def tensor(pe, buckets):
                pe.wait_ge(s_tot, 1)
                nc.tensor.matmul(bank[0][:, 0:buckets], below[:], tot[:, 0:buckets], start=True, stop=True)
                nc.tensor.matmul(bank[0][:, 128:128 + buckets], ones[:], tot[:, 0:buckets], start=True, stop=True)
                pe.drain().then_inc(s_sum, 1)

            return vector, tensor

        with ExitStack() as scope:
            rec_d = sb("rec_d", [128, EC, 4], F32, scope)
            src_i = sb("src_i", [128, EC], I32, scope)
            dst_i = sb("dst_i", [128, EC], I32, scope)
            next_i = sb("next_i", [128, EC], I32, scope)
            wgt_s = sb("wgt_s", [128, EC], F32, scope)
            wgt_d = sb("wgt_d", [128, EC], F32, scope)
            digit = sb("digit", [128, EC], F32, scope)
            equal = sb("equal", [128, 2, EC], F32, scope)
            run = sb("run", [128, 2, EC], F32, scope)
            place = sb("place", [128, EC], F32, scope)
            tot, cnt, incl, off = (sb(k, [128, 128], F32, scope) for k in ("tot", "cnt", "incl", "off"))
            falls = sb("falls", [128, 1], F32, scope)
            falls1 = sb("falls1", [1, 1], F32, scope)
            w_nat = [sb(f"w_nat{i}", [128, KD, D], F32, scope) for i in range(2)]
            a_blk = [sb(f"a_blk{i}", [128, KD, 2 * HEADS], F32, scope) for i in range(2)]
            tmp = (digit, equal, run, place, tot, cnt, incl, off)
            s_iota, s_const, s_x, s_pad, s_in, s_c = (sem(k) for k in ("iota", "const", "in_x", "pad", "in_edges", "order_c"))
            s_w, s_rd, s_recd, s_fl, s_fm, s_wt = (sem(k) for k in ("in_w", "rec_d_out", "rec_d_made", "falls_v", "falls_m", "w_trans"))
            rank_v, rank_t = rank("rank", tmp)

            with nc.Block() as block:
                @block.sync
                def _(sp):
                    full = E // EC
                    rest = E - full * EC
                    sp.wait_ge(s_pad, 1)
                    loads = 0
                    for t, a, shift in ((src_i, src, 0), (dst_i, dst, 0), (wgt_s, edge_weight_n2, 0), (wgt_d, edge_weight, 0),
                                        (next_i, dst, 1)):
                        sp.dma_start(t[0:full, :], a[shift:shift + full * EC].rearrange("(p j) -> p j", j=EC)).then_inc(s_in, 16)
                        sp.dma_start(t[full:full + 1, 0:rest - shift],
                                     a[shift + full * EC:E].rearrange("(o j) -> o j", o=1)).then_inc(s_in, 16)
                    sp.dma_start(x_sb[:], x.rearrange("(t p) d -> p t d", p=TN)).then_inc(s_x, 16)
                    with nc.allow_non_contiguous_dma(reason="a few hundred words"):
                        for i, (W, a, heads) in enumerate(((W1.rearrange("h o i -> (h o) i"), a1, HEADS),
                                                           (W2, a2.rearrange("(o n) -> o n", o=1), 1))):
                            sp.dma_start(w_nat[i][:], W.rearrange("(k p) i -> p k i", p=128)).then_inc(s_w, 16)
                            loads += 1
                            hid = D // heads
                            for half in range(2):
                                for h in range(heads):
                                    for k in range(KD):
                                        lo, hi = max(h * hid, k * 128), min((h + 1) * hid, (k + 1) * 128)
                                        if lo < hi:
                                            sp.dma_start(a_blk[i][lo - k * 128:hi - k * 128, k, half * heads + h:half * heads + h + 1],
                                                         a[h:h + 1, half * hid + lo - h * hid:half * hid + hi - h * hid].rearrange("o n -> n o")).then_inc(s_w, 16)
                                            loads += 1
                    sp.wait_ge(s_recd, 1)
                    sp.dma_start(rec_dst.rearrange("(p j) f -> p j f", p=128), rec_d[:]).then_inc(s_rd, 16)
                    sp.wait_ge(s_rd, 16)
                    sp.wait_ge(s_x, 16)
                    sp.wait_ge(s_w, 16 * loads)
                    sp.sem_inc(s_wt, 1)

                @block.gpsimd
                def _(pool):
                    for t, pattern, per in ((part, [[0, 1]], 1), (col, [[1, 128]], 0), (item_no, [[1, IQ]], IQ)):
                        nc.gpsimd.iota(t[:], pattern, base=0, channel_multiplier=per,
                                       allow_small_or_imprecise_dtypes=True).then_inc(s_iota, 1)

                @block.vector
                def _(dve):
                    c = Chain(dve, s_c)
                    v = nc.vector
                    for t in a_blk:
                        v.memset(t[:], 0.0)
                    v.memset(src_i[:], int(PAD_KEY))
                    v.memset(dst_i[:], int(PAD_KEY))
                    v.memset(next_i[:], int(PAD_KEY))
                    v.memset(wgt_s[:], 0.0)
                    v.memset(wgt_d[:], 0.0)
                    v.drain().then_inc(s_pad, 1)
                    v.memset(rec_s[:], 0.0)
                    v.memset(rec_d[:], 0.0)
                    v.memset(ones[:], 1.0)
                    v.memset(eps[:], EPS)
                    dve.wait_ge(s_iota, 3)
                    c(v.tensor_scalar(ident[:], col[:], part[:], None, ALU.is_equal))
                    c(v.tensor_scalar(below[:], col[:], part[:], None, ALU.is_gt))
                    v.drain().then_inc(s_const, 1)
                    dve.wait_ge(s_in, 160)
                    for rec, key, other, weight in ((rec_s, src_i, dst_i, wgt_s), (rec_d, dst_i, src_i, wgt_d)):
                        c.step(v.tensor_copy(rec[:, :, 0], key[:]))
                        c.step(v.tensor_copy(rec[:, :, 1], other[:]))
                        c.step(v.tensor_copy(rec[:, :, 2], weight[:]))
                    c.wait()
                    v.drain().then_inc(s_recd, 1)
                    c(v.tensor_tensor(equal[:, 0, :], dst_i[:], next_i[:], ALU.is_gt))
                    c(v.tensor_reduce(falls[:], equal[:, 0, :], AX.X, ALU.add))
                    v.drain().then_inc(s_fl, 1)
                    sort_digit(c, rec_d, digit, False)
                    with c.loop(NT, 1) as b:
                        c(v.tensor_scalar(equal[:, 0, :], digit[:], col[:, bass.ds(b, 1)], 0.0, ALU.is_equal, ALU.add,
                                                 accum_out=tot[:, bass.ds(b, 1)]))
                    c.wait()
                    v.drain().then_inc(s_fl, 1)
                    dve.wait_ge(s_fm, 2)
                    c(v.tensor_copy(cnt_d[:], bank[1][:, 128:128 + NT]))
                    c(v.tensor_scalar(falls1[:], bank[1][0:1, 0:1], 1.0, None, ALU.min))
                    c(v.tensor_copy(disorder[:], falls1[:]))
                    rank_v(dve, c, rec_s, False, NT)
                    c(v.tensor_copy(cnt_s[:], cnt[:, 0:NT]))

                @block.tensor
                def _(pe):
                    pe.wait_ge(s_fl, 1)
                    nc.tensor.matmul(bank[1][:, 0:1], ones[:], falls[:], start=True, stop=True).then_inc(s_fm, 1)
                    pe.wait_ge(s_fl, 2)
                    nc.tensor.matmul(bank[1][:, 128:128 + NT], ones[:], tot[:, 0:NT], start=True, stop=True).then_inc(s_fm, 1)
                    rank_t(pe, NT)
                    pe.wait_ge(s_wt, 1)
                    for i, heads in enumerate((HEADS, 1)):
                        for k in range(KD):
                            for m in range(KD):
                                nc.tensor.transpose(bank[2 + 3 * i + k][:, m * 128:(m + 1) * 128], w_nat[i][:, m, k * 128:(k + 1) * 128], ident[:])
                        for k in range(KD):
                            for m in range(KD):
                                nc.tensor.matmul(bank[4 + 3 * i][:, k * 2 * heads:(k + 1) * 2 * heads], w_nat[i][:, m, k * 128:(k + 1) * 128],
                                                 a_blk[i][:, m, 0:2 * heads], start=(m == 0), stop=(m == KD - 1))
                    pe.drain().then_inc(s_wt, 1)

                @block.scalar
                def _(act):
                    act.wait_ge(s_wt, 2)
                    for i, heads in enumerate((HEADS, 1)):
                        for k in range(KD):
                            nc.scalar.activation(w_aug[i][:, k, 0:D], bank[2 + 3 * i + k][:, 0:D], ACT.Copy)
                            nc.scalar.activation(w_aug[i][:, k, D:D + 2 * heads], bank[4 + 3 * i][:, k * 2 * heads:(k + 1) * 2 * heads], ACT.Copy)
            end_stage()

            rec_u = rec_d
            place_keep = sb("place_keep", [128, EC], I32, scope)
            s_c, s_pl, s_sc, s_re = (sem(k) for k in ("sort_c", "sort_places", "sort_scattered", "sort_reload"))
            passes = [rank(f"rank{i}", tmp) for i in range(2)]
            with nc.Block() as block:
                @block.vector
                def _(dve):
                    flag = dve.value_load(disorder[0:1, 0:1], min_val=0, max_val=1)
                    with dve.If(flag != 0):
                        c = Chain(dve, s_c)
                        c(nc.vector.tensor_copy(place_keep[:], place_i[:]))
                        for i in range(2):
                            if i:
                                dve.wait_ge(s_re, 16)
                            passes[i][0](dve, c, rec_u, i == 0, TN if i == 0 else NT)
                            dve.drain().then_inc(s_pl, 1)
                            dve.wait_ge(s_sc, i + 1)
                        c(nc.vector.tensor_copy(place_i[:], place_keep[:]))

                @block.tensor
                def _(pe):
                    flag = pe.value_load(disorder[0:1, 0:1], min_val=0, max_val=1)
                    with pe.If(flag != 0):
                        for i in range(2):
                            passes[i][1](pe, TN if i == 0 else NT)

                @block.gpsimd
                def _(pool):
                    flag = pool.value_load(disorder[0:1, 0:1], min_val=0, max_val=1)
                    with pool.If(flag != 0):
                        for i in range(2):
                            pool.wait_ge(s_pl, i + 1)
                            scatter(f"sort{i}", pool, rec_u, rec_dst if i else rec_half, 0, EC // (2 * SH))
                            pool.sem_inc(s_sc, 1)

                @block.sync
                def _(sp):
                    flag = sp.value_load(disorder[0:1, 0:1], min_val=0, max_val=1)
                    with sp.If(flag != 0):
                        sp.wait_ge(s_sc, 1)
                        sp.dma_start(rec_u[:], rec_half.rearrange("(p j) f -> p j f", p=128)).then_inc(s_re, 16)
                        sp.wait_ge(s_re, 16)
            end_stage()

        def items(block, scope, name, which, recs, counts, it, attention):
            t25 = [sb(f"{name}_b{i}", [128, NT], F32, scope) for i in range(8)]
            start, end, sc, ec, n, ib, dl, tmp = t25
            ge = sb(name + "_ge", [IP, IQ, NT], F32, scope)
            gd = sb(name + "_gd", [IP, IQ, NT], F32, scope)
            tcol = sb(name + "_tcol", [IP, IQ], F32, scope)
            jcol = sb(name + "_jcol", [IP, IQ], F32, scope)
            tcol_i = sb(name + "_tcol_i", [IP, IQ], I32, scope)
            jcol_i = sb(name + "_jcol_i", [IP, IQ], I32, scope)
            rows = sb(name + "_rows", [IP, IQ, CH * 4], F32, scope)
            loc = sb(name + "_loc", [IP, IQ, CH], F32, scope)
            oth = sb(name + "_oth", [IP, IQ, CH], F32, scope)
            wg = sb(name + "_wg", [IP, IQ, CH], F32, scope)
            hi = sb(name + "_hi", [IP, IQ, CH], F32, scope)
            lo = sb(name + "_lo", [IP, IQ, CH], F32, scope)
            loc_b = sb(name + "_loc_b", [IP, IQ, CH], BF16, scope)
            lo_b = sb(name + "_lo_b", [IP, IQ, CH], BF16, scope)
            prev = sb(name + "_prev", [IP, 2], F32, scope)
            whole = sb(name + "_whole", [IP, 2], F32, scope)
            s_c, s_j, s_rows, s_t, s_tl, s_rw, s_tr, s_ed, s_b = (sem(name + k) for k in (
                "_c", "_j", "_rows", "_t", "_tl", "_rw", "_tr", "_ed", "_b"))
            f = rows[:].rearrange("p q (s f) -> p q s f", f=4)
            key = f[:, :, :, 0]

            @block.vector
            def _(dve):
                c = Chain(dve, s_c)
                v = nc.vector

                def floor128(o, i):
                    c(v.tensor_scalar(o[:], i[:], 1.0 / CH, -0.498, ALU.mult, ALU.add))
                    c(v.tensor_scalar(o[:], o[:], ROUND, ROUND, ALU.add, ALU.subtract))

                c(v.tensor_tensor_scan(end[:], counts[:], counts[:], 0.0, ALU.add, ALU.bypass))
                c(v.tensor_tensor(start[:], end[:], counts[:], ALU.subtract))
                c(v.tensor_scalar(end[:], end[:], -1.0, None, ALU.add))
                floor128(sc, start)
                floor128(ec, end)
                c(v.tensor_tensor(n[:], ec[:], sc[:], ALU.subtract))
                c(v.tensor_scalar(tmp[:], counts[:], 0.0, None, ALU.is_gt))
                c(v.scalar_tensor_tensor(n[:], n[:], 1.0, tmp[:], ALU.add, ALU.mult))
                c(v.tensor_tensor_scan(ib[:], n[:], n[:], 0.0, ALU.add, ALU.bypass))
                c(v.tensor_tensor(ib[:], ib[:], n[:], ALU.subtract))
                c(v.tensor_tensor(tmp[:], sc[:], ib[:], ALU.subtract))
                c(v.tensor_copy(dl[:], tmp[:]))
                c(v.tensor_tensor(dl[:, 1:NT], tmp[:, 1:NT], tmp[:, 0:NT - 1], ALU.subtract))
                c(v.tensor_tensor(ge[:], item_no[0:IP, :].unsqueeze(2).to_broadcast([IP, IQ, NT]),
                                  ib[0:IP, :].unsqueeze(1).to_broadcast([IP, IQ, NT]), ALU.is_ge))
                c(v.tensor_reduce(tcol[:], ge[:], AX.X, ALU.add))
                c(v.tensor_scalar(tcol[:], tcol[:], -1.0, None, ALU.add))
                c(v.tensor_tensor(gd[:], ge[:], dl[0:IP, :].unsqueeze(1).to_broadcast([IP, IQ, NT]), ALU.mult))
                c(v.tensor_reduce(jcol[:], gd[:], AX.X, ALU.add))
                c(v.tensor_tensor(jcol[:], jcol[:], item_no[0:IP, :], ALU.add))
                c(v.tensor_scalar(jcol[:], jcol[:], float(EC - 1), None, ALU.min))
                c(v.tensor_copy(jcol_i[:], jcol[:]))
                c(v.tensor_copy(tcol_i[:], tcol[:]))
                dve.drain().then_inc(s_j, 1)
                dve.wait_ge(s_rows, 16 * IQ)
                c(v.scalar_tensor_tensor(loc[:], tcol[:].unsqueeze(2).to_broadcast([IP, IQ, CH]), -float(TN), key, ALU.mult, ALU.add))
                c(v.tensor_scalar(oth[:], f[:, :, :, 1], float(N - 1), None, ALU.min))
                c(v.tensor_scalar(hi[:], oth[:], 1.0 / TN, -0.496, ALU.mult, ALU.add))
                c(v.tensor_scalar(hi[:], hi[:], ROUND, ROUND, ALU.add, ALU.subtract))
                c(v.scalar_tensor_tensor(lo[:], hi[:], -float(TN), oth[:], ALU.mult, ALU.add))
                c(v.tensor_copy(wg[:], f[:, :, :, 2]))
                c(v.tensor_copy(loc_b[:], loc[:]))
                c(v.tensor_copy(lo_b[:], lo[:]))
                dve.drain().then_inc(s_rw, 1)
                if attention:
                    k2 = rows[:].rearrange("p q (s f) -> p (q s) f", f=4)[:, :, 0]
                    L = IQ * CH
                    c(v.memset(same_f[:], 1.0))
                    c(v.memset(same_b[:], 1.0))
                    c(v.tensor_tensor(same_f[:, 1:L], k2[:, 1:L], k2[:, 0:L - 1], ALU.not_equal))
                    c(v.tensor_tensor(same_b[:, 0:L - 1], k2[:, 1:L], k2[:, 0:L - 1], ALU.not_equal))
                    c(v.tensor_scalar(same_f[:], same_f[:], -BIG, None, ALU.mult))
                    c(v.tensor_scalar(same_b[:], same_b[:], -BIG, None, ALU.mult))
                    c(v.memset(prev[:], -5.0))
                    dve.drain().then_inc(s_b, 1)
                    dve.wait_ge(s_ed, 32 + 32)
                    c(v.tensor_tensor(link[:, 0:1], prev[:, 0:1], k2[:, 0:1], ALU.not_equal))
                    c(v.tensor_tensor(link[:, 1:2], prev[:, 1:2], k2[:, L - 1:L], ALU.not_equal))
                    c(v.tensor_tensor(whole[:, 0:1], k2[:, 0:1], k2[:, L - 1:L], ALU.not_equal))
                    c(v.tensor_scalar(link[:, 2:4], link[:, 0:2], whole[:, 0:1], None, ALU.max))
                    c(v.tensor_scalar(link[:], link[:], -BIG, None, ALU.mult))
                dve.wait_ge(s_tr, 1)
                for b, to in ((0, it["local"]), (1, it["index"]), (2, it["weight"]), (3, high)):
                    if b == 3 and not attention:
                        continue
                    v.tensor_copy(to[:].rearrange("e (p q) -> e q p", q=IQ),
                                  bank[b][:, 0:NI].rearrange("e (q p) -> e q p", q=IQ))

            @block.gpsimd
            def _(pool):
                pool.wait_ge(s_j, 1)
                for q in range(IQ):
                    nc.gpsimd.indirect_dma_start(rows[:, q, :], None, recs.rearrange("(c s) f -> c (s f)", s=CH),
                                                 bass.IndirectOffsetOnAxis(ap=jcol_i[:, q:q + 1], axis=0)).then_inc(s_rows, 16)

            @block.sync
            def _(sp):
                sp.wait_ge(s_j, 1)
                sp.dma_start(tile_tab[which].rearrange("(p q) -> p q", q=IQ), tcol_i[:]).then_inc(s_t, 16)
                sp.wait_ge(s_t, 16)
                sp.dma_start(it["tiles"][:], tile_tab[which].rearrange("(o n) -> o n", o=1)).then_inc(s_tl, 16)
                if attention:
                    sp.wait_ge(s_rw, 1)
                    sp.dma_start(row_local.rearrange("(p n) -> p n", p=IP), loc_b[:].rearrange("p q s -> p (q s)")).then_inc(s_tl, 16)
                    sp.dma_start(row_other.rearrange("(p n) -> p n", p=IP), lo_b[:].rearrange("p q s -> p (q s)")).then_inc(s_tl, 16)
                    sp.wait_ge(s_b, 1)
                    for i, q, s in ((0, IQ - 1, CH - 1), (1, 0, 0)):
                        sp.dma_start(edge_tab[i:i + 1, :].rearrange("o p -> p o"), f[:, q, s, 0:1]).then_inc(s_ed, 16)
                    sp.wait_ge(s_ed, 32)
                    sp.dma_start(prev[1:IP, 0:1], edge_tab[0:1, 0:IP - 1].rearrange("o p -> p o")).then_inc(s_ed, 16)
                    sp.dma_start(prev[0:IP - 1, 1:2], edge_tab[1:2, 1:IP].rearrange("o p -> p o")).then_inc(s_ed, 16)
                    sp.wait_ge(s_ed, 64)
                sp.wait_ge(s_tl, 48 if attention else 16)

            @block.tensor
            def _(pe):
                pe.wait_ge(s_rw, 1)
                for b, t in enumerate((loc, oth, wg, hi)):
                    for q in range(IQ):
                        nc.tensor.transpose(bank[b][:, q * IP:(q + 1) * IP], t[:, q, :], ident[0:IP, 0:IP])
                pe.drain().then_inc(s_tr, 1)


        def row_stats(block, name):
            s_c, s_v, s_q = sem(name + "_c"), sem(name + "_v"), sem(name + "_q")
            st = stats[:].rearrange("p (t s) -> p t s", s=6)

            @block.vector
            def _(dve):
                c = Chain(dve, s_c)
                v = nc.vector
                with dve.Fori(0, NT) as t:
                    v.bn_stats(stats[:, bass.ds(t * 6, 6)], x_flat[:, bass.ds(t * D, D)])
                c(dve.drain())
                c(v.tensor_tensor(mean[:], st[:, :, 1], st[:, :, 4], ALU.add))
                c(v.tensor_scalar(mean[:], mean[:], 0.5, None, ALU.mult))
                c(v.tensor_tensor(spread[:], st[:, :, 1], st[:, :, 4], ALU.subtract))
                c(v.scalar_tensor_tensor(spread[:], spread[:], 0.25, spread[:], ALU.mult, ALU.mult))
                c(v.tensor_tensor(rstd[:], st[:, :, 2], st[:, :, 5], ALU.add))
                c(v.scalar_tensor_tensor(rstd[:], rstd[:], 1.0 / D, spread[:], ALU.mult, ALU.add))
                dve.drain().then_inc(s_v, 1)
                dve.wait_ge(s_q, 1)
                c(v.reciprocal(rstd[:], rstd[:]))

            @block.scalar
            def _(act):
                act.wait_ge(s_v, 1)
                nc.scalar.activation(rstd[:], rstd[:], ACT.Sqrt, bias=eps[0:TN, :]).then_inc(s_q, 1)

        def project(block, scope, name, srcs, weights, bias, width, func, finish, store, prepare=None, act_ahead=None):
            K = KD * srcs
            s_h, s_tr, s_ht, s_z, s_zc, s_c = (sem(name + k) for k in ("_h", "_tr", "_ht", "_z", "_zc", "_c"))
            s_w = [sem(name + f"_w{b}") for b in range(2)]
            hbuf = sb(name + "_hbuf", [TN, 2, K * 128], F32, scope)
            h_t = sb(name + "_h_t", [128, 2, K, TN], F32, scope)
            res = sb(name + "_res", [TN, 2, width], F32, scope)
            nb = (K + 3) // 4
            flow = Flow(hbuf=hbuf, res=res, s_tr=s_tr, s_h=s_h, s_zc=s_zc, s_w=s_w)

            def product(b):
                return bank[4 + b][0:TN, 0:width]

            @block.vector
            def _(dve):
                dve.sem_inc(s_h, 2)
                prepare(dve, Chain(dve, s_c), flow)

            @block.tensor
            def _(pe):
                pe.sem_inc(s_tr, 2)
                pe.sem_inc(s_z, 2)

                def ahead(n, b, r):
                    pe.wait_ge(s_h, n + 3)
                    pe.wait_ge(s_ht, n + 1)
                    for k in range(K):
                        last = nc.tensor.transpose(bank[2 * b + k // 4][:, (k % 4) * TN:(k % 4 + 1) * TN],
                                                   hbuf[:, b, k * 128:(k + 1) * 128], ident[0:TN, 0:TN])
                    last.then_inc(s_tr, 1)

                def behind(n, b, r):
                    pe.wait_ge(s_ht, n + 3)
                    pe.wait_ge(s_zc, n + 1)
                    for k in range(K):
                        last = nc.tensor.matmul(product(b), h_t[:, b, k, :], weights[:, k, 0:width],
                                                start=(k == 0), stop=(k == K - 1 and bias is None))
                    if bias is not None:
                        last = nc.tensor.matmul(product(b), ones[0:1, 0:TN], bias[:], start=False, stop=True)
                    last.then_inc(s_z, 1)

                skewed(pe, NT, ahead, behind)

            @block.scalar
            def _(act):
                act.sem_inc(s_ht, 2)
                act.sem_inc(s_zc, 2)

                def ahead(n, b, r):
                    if act_ahead is not None:
                        act_ahead(act, n, b)
                    act.wait_ge(s_tr, n + 3)
                    act.wait_ge(s_z, n + 1)
                    for k in range(nb):
                        m = min(4, K - 4 * k)
                        last = nc.scalar.activation(h_t[:, b, 4 * k:4 * k + m, :],
                                                    bank[2 * b + k][:, 0:m * TN].rearrange("p (k n) -> p k n", k=m), func)
                    last.then_inc(s_ht, 1)

                def behind(n, b, r):
                    act.wait_ge(s_z, n + 3)
                    act.wait_ge(s_w[b], r * 16 + 16)
                    finish(act, n, product(b), res[:, b, :]).then_inc(s_zc, 1)

                skewed(act, NT, ahead, behind)

            @block.sync
            def _(sp):
                for b in range(2):
                    sp.sem_inc(s_w[b], 16)

                alternate(sp, NT, lambda n, b, r: store(sp, n, b, flow))
                for b in range(2):
                    sp.wait_ge(s_w[b], 16 + 16 * ((NT + 1 - b) // 2))

        def attention_finish(heads):
            def finish(act, n, product, res):
                nc.scalar.activation(res[:, 0:D], product[:, 0:D], ACT.Copy)
                nc.scalar.activation(s_tab[:, 0:heads * NT].rearrange("p (h t) -> p h t", h=heads)[:, :, bass.ds(n, 1)],
                                     product[:, D:D + heads].unsqueeze(2), ACT.Copy)
                return nc.scalar.activation(d_tab[:, bass.ds(n * heads, heads)], product[:, D + heads:D + 2 * heads], ACT.Copy)
            return finish

        def table_store(table):
            def store(sp, n, b, flow):
                sp.wait_ge(flow.s_zc, n + 3)
                sp.dma_start(table[bass.ds(n * TN, TN), :], flow.res[:, b, 0:D]).then_inc(flow.s_w[b], 16)
            return store

        def split_tables(block, name, heads):
            s_c = sem(name)

            @block.vector
            def _(dve):
                c = Chain(dve, s_c)
                for tab, parts in ((s_tab, s_part), (d_tab, d_part)):
                    for k in range(3):
                        c(nc.vector.tensor_copy(parts[:, k, 0:heads * NT], tab[:, 0:heads * NT]))
                        if k < 2:
                            c(nc.vector.tensor_tensor(tab[:, 0:heads * NT], tab[:, 0:heads * NT], parts[:, k, 0:heads * NT], ALU.subtract))

        def edge_softmax(block, scope, name, H):
            s_lo, s_l, s_sum, s_c = (sem(name + k) for k in ("_sel", "_look", "_sum", "_c"))
            s_r = [sem(name + f"_row{b}") for b in range(2)]
            rows_l = sb(name + "_rows_l", [128, 2, G * CH], BF16, scope)
            rows_o = sb(name + "_rows_o", [128, 2, G * CH], BF16, scope)
            sel_l = sb(name + "_sel_l", [128, 2, G * CH], BF16, scope)
            sel_o = sb(name + "_sel_o", [128, 2, G * CH], BF16, scope)
            hot = sb(name + "_hot", [128, 2, G, NT], F32, scope)
            prod = sb(name + "_prod", [128, G, H, NT], F32, scope)
            es = sb(name + "_es", [128, G, H], F32, scope)
            e_all = sb(name + "_e", [128, H, NI], F32, scope)
            hg = G // 2 if H > 1 else G
            nb = G // hg

            def rows_of(row, n):
                return row.rearrange("(o n) -> o n", o=1)[:, bass.ds(n * (G * CH), G * CH)].to_broadcast([128, G * CH])

            @block.sync
            def _(sp):
                sp.sem_inc(s_lo, 2)

                def step(n, b, r):
                    sp.wait_ge(s_lo, n + 1)
                    sp.dma_start(rows_l[:, b, :], rows_of(row_local, n)).then_inc(s_r[b], 16)
                    sp.dma_start(rows_o[:, b, :], rows_of(row_other, n)).then_inc(s_r[b], 16)

                alternate(sp, NG, step)

            @block.vector
            def _(dve):
                c = Chain(dve, s_c)
                v = nc.vector
                dve.sem_inc(s_sum, 2)

                def select(n, b, r):
                    dve.wait_ge(s_r[b], r * 32 + 32)
                    dve.wait_ge(s_l, n + 1)
                    v.tensor_scalar(sel_l[:, b, :], rows_l[:, b, :], part[:], None, ALU.is_equal)
                    v.tensor_scalar(sel_o[:, b, :], rows_o[:, b, :], part[:], None, ALU.is_equal).then_inc(s_lo, 1)
                    c.step(v.tensor_tensor(hot[:, b], high[:, bass.ds(n * G, G)].unsqueeze(2).to_broadcast([128, G, NT]),
                                             col[:, 0:NT].unsqueeze(1).to_broadcast([128, G, NT]), ALU.is_equal))

                def sums(n, b, r):
                    dve.wait_ge(s_l, n + 3)
                    c.wait(1)
                    for k in range(nb):
                        c.step(v.tensor_tensor(prod[:, k * hg:(k + 1) * hg],
                                                 bank[b * 2 + k][:, 0:hg * H * NT].rearrange("e (g h t) -> e g h t", g=hg, h=H),
                                                 hot[:, b, k * hg:(k + 1) * hg].unsqueeze(2).to_broadcast([128, hg, H, NT]), ALU.mult))
                    c.wait()
                    c(v.tensor_reduce(es[:], prod[:], AX.X, ALU.add))
                    v.tensor_tensor(e_all[:, :, bass.ds(n * G, G)], es[:].rearrange("e g h -> e h g"),
                                    bank[4 + b][:, 0:G * H].rearrange("e (g h) -> e h g", h=H), ALU.add).then_inc(s_sum, 1)

                skewed(dve, NG, select, sums, c, 2 + nb)
                c(dve.drain())
                c(v.scalar_tensor_tensor(e_all[:], e_all[:], 0.01, e_all[:], ALU.mult, ALU.max))

            @block.tensor
            def _(pe):
                pe.sem_inc(s_l, 2)

                def step(n, b, r):
                    _, tiles = nc.values_load_multi_w_load_instructions(
                        it_d["tiles"][0:1, bass.ds(n * G, G)], engines=[mybir.EngineType.PE], min_val=0, max_val=NT - 1,
                        skip_runtime_bounds_check_because="the items' tiles are sums of at most NT marks, less one")
                    pe.wait_ge(s_lo, n + 3)
                    pe.wait_ge(s_sum, n + 1)
                    for k in range(G):
                        o = bank[b * 2 + k // hg][:, (k % hg) * H * NT:(k % hg + 1) * H * NT]
                        for m in range(3):
                            nc.tensor.matmul(o, sel_o[0:TN, b, k * CH:(k + 1) * CH], s_part[:, m, 0:H * NT],
                                             start=(m == 0), stop=(m == 2))
                    for k in range(G):
                        for m in range(3):
                            last = nc.tensor.matmul(bank[4 + b][:, k * H:(k + 1) * H], sel_l[0:TN, b, k * CH:(k + 1) * CH],
                                                    d_part[:, m, bass.ds(tiles[k] * H, H)], start=(m == 0), stop=(m == 2))
                    last.then_inc(s_l, 1)

                alternate(pe, NG, step)

            fence(block, name + "_f1")
            L = IQ * CH
            e_t = sb(name + "_e_t", [IP, H, L], F32, scope)
            fwd = sb(name + "_fwd", [IP, H, L], F32, scope)
            bwd = sb(name + "_bwd", [IP, H, L], F32, scope)
            res = sb(name + "_res", [IP, H, L], F32, scope)
            ends = sb(name + "_ends", [IP, 4, H], F32, scope)
            c_row = sb(name + "_c_row", [H, 4, IP], F32, scope)
            c_run = sb(name + "_c_run", [H, 2, IP], F32, scope)
            c_in = sb(name + "_c_in", [H, 2, IP], F32, scope)
            c_col = sb(name + "_c_col", [IP, 2, H], F32, scope)
            s_1, s_2, s_3, s_4, s_5, s_6, s_7, s_8 = (sem(name + f"_s{i}") for i in range(8))

            def scan(c, o, e, same, forward):
                r = res[:].rearrange("p h l -> p (h l)")
                c(nc.vector.tensor_copy(res[:], same[:].unsqueeze(1).to_broadcast([IP, H, L])))
                o, e = o[:].rearrange("p h l -> p (h l)"), e[:].rearrange("p h l -> p (h l)")
                if not forward:
                    o, e, r = o[:, ::-1], e[:, ::-1], r[:, ::-1]
                c(nc.vector.tensor_tensor_scan(o, r, e, -BIG, ALU.add, ALU.max))

            @block.tensor
            def _(pe):
                for h in range(H):
                    for q in range(IQ):
                        nc.tensor.transpose(bank[h][0:IP, q * CH:(q + 1) * CH],
                                            e_all[:, h, :].rearrange("e (p q) -> e q p", q=IQ)[:, q, :], ident[:])
                pe.drain().then_inc(s_1, 1)
                pe.wait_ge(s_3, 1)
                for k in range(4):
                    nc.tensor.transpose(bank[4][0:H, k * IP:(k + 1) * IP], ends[:, k, :], ident[0:IP, 0:IP])
                pe.drain().then_inc(s_4, 1)
                pe.wait_ge(s_5, 1)
                for k in range(2):
                    nc.tensor.transpose(bank[5][0:IP, k * H:(k + 1) * H], c_in[:, k, :], ident[0:H, 0:H])
                pe.drain().then_inc(s_6, 1)
                pe.wait_ge(s_7, 1)
                for h in range(H):
                    for q in range(IQ):
                        nc.tensor.transpose(bank[h][:, q * IP:(q + 1) * IP], fwd[:, h, q * CH:(q + 1) * CH], ident[0:IP, 0:IP])
                pe.drain().then_inc(s_8, 1)

            @block.scalar
            def _(act):
                act.wait_ge(s_1, 1)
                for h in range(H):
                    nc.scalar.activation(e_t[:, h, :], bank[h][0:IP, :], ACT.Copy)
                act.drain().then_inc(s_2, 1)

            @block.vector
            def _(dve):
                c = Chain(dve, sem(name + "_c2"))
                v = nc.vector
                dve.wait_ge(s_2, 1)
                scan(c, fwd, e_t, same_f, True)
                scan(c, bwd, e_t, same_b, False)
                c(v.tensor_copy(ends[:, 0, :], fwd[:, :, L - 1]))
                c(v.tensor_copy(ends[:, 1, :], bwd[:, :, 0]))
                c(v.tensor_copy(ends[:, 2:4, :], link[:, 2:4].unsqueeze(2).to_broadcast([IP, 2, H])))
                dve.drain().then_inc(s_3, 1)
                dve.wait_ge(s_4, 1)
                c(v.tensor_copy(c_row[:], bank[4][0:H, 0:4 * IP].rearrange("h (k p) -> h k p", k=4)))
                c(v.tensor_tensor_scan(c_run[:, 0, :], c_row[:, 2, :], c_row[:, 0, :], -BIG, ALU.add, ALU.max))
                c(v.tensor_tensor_scan(c_run[:, 1, ::-1], c_row[:, 3, ::-1], c_row[:, 1, ::-1], -BIG, ALU.add, ALU.max))
                c(v.memset(c_in[:], -BIG))
                c(v.tensor_copy(c_in[:, 0, 1:IP], c_run[:, 0, 0:IP - 1]))
                c(v.tensor_copy(c_in[:, 1, 0:IP - 1], c_run[:, 1, 1:IP]))
                dve.drain().then_inc(s_5, 1)
                dve.wait_ge(s_6, 1)
                for k, at in ((0, 0), (1, L - 1)):
                    c(v.tensor_scalar(c_col[:, k, :], bank[5][0:IP, k * H:(k + 1) * H], link[:, k:k + 1], None, ALU.add))
                    c(v.tensor_tensor(e_t[:, :, at], e_t[:, :, at], c_col[:, k, :], ALU.max))
                scan(c, fwd, e_t, same_f, True)
                scan(c, bwd, e_t, same_b, False)
                c(v.tensor_tensor(fwd[:], fwd[:], bwd[:], ALU.max))
                dve.drain().then_inc(s_7, 1)
                dve.wait_ge(s_8, 1)
                for h in range(H):
                    c(v.tensor_tensor(e_all[:, h, :].rearrange("e (p q) -> e q p", q=IQ),
                                      e_all[:, h, :].rearrange("e (p q) -> e q p", q=IQ),
                                      bank[h][:, 0:NI].rearrange("e (q p) -> e q p", q=IQ), ALU.subtract))

            fence(block, name + "_f2")

            @block.scalar
            def _(act):
                nc.scalar.activation(w_all[:, 0:NI * H].rearrange("e (n h) -> e h n", h=H), e_all[:], ACT.Exp)

        def aggregate(name, table, it, W, into, weight=None, heads=1):
            s_g = [sem(name + f"_g{k}") for k in range(RB)]
            s_ix, s_half, s_use, s_sel, s_mm, s_add, s_z, s_turn = (
                sem(name + k) for k in ("_ix", "_half", "_use", "_sel", "_mm", "_add", "_z", "_turn"))
            IXB = 4
            UN = IXB * G
            HH = heads // 2
            with ExitStack() as scope:
                ix = sb(name + "_ixb", [128, UN], I32, scope)
                rows = sb(name + "_rowb", [128, RB, D + 1], F32, scope)
                sel = sb(name + "_selb", [128, RING, TN], F32, scope)
                scaled = sb(name + "_scl", [128, RING, D], F32, scope) if heads > 1 else None
                with nc.Block() as block:
                    @block.gpsimd
                    def _(pool):
                        pool.wait_ge(s_z, 1)

                        def turn(i, begin=False):
                            for g in range(IXB):
                                pool.wait_ge(s_ix, i * IXB + (g + 1))
                                pool.sem_inc(s_turn, 1)
                                for k in range(g * G, (g + 1) * G):
                                    if k % 4 == 0 and not (begin and k < RB):
                                        used = i * UN + (k + 4 - RB)
                                        if heads == 1:
                                            pool.wait_ge(s_mm, used + RING)
                                        else:
                                            pool.wait_ge(s_use, used)
                                            pool.wait_ge(s_half, used)
                                        pool.sem_inc(s_turn, 1)
                                    nc.gpsimd.indirect_dma_start(rows[:, k % RB, 0:D], None, table,
                                                                 bass.IndirectOffsetOnAxis(ap=ix[:, k:k + 1], axis=0)).then_inc(s_g[k % RB], 16)
                        turn(0, True)
                        with pool.Fori(1, NI // UN) as i:
                            turn(i)

                    @block.scalar
                    def _(act):
                        def indices(i, g, begin=False):
                            if not begin:
                                act.wait_ge(s_mm, (i - 1) * UN + ((g + 1) * G + RING))
                            nc.scalar.activation(ix[:, g * G:(g + 1) * G], it["index"][:, bass.ds((i * IXB + g) * G, G)], ACT.Copy).then_inc(s_ix, 1)

                        def scale(n, k, r):
                            act.wait_ge(s_g[k], r * 16 + 16)
                            act.wait_ge(s_mm, n + 1)
                            for h in range(HH):
                                last = nc.scalar.activation(scaled[:, k % RING, h * HID:(h + 1) * HID], rows[:, k, h * HID:(h + 1) * HID],
                                                            ACT.Copy, scale=w_all[:, bass.ds(n * HEADS + h, 1)])
                            last.then_inc(s_half, 1)

                        if heads == 1:
                            for g in range(IXB):
                                indices(0, g, True)
                            with act.Fori(1, NI // UN) as i:
                                for g in range(IXB):
                                    indices(i, g)
                        else:
                            for g in range(IXB):
                                indices(0, g, True)

                            with act.Fori(0, NI // UN - 1) as i:
                                for g in range(IXB):
                                    for k in range(g * G, (g + 1) * G):
                                        scale(i * UN + k, k % RB, i * (UN // RB) + k // RB)
                                    if g >= 1:
                                        indices(i + 1, g - 1)
                                indices(i + 1, IXB - 1)
                            i = NI // UN - 1
                            for k in range(UN):
                                scale(i * UN + k, k % RB, i * (UN // RB) + k // RB)

                    @block.vector
                    def _(dve):
                        nc.vector.memset(into, 0.0)
                        nc.vector.memset(rows[:, :, D:D + 1], 1.0)
                        dve.drain().then_inc(s_z, 1)
                        dve.wait_ge(s_z, 1)
                        dve.sem_inc(s_mm, RING)
                        dve.sem_inc(s_add, RING)

                        def make(n, k, r):
                            dve.wait_ge(s_mm, n + 1)
                            o = sel[:, k % RING, :]
                            if heads == 1:
                                nc.vector.tensor_scalar(o, col[:, 0:TN], it["local"][:, bass.ds(n, 1)],
                                                        weight[:, bass.ds(n, 1)], ALU.is_equal, ALU.mult).then_inc(s_sel, 1)
                            else:
                                nc.vector.tensor_scalar(o, col[:, 0:TN], it["local"][:, bass.ds(n, 1)],
                                                        None, ALU.is_equal).then_inc(s_sel, 1)
                                dve.wait_ge(s_g[k], r * 16 + 16)
                                wv = w_all[:, bass.ds(n * HEADS + HH, HEADS - HH)]
                                nc.vector.tensor_tensor(scaled[:, k % RING, HH * HID:].rearrange("e (h o) -> e h o", o=HID),
                                                        rows[:, k, HH * HID:D].rearrange("e (h o) -> e h o", o=HID),
                                                        wv.unsqueeze(2).to_broadcast([128, HEADS - HH, HID]), ALU.mult).then_inc(s_use, 1)

                        def tiles_of(n):
                            return nc.values_load_multi_w_load_instructions(
                                it["tiles"][0:1, bass.ds(n, RB)], engines=[mybir.EngineType.DVE], min_val=0, max_val=NT - 1,
                                skip_runtime_bounds_check_because="the items' tiles are sums of at most NT marks, less one")[1]

                        def add(n, k, t):
                            dve.wait_ge(s_mm, n + (1 + RING))
                            dve.wait_ge(s_add, n + RING)
                            o = into[:, bass.ds(t * W, W)]
                            nc.vector.tensor_tensor(o, o, bank[k % RING][0:TN, 0:W], ALU.add).then_inc(s_add, 1)

                        for k in range(LEAD):
                            make(k, k, 0)
                        turns = NI // RB
                        with dve.Fori(0, turns - 1) as i:
                            tiles = tiles_of(i * RB)
                            for k in range(RB):
                                make(i * RB + (k + LEAD), (k + LEAD) % RB, i + (k + LEAD) // RB)
                                add(i * RB + k, k, tiles[k])
                        at = (turns - 1) * RB
                        tiles = tiles_of(at)
                        for k in range(RB):
                            if k + LEAD < RB:
                                make(at + k + LEAD, k + LEAD, turns - 1)
                            add(at + k, k, tiles[k])

                    @block.tensor
                    def _(pe):
                        with pe.Fori(0, NI // RB) as i:
                            for k in range(RB):
                                n = i * RB + k
                                o = bank[k % RING][0:TN, :]
                                pe.wait_ge(s_sel, n + 1)
                                pe.wait_ge(s_add, n + 1)
                                if heads == 1:
                                    pe.wait_ge(s_g[k], i * 16 + 16)
                                    nc.tensor.matmul(o[:, 0:W], sel[:, k % RING, :], rows[:, k, 0:W], start=True, stop=True).then_inc(s_mm, 1)
                                else:
                                    nc.tensor.matmul(o[:, D:W], sel[:, k % RING, :], w_all[:, bass.ds(n * HEADS, HEADS)], start=True, stop=True)
                                    pe.wait_ge(s_use, n + 1)
                                    pe.wait_ge(s_half, n + 1)
                                    nc.tensor.matmul(o[:, 0:D], sel[:, k % RING, :], scaled[:, k % RING, :], start=True, stop=True).then_inc(s_mm, 1)
                end_stage()

        ROUNDS = EC // (2 * SH)
        part1, part2 = 8, 11

        def prep_norm(dve, c, flow):
            def step(n, b, r):
                dve.wait_ge(flow.s_tr, n + 1)
                nc.vector.tensor_scalar(flow.hbuf[:, b, :], x_flat[:, bass.ds(n * D, D)], mean[:, bass.ds(n, 1)], rstd[:, bass.ds(n, 1)],
                                        ALU.subtract, ALU.mult).then_inc(flow.s_h, 1)
            alternate(dve, NT, step)

        with ExitStack() as scope:
            with nc.Block() as block:
                with ExitStack() as inner:
                    items(block, inner, "id", 1, rec_dst, cnt_d, it_d, True)

                @block.gpsimd
                def _(pool):
                    scatter("sc1", pool, rec_s, rec_src, 0, part1)

                fence(block, "f1")
                row_stats(block, "st1")
                fence(block, "f2")
                with ExitStack() as inner:
                    project(block, inner, "pr1", 1, w_aug[0], None, D + 2 * HEADS, ACT.Relu, attention_finish(HEADS),
                            table_store(z_tab), prepare=prep_norm)
                fence(block, "f3")
                split_tables(block, "sp1", HEADS)
                fence(block, "f4")
                with ExitStack() as inner:
                    edge_softmax(block, inner, "es1", HEADS)
            end_stage()

        W = D + HEADS
        aggregate("ag1", z_tab, it_d, W, acc[:], heads=HEADS)

        with ExitStack() as scope:
            inv = sb("inv", [TN, NT, HEADS], F32, scope)
            up = sb("up", [TN, 2, D], F32, scope)
            neg = sb("neg", [TN, 2, D], F32, scope)
            ex = sb("ex", [TN, 2, D], F32, scope)
            s_mn, s_ex = sem("s_mn"), sem("s_ex")

            def prep_elu(dve, c, flow):
                v = nc.vector
                c(v.tensor_scalar(inv[:], acc[:].rearrange("p (t w) -> p t w", w=W)[:, :, D:W], 1e-30, None, ALU.max))
                c(v.reciprocal(inv[:], inv[:]))

                def ahead(n, b, r):
                    dve.wait_ge(flow.s_h, n + 1)
                    c(v.tensor_tensor(up[:, b, :].rearrange("p (h o) -> p h o", h=HEADS),
                                      acc[:, bass.ds(n * W, D)].rearrange("p (h o) -> p h o", h=HEADS),
                                      inv[:].rearrange("p t h -> p (t h)")[:, bass.ds(n * HEADS, HEADS)].unsqueeze(2).to_broadcast([TN, HEADS, HID]), ALU.mult))
                    v.tensor_scalar(neg[:, b, :], up[:, b, :], 0.0, None, ALU.min).then_inc(s_mn, 1)
                    c.step(v.tensor_scalar(up[:, b, :], up[:, b, :], 0.0, -1.0, ALU.max, ALU.add))

                def behind(n, b, r):
                    dve.wait_ge(flow.s_tr, n + 1)
                    dve.wait_ge(s_ex, n + 1)
                    c.wait(2)
                    v.tensor_tensor(flow.hbuf[:, b, :], up[:, b, :], ex[:, b, :], ALU.add).then_inc(flow.s_h, 1)

                skewed(dve, NT, ahead, behind, c, 2)

            def exp_step(act, n, b):
                act.wait_ge(s_mn, n + 1)
                nc.scalar.activation(ex[:, b, :], neg[:, b, :], ACT.Exp).then_inc(s_ex, 1)

            with nc.Block() as block:
                @block.gpsimd
                def _(pool):
                    scatter("sc2", pool, rec_s, rec_src, part1, part2)

                with ExitStack() as inner:
                    project(block, inner, "pr2", 1, w_aug[1], None, D + 2, ACT.Copy, attention_finish(1), table_store(z2_tab),
                            prepare=prep_elu, act_ahead=exp_step)
                fence(block, "f5")
                split_tables(block, "sp2", 1)
                fence(block, "f6")
                with ExitStack() as inner:
                    edge_softmax(block, inner, "es2", 1)
            end_stage()

        W_ = D + 1
        aggregate("ag2", z2_tab, it_d, W_, acc[:, 0:NT * W_], weight=w_all)

        hb = sb("hb", [TN, NT, D])
        hb_flat = hb[:].rearrange("p t d -> p (t d)")
        a_out = sb("a_out", [TN, NT * D])
        sq = a_out[:].rearrange("p (t d) -> p t d", d=D)
        vec = sb("vec", [TN, 4, D])
        w_io = sb("w_io", [128, KD, 2 * D])
        w_g = sb("w_g", [128, 3 * KD, 2 * D])
        b_io = sb("b_io", [1, 2 * D])
        b_g = sb("b_g", [1, 2 * D])
        s_rc, s_c, s_p, s_p2, s_v, s_q, s_w = (sem("bn" + k) for k in ("_rc", "_c", "_p", "_p2", "_v", "_q", "_w"))
        with nc.Block() as block:
            @block.gpsimd
            def _(pool):
                scatter("sc3", pool, rec_s, rec_src, part2, ROUNDS)

            @block.sync
            def _(sp):
                for to, of in ((vec[:, 0, :], gamma.rearrange("(o d) -> o d", o=1).to_broadcast([TN, D])),
                               (vec[:, 1, :], beta.rearrange("(o d) -> o d", o=1).to_broadcast([TN, D])),
                               (w_io[:, :, 0:D], W_in.rearrange("(k p) n -> p k n", p=128)),
                               (w_io[:, :, D:2 * D], W_out.rearrange("(k p) n -> p k n", p=128)),
                               (w_g[:, 0:2 * KD, :], W_x2i.rearrange("(k p) n -> p k n", p=128)),
                               (w_g[:, 2 * KD:3 * KD, :], W_h2h.rearrange("(k p) n -> p k n", p=128)),
                               (b_io[:, 0:D], b_in.rearrange("(o d) -> o d", o=1)),
                               (b_io[:, D:2 * D], b_out.rearrange("(o d) -> o d", o=1)),
                               (b_g[:], b_x2i.rearrange("(o d) -> o d", o=1))):
                    sp.dma_start(to, of).then_inc(s_w, 16)
                sp.wait_ge(s_w, 16 * 9)

            @block.vector
            def _(dve):
                c = Chain(dve, s_rc)
                a3 = acc[:, 0:NT * W_].rearrange("p (t w) -> p t w", w=W_)
                c(nc.vector.tensor_scalar(spread[:], a3[:, :, D], 1e-30, None, ALU.max))
                c(nc.vector.reciprocal(spread[:], spread[:]))
                c(nc.vector.tensor_tensor(a3[:, :, 0:D], a3[:, :, 0:D], spread[:].unsqueeze(2).to_broadcast([TN, NT, D]), ALU.mult))
                c(nc.vector.tensor_tensor(x_sb[:], x_sb[:], a3[:, :, 0:D], ALU.add))

            row_stats(block, "st2")

            @block.vector
            def _(dve):
                c = Chain(dve, s_c)
                v = nc.vector

                def wide(a):
                    return a.unsqueeze(2).to_broadcast([TN, NT, D])

                def tall(k):
                    return vec[:, k:k + 1, :].to_broadcast([TN, NT, D])

                c(v.tensor_tensor(hb[:], x_sb[:], wide(mean[:]), ALU.subtract))
                c(v.tensor_tensor(hb[:], hb[:], wide(rstd[:]), ALU.mult))
                c(v.tensor_scalar(hb[:], hb[:], 0.0, None, ALU.max))
                dve.drain().then_inc(s_v, 1)
                dve.wait_ge(s_p, 1)
                c(v.tensor_scalar(vec[:, 2, :], bank[0][0:TN, 0:D], 1.0 / N, None, ALU.mult))
                c(v.tensor_tensor(hb[:], hb[:], tall(2), ALU.subtract))
                c(v.tensor_tensor(sq, hb[:], hb[:], ALU.mult))
                dve.drain().then_inc(s_v, 1)
                dve.wait_ge(s_p2, 1)
                c(v.tensor_scalar(vec[:, 3, :], bank[1][0:TN, 0:D], 1.0 / N, None, ALU.mult))
                dve.drain().then_inc(s_v, 1)
                dve.wait_ge(s_q, 1)
                c(v.reciprocal(vec[:, 3, :], vec[:, 3, :]))
                dve.wait_ge(s_w, 16 * 9)
                c(v.tensor_tensor(vec[:, 3, :], vec[:, 3, :], vec[:, 0, :], ALU.mult))
                c(v.tensor_tensor(hb[:], hb[:], tall(3), ALU.mult))
                c(v.tensor_tensor(hb[:], hb[:], tall(1), ALU.add))

            @block.scalar
            def _(act):
                act.wait_ge(s_v, 3)
                nc.scalar.activation(vec[:, 3, :], vec[:, 3, :], ACT.Sqrt, bias=eps[0:TN, :]).then_inc(s_q, 1)

            @block.tensor
            def _(pe):
                for i, (t, s) in enumerate(((hb[:], s_p), (sq, s_p2))):
                    pe.wait_ge(s_v, i + 1)
                    for k in range(NT):
                        last = nc.tensor.matmul(bank[i][0:TN, 0:D], ones[0:TN, 0:TN], t[:, k, :], start=(k == 0), stop=(k == NT - 1))
                    last.then_inc(s, 1)

            fence(block, "f7")

            def prep_copy(dve, c, flow):
                def step(n, b, r):
                    dve.wait_ge(flow.s_tr, n + 1)
                    nc.vector.tensor_copy(flow.hbuf[:, b, :], hb_flat[:, bass.ds(n * D, D)]).then_inc(flow.s_h, 1)
                alternate(dve, NT, step)

            def io_finish(act, n, product, res):
                return nc.scalar.activation(res, product, ACT.Copy)

            s_w2 = sem("fout_w")

            def io_store(sp, n, b, flow):
                sp.wait_ge(flow.s_zc, n + 3)
                sp.dma_start(fout_tab[bass.ds(n * TN, TN), :], flow.res[:, b, D:2 * D]).then_inc(s_w2, 16)
                sp.wait_ge(s_w2, n * 16 + 16)
                sp.dma_start(fin_tab[bass.ds(n * TN, TN), :], flow.res[:, b, 0:D]).then_inc(flow.s_w[b], 16)

            with ExitStack() as inner:
                project(block, inner, "fp", 1, w_io, b_io, 2 * D, ACT.Copy, io_finish, io_store, prepare=prep_copy)
        end_stage()
        with ExitStack() as scope:
            with nc.Block() as block:
                items(block, scope, "is", 0, rec_src, cnt_s, it_s, False)
            end_stage()
        aggregate("ag3", fin_tab, it_d, D, acc[:, 0:NT * D], weight=it_d["weight"])
        aggregate("ag4", fout_tab, it_s, D, a_out[:], weight=it_s["weight"])

        with ExitStack() as scope:
            outb = sb("outb", [TN, 2, D], F32, scope)
            s_go = sem("gru_out")

            def prep_gru(dve, c, flow):
                v = nc.vector

                def ahead(n, b, r):
                    dve.wait_ge(flow.s_tr, n + 1)
                    for i, s in enumerate((acc[:, 0:NT * D], a_out[:], hb_flat)):
                        last = v.tensor_copy(flow.hbuf[:, b, i * D:(i + 1) * D], s[:, bass.ds(n * D, D)])
                    last.then_inc(flow.s_h, 1)

                def behind(n, b, r):
                    dve.wait_ge(flow.s_zc, n + 3)
                    dve.wait_ge(flow.s_w[b], r * 16 + 16)
                    o, gate, new = outb[:, b, :], flow.res[:, b, 0:D], flow.res[:, b, D:2 * D]
                    c(v.tensor_tensor(o, hb_flat[:, bass.ds(n * D, D)], new, ALU.subtract))
                    c(v.tensor_tensor(o, o, gate, ALU.mult))
                    c(v.tensor_tensor(o, o, new, ALU.add))
                    v.tensor_tensor(o, o, x_flat[:, bass.ds(n * D, D)], ALU.add).then_inc(s_go, 1)

                skewed(dve, NT, ahead, behind, c, 3)

            def gates(act, n, product, res):
                nc.scalar.activation(res[:, 0:D], product[:, 0:D], ACT.Sigmoid)
                return nc.scalar.activation(res[:, D:2 * D], product[:, D:2 * D], ACT.Tanh)

            def out_store(sp, n, b, flow):
                sp.wait_ge(s_go, n + 1)
                sp.dma_start(out[bass.ds(n * TN, TN), :], outb[:, b, :]).then_inc(flow.s_w[b], 16)

            with nc.Block() as block:
                project(block, scope, "gr", 3, w_g, b_g, 2 * D, ACT.Copy, gates, out_store, prepare=prep_gru)
            end_stage()


_INS = ["x", "src", "dst", "edge_weight", "edge_weight_n2", "L0_gnn_W1", "L0_gnn_a1", "L0_gnn_W2", "L0_gnn_a2",
        "L1_gnn_gamma", "L1_gnn_beta", "L1_gnn_W_in", "L1_gnn_b_in", "L1_gnn_W_out", "L1_gnn_b_out",
        "L1_gnn_W_x2i", "L1_gnn_b_x2i", "L1_gnn_W_h2h"]


def kernel(**inputs):
    import numpy as np
    import concourse.bacc as bacc
    from concourse.bass_utils import run_bass_kernel_spmd

    nc = bacc.Bacc("TRN2", target_bir_lowering=False, num_devices=1)
    arrays, args = {}, []
    for name in _INS:
        a = np.ascontiguousarray(inputs[name])
        arrays[f"in_{name}"] = a
        args.append(nc.dram_tensor(f"in_{name}", a.shape, mybir.dt.from_np(a.dtype), kind="ExternalInput").ap())
    out = nc.dram_tensor("out", (N, D), F32, kind="ExternalOutput").ap()
    build(nc, *args, out)
    r = run_bass_kernel_spmd(nc, [arrays], core_ids=[0])
    return r.results[0]["out"]
```

```python
import concourse.bass as bass
from concourse import mybir
from contextlib import ExitStack, contextmanager

F32, I32, BF16, U32 = mybir.dt.float32, mybir.dt.int32, mybir.dt.bfloat16, mybir.dt.uint32
ALU, ACT, AX = mybir.AluOpType, mybir.ActivationFunctionType, mybir.AxisListType

N, D, E = 3125, 256, 50000
HEADS, HID = 4, 64
TN = 125
NT = N // TN
CH = 128
SH = 14
EC = 392
EP = EC * CH
IQ, IP = 4, 104
NI = IQ * IP
G = 8
NG = NI // G
TURN = 16
RING = 8
LEAD = 4
PAD_KEY = 4000.0
BIG = 1e30
ROUND = 12582912.0
EPS = 1e-5
assert NI >= EC + NT - 1 and EC % (2 * SH) == 0 and EP >= E


class Chain:

    def __init__(self, eng, sem):
        self.eng, self.sem, self.done, self.here, self.turn, self.per = eng, sem, 0, 0, None, 0

    def step(self, ins):
        ins.then_inc(self.sem, 1)
        self.here += 1

    def wait(self, back=0):
        n = self.done + self.here - back
        self.eng.wait_ge(self.sem, n if self.turn is None else self.turn * self.per + n)

    def __call__(self, ins):
        self.step(ins)
        self.wait()

    @contextmanager
    def loop(self, turns, per):
        self.done, self.here = self.done + self.here, 0
        with self.eng.Fori(0, turns) as i:
            self.turn, self.per = i, per
            yield i
            assert self.here == per, (self.here, per)
        self.turn, self.done, self.here = None, self.done + turns * per, 0


class Flow:

    def __init__(self, hbuf, res, s_turned, s_input, s_taken, s_stored):
        self.hbuf, self.res, self.s_turned, self.s_input, self.s_taken, self.s_stored = hbuf, res, s_turned, s_input, s_taken, s_stored


@contextmanager
def turns_of(eng, turns, chain=None, per=0):
    if chain is None:
        with eng.Fori(0, turns) as i:
            yield i
    else:
        with chain.loop(turns, per) as i:
            yield i


def alternate(eng, count, step, chain=None, per=0):
    with turns_of(eng, count // 2, chain, 2 * per) as i:
        step(i * 2, 0, i)
        step(i * 2 + 1, 1, i)
    if count % 2:
        step(count - 1, 0, count // 2)


def staggered(eng, count, steps, chain=None, per=0, ways=2):
    def plain(m):
        for step, lead in steps:
            n = m + lead
            if 0 <= n < count:
                step(n, n % ways, n // ways)

    most = max(lead for _, lead in steps)
    for m in range(-most, 0):
        plain(m)
    turns = (count - most) // ways - 1
    with turns_of(eng, turns, chain, ways * per) as i:
        for k in range(ways):
            for step, lead in steps:
                step(i * ways + (k + lead), (k + lead) % ways, i + (k + lead) // ways)
    for m in range(ways * turns, count):
        plain(m)


def skewed(eng, count, ahead, behind, chain=None, per=0):
    staggered(eng, count, ((ahead, 1), (behind, 0)), chain, per)


def build(nc, x, src, dst, edge_weight, edge_weight_n2, W1, a1, W2, a2, gamma, beta,
          W_in, b_in, W_out, b_out, W_x2i, b_x2i, W_h2h, out):
    ctx = ExitStack()
    with ctx:
        held = []

        def sem(name):
            held.append(nc.alloc_semaphore(name=name))
            return held[-1]

        def end_stage():
            with nc.Block() as block:
                @block.gpsimd
                def _(pool):
                    nc.clear_and_free_semaphores(held)
            held.clear()

        def fence(block, name, engines=("sync", "scalar", "tensor", "vector")):
            s_here = sem(name)
            for which in engines:
                def program(eng):
                    eng.drain().then_inc(s_here, 1)
                    eng.wait_ge(s_here, len(engines))
                {"sync": block.sync, "scalar": block.scalar, "tensor": block.tensor,
                 "vector": block.vector, "gpsimd": block.gpsimd}[which](program)

        def sb(name, shape, dt=F32, scope=ctx):
            return scope.enter_context(nc.sbuf_tensor(name, shape, dt))

        def dram(name, shape, dt=F32):
            return nc.dram_tensor(name, shape, dt, kind="Internal").ap()

        rec_half = dram("rec_half", (EP, 4))
        rec_src = dram("rec_src", (EP, 4))
        rec_dst = dram("rec_dst", (EP, 4))
        row_local = dram("row_local", (NI * CH,), BF16)
        row_other = dram("row_other", (NI * CH,), BF16)
        tile_tab = [dram(f"tile_tab{i}", (NI,), I32) for i in range(2)]
        edge_tab = dram("edge_tab", (2, IP))
        z_tab, z2_tab = dram("z_tab", (N, D)), dram("z2_tab", (N, D))
        fin_tab, fout_tab = dram("fin_tab", (N, D)), dram("fout_tab", (N, D))

        bank = [ctx.enter_context(nc.psum_tensor(f"bank{i}", [128, 512], F32)) for i in range(8)]

        part = sb("part", [128, 1])
        col = sb("col", [128, 128])
        item_no = sb("item_no", [128, IQ])
        ident = sb("ident", [128, 128])
        below = sb("below", [128, 128])
        ones = sb("ones", [128, 128])
        eps = sb("eps", [128, 1])
        KD = D // 128
        x_sb = sb("x_sb", [TN, NT, D])
        x_flat = x_sb[:].rearrange("p t d -> p (t d)")
        acc = sb("acc", [TN, NT * (D + HEADS)])
        w_aug = [sb(f"w_aug{i}", [128, KD, D + 2 * HEADS]) for i in range(2)]
        cnt_s = sb("cnt_s", [128, NT])
        cnt_d = sb("cnt_d", [128, NT])
        place_i = sb("place_i", [128, EC], I32)
        rec_s = sb("rec_s", [128, EC, 4])
        stage_p = sb("stage_p", [128, 2, SH], I32)
        stage_r = sb("stage_r", [128, 2, SH, 4])
        disorder = sb("disorder", [1, 1], I32)

        def item_arrays(name):
            return {"local": sb(name + "_local", [128, NI]), "index": sb(name + "_index", [128, NI], I32),
                    "weight": sb(name + "_weight", [128, NI]), "tiles": sb(name + "_tiles", [1, NI], I32)}

        it_s, it_d = item_arrays("src"), item_arrays("dst")
        high = sb("high", [128, NI])
        same_f = sb("same_f", [IP, IQ * CH])
        same_b = sb("same_b", [IP, IQ * CH])
        link = sb("link", [IP, 4])
        s_tab = sb("s_tab", [TN, HEADS * NT])
        d_tab = sb("d_tab", [TN, NT * HEADS])
        s_part = sb("s_part", [TN, 3, HEADS * NT], BF16)
        d_part = sb("d_part", [TN, NT * 3 * HEADS], BF16)
        stats = sb("stats", [TN, NT * 6])
        mean = sb("mean", [TN, NT])
        rstd = sb("rstd", [TN, NT])
        spread = sb("spread", [TN, NT])
        shift = sb("shift", [TN, NT])
        w_all = sb("w_all", [128, NI * HEADS])

        def scatter(name, pool, rec, to, first, last, ready=None):
            s_stage, s_turn = sem(name + "_stage"), sem(name + "_turn")
            s_free = [sem(name + f"_free{h}") for h in range(2)]
            flat = rec[:].rearrange("p j f -> p (j f)")

            def half(g, r, h, first_use):
                if not first_use:
                    pool.wait_ge(s_free[h], r * (16 * SH))
                at = (g * 2 + h) * SH
                nc.gpsimd.tensor_copy(stage_p[:, h, :], place_i[:, bass.ds(at, SH)]).then_inc(s_stage, 1)
                nc.gpsimd.tensor_copy(stage_r[:, h, :, :].rearrange("p a f -> p (a f)"),
                                      flat[:, bass.ds(at * 4, SH * 4)]).then_inc(s_stage, 1)
                pool.wait_ge(s_stage, r * 4 + (2 * h + 2))
                pool.sem_inc(s_turn, 1)
                for k in range(SH):
                    nc.gpsimd.indirect_dma_start(to, bass.IndirectOffsetOnAxis(ap=stage_p[:, h, k:k + 1], axis=0),
                                                 stage_r[:, h, k, :], None).then_inc(s_free[h], 16)

            for h in range(2):
                half(first, 0, h, True)
            with pool.Fori(1, last - first) as r:
                for h in range(2):
                    half(r + first, r, h, False)
            for h in range(2):
                pool.wait_ge(s_free[h], (last - first) * 16 * SH)

        def sort_digit(c, rec, digit, low):
            v = nc.vector
            c(v.tensor_scalar(digit[:], rec[:, :, 0], 1.0 / TN, -0.496, ALU.mult, ALU.add))
            c(v.tensor_scalar(digit[:], digit[:], ROUND, ROUND, ALU.add, ALU.subtract))
            c(v.tensor_scalar(digit[:], digit[:], float(NT - 1), None, ALU.min))
            if low:
                c(v.scalar_tensor_tensor(digit[:], digit[:], -float(TN), rec[:, :, 0], ALU.mult, ALU.add))
                c(v.tensor_scalar(digit[:], digit[:], float(TN - 1), None, ALU.min))

        def count_all(c, digit, equal, tot, buckets):
            with c.loop(buckets // 5, 5) as i:
                for k in range(5):
                    c.wait(1)
                    b = i * 5 + k
                    c.step(nc.vector.tensor_scalar(equal[:, k % 2 if k < 4 else 2, :], digit[:], col[:, bass.ds(b, 1)], 0.0,
                                                   ALU.is_equal, ALU.add, accum_out=tot[:, bass.ds(b, 1)]))
            c.wait()

        def rank(name, tmp):
            digit, equal, run, place, tot, cnt, incl, off = tmp
            s_tot, s_sum, s_turn = sem(name + "_tot"), sem(name + "_sum"), sem(name + "_turn")

            def vector(dve, c, rec, low, buckets):
                v = nc.vector
                sort_digit(c, rec, digit, low)
                count_all(c, digit, equal, tot, buckets)
                c.wait()
                dve.drain().then_inc(s_tot, 1)
                dve.wait_ge(s_sum, 1)
                c(v.tensor_copy(cnt[:, 0:buckets], bank[0][:, 128:128 + buckets]))
                c(v.tensor_tensor_scan(incl[:, 0:buckets], cnt[:, 0:buckets], cnt[:, 0:buckets], 0.0, ALU.add, ALU.bypass))
                c(v.tensor_tensor(off[:, 0:buckets], incl[:, 0:buckets], cnt[:, 0:buckets], ALU.subtract))
                c(v.scalar_tensor_tensor(off[:, 0:buckets], off[:, 0:buckets], -1.0, bank[0][:, 0:buckets], ALU.add, ALU.add))
                c(v.memset(place[:], 0.0))

                def mark(b, i):
                    c.step(v.tensor_scalar(equal[:, i, :], digit[:], col[:, bass.ds(b, 1)], None, ALU.is_equal))

                def count(b, i):
                    c.step(v.tensor_tensor_scan(run[:, i, :], equal[:, i, :], equal[:, i, :], off[:, bass.ds(b, 1)], ALU.add, ALU.bypass))

                def take(i):
                    c.step(v.copy_predicated(place[:], equal[:, i, :].bitcast(U32), run[:, i, :]))

                with c.loop(buckets // 2, 6) as i:
                    mark(i * 2, 0)
                    c.wait(1)
                    mark(i * 2 + 1, 1)
                    c.wait(1)
                    count(i * 2, 0)
                    c.wait(1)
                    count(i * 2 + 1, 1)
                    c.wait(1)
                    dve.sem_inc(s_turn, 1)
                    take(0)
                    c.wait(0)
                    dve.sem_inc(s_turn, 1)
                    take(1)
                c.wait()
                mark(buckets - 1, 0)
                c.wait()
                count(buckets - 1, 0)
                c.wait()
                take(0)
                c.wait()
                c(v.tensor_copy(place_i[:], place[:]))

            def tensor(pe, buckets):
                pe.wait_ge(s_tot, 1)
                nc.tensor.matmul(bank[0][:, 0:buckets], below[:], tot[:, 0:buckets], start=True, stop=True)
                nc.tensor.matmul(bank[0][:, 128:128 + buckets], ones[:], tot[:, 0:buckets], start=True, stop=True)
                pe.drain().then_inc(s_sum, 1)

            return vector, tensor

        with ExitStack() as scope:
            rec_d = sb("rec_d", [128, EC, 4], F32, scope)
            src_i = sb("src_i", [128, EC], I32, scope)
            dst_i = sb("dst_i", [128, EC], I32, scope)
            next_i = sb("next_i", [128, EC], I32, scope)
            wgt_s = sb("wgt_s", [128, EC], F32, scope)
            wgt_d = sb("wgt_d", [128, EC], F32, scope)
            digit = sb("digit", [128, EC], F32, scope)
            equal = sb("equal", [128, 3, EC], F32, scope)
            run = sb("run", [128, 2, EC], F32, scope)
            place = sb("place", [128, EC], F32, scope)
            tot, cnt, incl, off = (sb(k, [128, 128], F32, scope) for k in ("tot", "cnt", "incl", "off"))
            falls = sb("falls", [128, 1], F32, scope)
            falls1 = sb("falls1", [1, 1], F32, scope)
            w_nat = [sb(f"w_nat{i}", [128, KD, D], F32, scope) for i in range(2)]
            a_blk = [sb(f"a_blk{i}", [128, KD, 2 * HEADS], F32, scope) for i in range(2)]
            tmp = (digit, equal, run, place, tot, cnt, incl, off)
            s_iota, s_x, s_pad, s_in, s_c = (sem(k) for k in ("iota", "in_x", "pad", "in_edges", "order_c"))
            s_w, s_rd, s_recd, s_fl, s_fm, s_wt = (sem(k) for k in ("in_w", "rec_d_out", "rec_d_made", "falls_v", "falls_m", "w_trans"))
            rank_v, rank_t = rank("rank", tmp)

            with nc.Block() as block:
                @block.sync
                def _(sp):
                    full = E // EC
                    rest = E - full * EC
                    sp.wait_ge(s_pad, 1)
                    loads = 0
                    for t, a, shift in ((src_i, src, 0), (dst_i, dst, 0), (wgt_s, edge_weight_n2, 0), (wgt_d, edge_weight, 0),
                                        (next_i, dst, 1)):
                        sp.dma_start(t[0:full, :], a[shift:shift + full * EC].rearrange("(p j) -> p j", j=EC)).then_inc(s_in, 16)
                        sp.dma_start(t[full:full + 1, 0:rest - shift],
                                     a[shift + full * EC:E].rearrange("(o j) -> o j", o=1)).then_inc(s_in, 16)
                    sp.dma_start(x_sb[:], x.rearrange("(t p) d -> p t d", p=TN)).then_inc(s_x, 16)
                    with nc.allow_non_contiguous_dma(reason="a few hundred words"):
                        for i, (W, a, heads) in enumerate(((W1.rearrange("h o i -> (h o) i"), a1, HEADS),
                                                           (W2, a2.rearrange("(o n) -> o n", o=1), 1))):
                            sp.dma_start(w_nat[i][:], W.rearrange("(k p) i -> p k i", p=128)).then_inc(s_w, 16)
                            loads += 1
                            hid = D // heads
                            for half in range(2):
                                for h in range(heads):
                                    for k in range(KD):
                                        lo, hi = max(h * hid, k * 128), min((h + 1) * hid, (k + 1) * 128)
                                        if lo < hi:
                                            sp.dma_start(a_blk[i][lo - k * 128:hi - k * 128, k, half * heads + h:half * heads + h + 1],
                                                         a[h:h + 1, half * hid + lo - h * hid:half * hid + hi - h * hid].rearrange("o n -> n o")).then_inc(s_w, 16)
                                            loads += 1
                    sp.wait_ge(s_recd, 1)
                    sp.dma_start(rec_dst.rearrange("(p j) f -> p j f", p=128), rec_d[:]).then_inc(s_rd, 16)
                    sp.wait_ge(s_rd, 16)
                    sp.wait_ge(s_x, 16)
                    sp.wait_ge(s_w, 16 * loads)
                    sp.sem_inc(s_wt, 1)

                @block.gpsimd
                def _(pool):
                    for t, pattern, per in ((part, [[0, 1]], 1), (col, [[1, 128]], 0), (item_no, [[1, IQ]], IQ)):
                        nc.gpsimd.iota(t[:], pattern, base=0, channel_multiplier=per,
                                       allow_small_or_imprecise_dtypes=True).then_inc(s_iota, 1)

                @block.vector
                def _(dve):
                    c = Chain(dve, s_c)
                    v = nc.vector
                    for t in a_blk:
                        v.memset(t[:], 0.0)
                    v.memset(src_i[:], int(PAD_KEY))
                    v.memset(dst_i[:], int(PAD_KEY))
                    v.memset(next_i[:], int(PAD_KEY))
                    v.memset(wgt_s[:], 0.0)
                    v.memset(wgt_d[:], 0.0)
                    v.drain().then_inc(s_pad, 1)
                    v.memset(rec_s[:], 0.0)
                    v.memset(rec_d[:], 0.0)
                    v.memset(ones[:], 1.0)
                    v.memset(eps[:], EPS)
                    dve.wait_ge(s_iota, 3)
                    c(v.tensor_scalar(ident[:], col[:], part[:], None, ALU.is_equal))
                    c(v.tensor_scalar(below[:], col[:], part[:], None, ALU.is_gt))
                    dve.wait_ge(s_in, 160)
                    for rec, key, other, weight in ((rec_s, src_i, dst_i, wgt_s), (rec_d, dst_i, src_i, wgt_d)):
                        c.step(v.tensor_copy(rec[:, :, 0], key[:]))
                        c.step(v.tensor_copy(rec[:, :, 1], other[:]))
                        c.step(v.tensor_copy(rec[:, :, 2], weight[:]))
                    c.wait()
                    v.drain().then_inc(s_recd, 1)
                    c(v.tensor_tensor(equal[:, 0, :], dst_i[:], next_i[:], ALU.is_gt))
                    c(v.tensor_reduce(falls[:], equal[:, 0, :], AX.X, ALU.add))
                    v.drain().then_inc(s_fl, 1)
                    sort_digit(c, rec_d, digit, False)
                    count_all(c, digit, equal, tot, NT)
                    c.wait()
                    v.drain().then_inc(s_fl, 1)
                    dve.wait_ge(s_fm, 2)
                    c(v.tensor_copy(cnt_d[:], bank[1][:, 128:128 + NT]))
                    c(v.tensor_scalar(falls1[:], bank[1][0:1, 0:1], 1.0, None, ALU.min))
                    c(v.tensor_copy(disorder[:], falls1[:]))
                    rank_v(dve, c, rec_s, False, NT)
                    c(v.tensor_copy(cnt_s[:], cnt[:, 0:NT]))

                @block.tensor
                def _(pe):
                    pe.wait_ge(s_fl, 1)
                    nc.tensor.matmul(bank[1][:, 0:1], ones[:], falls[:], start=True, stop=True).then_inc(s_fm, 1)
                    pe.wait_ge(s_fl, 2)
                    nc.tensor.matmul(bank[1][:, 128:128 + NT], ones[:], tot[:, 0:NT], start=True, stop=True).then_inc(s_fm, 1)
                    rank_t(pe, NT)
                    pe.wait_ge(s_wt, 1)
                    for i, heads in enumerate((HEADS, 1)):
                        for k in range(KD):
                            for m in range(KD):
                                nc.tensor.transpose(bank[2 + 3 * i + k][:, m * 128:(m + 1) * 128], w_nat[i][:, m, k * 128:(k + 1) * 128], ident[:])
                        for k in range(KD):
                            for m in range(KD):
                                nc.tensor.matmul(bank[4 + 3 * i][:, k * 2 * heads:(k + 1) * 2 * heads], w_nat[i][:, m, k * 128:(k + 1) * 128],
                                                 a_blk[i][:, m, 0:2 * heads], start=(m == 0), stop=(m == KD - 1))
                    pe.drain().then_inc(s_wt, 1)

                @block.scalar
                def _(act):
                    act.wait_ge(s_wt, 2)
                    for i, heads in enumerate((HEADS, 1)):
                        for k in range(KD):
                            nc.scalar.activation(w_aug[i][:, k, 0:D], bank[2 + 3 * i + k][:, 0:D], ACT.Copy)
                            nc.scalar.activation(w_aug[i][:, k, D:D + 2 * heads], bank[4 + 3 * i][:, k * 2 * heads:(k + 1) * 2 * heads], ACT.Copy)
            end_stage()

            rec_u = rec_d
            place_keep = sb("place_keep", [128, EC], I32, scope)
            s_c, s_pl, s_sc, s_re = (sem(k) for k in ("sort_c", "sort_places", "sort_scattered", "sort_reload"))
            passes = [rank(f"rank{i}", tmp) for i in range(2)]
            with nc.Block() as block:
                @block.vector
                def _(dve):
                    flag = dve.value_load(disorder[0:1, 0:1], min_val=0, max_val=1)
                    with dve.If(flag != 0):
                        c = Chain(dve, s_c)
                        c(nc.vector.tensor_copy(place_keep[:], place_i[:]))
                        for i in range(2):
                            if i:
                                dve.wait_ge(s_re, 16)
                            passes[i][0](dve, c, rec_u, i == 0, TN if i == 0 else NT)
                            dve.drain().then_inc(s_pl, 1)
                            dve.wait_ge(s_sc, i + 1)
                        c(nc.vector.tensor_copy(place_i[:], place_keep[:]))

                @block.tensor
                def _(pe):
                    flag = pe.value_load(disorder[0:1, 0:1], min_val=0, max_val=1)
                    with pe.If(flag != 0):
                        for i in range(2):
                            passes[i][1](pe, TN if i == 0 else NT)

                @block.gpsimd
                def _(pool):
                    flag = pool.value_load(disorder[0:1, 0:1], min_val=0, max_val=1)
                    with pool.If(flag != 0):
                        for i in range(2):
                            pool.wait_ge(s_pl, i + 1)
                            scatter(f"sort{i}", pool, rec_u, rec_dst if i else rec_half, 0, EC // (2 * SH))
                            pool.sem_inc(s_sc, 1)

                @block.sync
                def _(sp):
                    flag = sp.value_load(disorder[0:1, 0:1], min_val=0, max_val=1)
                    with sp.If(flag != 0):
                        sp.wait_ge(s_sc, 1)
                        sp.dma_start(rec_u[:], rec_half.rearrange("(p j) f -> p j f", p=128)).then_inc(s_re, 16)
                        sp.wait_ge(s_re, 16)
            end_stage()

        def items(block, scope, name, which, recs, counts, it, attention):
            t25 = [sb(f"{name}_b{i}", [128, NT], F32, scope) for i in range(8)]
            start, end, sc, ec, n, ib, dl, tmp = t25
            ge = sb(name + "_ge", [IP, IQ, NT], F32, scope)
            gd = sb(name + "_gd", [IP, IQ, NT], F32, scope)
            tcol = sb(name + "_tcol", [IP, IQ], F32, scope)
            jcol = sb(name + "_jcol", [IP, IQ], F32, scope)
            tcol_i = sb(name + "_tcol_i", [IP, IQ], I32, scope)
            jcol_i = sb(name + "_jcol_i", [IP, IQ], I32, scope)
            rows = sb(name + "_rows", [IP, IQ, CH * 4], F32, scope)
            loc = sb(name + "_loc", [IP, IQ, CH], F32, scope)
            oth = sb(name + "_oth", [IP, IQ, CH], F32, scope)
            wg = sb(name + "_wg", [IP, IQ, CH], F32, scope)
            hi = sb(name + "_hi", [IP, IQ, CH], F32, scope)
            lo = sb(name + "_lo", [IP, IQ, CH], F32, scope)
            loc_b = sb(name + "_loc_b", [IP, IQ, CH], BF16, scope)
            lo_b = sb(name + "_lo_b", [IP, IQ, CH], BF16, scope)
            prev = sb(name + "_prev", [IP, 2], F32, scope)
            whole = sb(name + "_whole", [IP, 2], F32, scope)
            s_c, s_j, s_rows, s_t, s_tl, s_rw, s_tr, s_ed, s_b = (sem(name + k) for k in (
                "_c", "_j", "_rows", "_t", "_tl", "_rw", "_tr", "_ed", "_b"))
            f = rows[:].rearrange("p q (s f) -> p q s f", f=4)
            key = f[:, :, :, 0]

            @block.vector
            def _(dve):
                c = Chain(dve, s_c)
                v = nc.vector

                def floor128(o, i):
                    c(v.tensor_scalar(o[:], i[:], 1.0 / CH, -0.498, ALU.mult, ALU.add))
                    c(v.tensor_scalar(o[:], o[:], ROUND, ROUND, ALU.add, ALU.subtract))

                c(v.tensor_tensor_scan(end[:], counts[:], counts[:], 0.0, ALU.add, ALU.bypass))
                c(v.tensor_tensor(start[:], end[:], counts[:], ALU.subtract))
                c(v.tensor_scalar(end[:], end[:], -1.0, None, ALU.add))
                floor128(sc, start)
                floor128(ec, end)
                c(v.tensor_tensor(n[:], ec[:], sc[:], ALU.subtract))
                c(v.tensor_scalar(tmp[:], counts[:], 0.0, None, ALU.is_gt))
                c(v.scalar_tensor_tensor(n[:], n[:], 1.0, tmp[:], ALU.add, ALU.mult))
                c(v.tensor_tensor_scan(ib[:], n[:], n[:], 0.0, ALU.add, ALU.bypass))
                c(v.tensor_tensor(ib[:], ib[:], n[:], ALU.subtract))
                c(v.tensor_tensor(tmp[:], sc[:], ib[:], ALU.subtract))
                c(v.tensor_copy(dl[:], tmp[:]))
                c(v.tensor_tensor(dl[:, 1:NT], tmp[:, 1:NT], tmp[:, 0:NT - 1], ALU.subtract))
                c(v.tensor_tensor(ge[:], item_no[0:IP, :].unsqueeze(2).to_broadcast([IP, IQ, NT]),
                                  ib[0:IP, :].unsqueeze(1).to_broadcast([IP, IQ, NT]), ALU.is_ge))
                c(v.tensor_reduce(tcol[:], ge[:], AX.X, ALU.add))
                c(v.tensor_scalar(tcol[:], tcol[:], -1.0, None, ALU.add))
                c(v.tensor_tensor(gd[:], ge[:], dl[0:IP, :].unsqueeze(1).to_broadcast([IP, IQ, NT]), ALU.mult))
                c(v.tensor_reduce(jcol[:], gd[:], AX.X, ALU.add))
                c(v.tensor_tensor(jcol[:], jcol[:], item_no[0:IP, :], ALU.add))
                c(v.tensor_scalar(jcol[:], jcol[:], float(EC - 1), None, ALU.min))
                c(v.tensor_copy(jcol_i[:], jcol[:]))
                c(v.tensor_copy(tcol_i[:], tcol[:]))
                dve.drain().then_inc(s_j, 1)
                dve.wait_ge(s_rows, 16 * IQ)
                c(v.scalar_tensor_tensor(loc[:], tcol[:].unsqueeze(2).to_broadcast([IP, IQ, CH]), -float(TN), key, ALU.mult, ALU.add))
                c(v.tensor_scalar(oth[:], f[:, :, :, 1], float(N - 1), None, ALU.min))
                c(v.tensor_scalar(hi[:], oth[:], 1.0 / TN, -0.496, ALU.mult, ALU.add))
                c(v.tensor_scalar(hi[:], hi[:], ROUND, ROUND, ALU.add, ALU.subtract))
                c(v.scalar_tensor_tensor(lo[:], hi[:], -float(TN), oth[:], ALU.mult, ALU.add))
                c(v.tensor_copy(wg[:], f[:, :, :, 2]))
                c(v.tensor_copy(loc_b[:], loc[:]))
                c(v.tensor_copy(lo_b[:], lo[:]))
                dve.drain().then_inc(s_rw, 1)
                if attention:
                    k2 = rows[:].rearrange("p q (s f) -> p (q s) f", f=4)[:, :, 0]
                    L = IQ * CH
                    c(v.memset(same_f[:], 1.0))
                    c(v.memset(same_b[:], 1.0))
                    c(v.tensor_tensor(same_f[:, 1:L], k2[:, 1:L], k2[:, 0:L - 1], ALU.not_equal))
                    c(v.tensor_tensor(same_b[:, 0:L - 1], k2[:, 1:L], k2[:, 0:L - 1], ALU.not_equal))
                    c(v.tensor_scalar(same_f[:], same_f[:], -BIG, None, ALU.mult))
                    c(v.tensor_scalar(same_b[:], same_b[:], -BIG, None, ALU.mult))
                    c(v.memset(prev[:], -5.0))
                    dve.drain().then_inc(s_b, 1)
                    dve.wait_ge(s_ed, 32 + 32)
                    c(v.tensor_tensor(link[:, 0:1], prev[:, 0:1], k2[:, 0:1], ALU.not_equal))
                    c(v.tensor_tensor(link[:, 1:2], prev[:, 1:2], k2[:, L - 1:L], ALU.not_equal))
                    c(v.tensor_tensor(whole[:, 0:1], k2[:, 0:1], k2[:, L - 1:L], ALU.not_equal))
                    c(v.tensor_scalar(link[:, 2:4], link[:, 0:2], whole[:, 0:1], None, ALU.max))
                    c(v.tensor_scalar(link[:], link[:], -BIG, None, ALU.mult))
                dve.wait_ge(s_tr, 1)
                for b, to in ((0, it["local"]), (1, it["index"]), (2, it["weight"]), (3, high)):
                    if b == 3 and not attention:
                        continue
                    v.tensor_copy(to[:].rearrange("e (p q) -> e q p", q=IQ),
                                  bank[b][:, 0:NI].rearrange("e (q p) -> e q p", q=IQ))

            @block.gpsimd
            def _(pool):
                pool.wait_ge(s_j, 1)
                for q in range(IQ):
                    nc.gpsimd.indirect_dma_start(rows[:, q, :], None, recs.rearrange("(c s) f -> c (s f)", s=CH),
                                                 bass.IndirectOffsetOnAxis(ap=jcol_i[:, q:q + 1], axis=0)).then_inc(s_rows, 16)
                pool.dma_start(tile_tab[which].rearrange("(p q) -> p q", q=IQ), tcol_i[:]).then_inc(s_t, 16)
                pool.wait_ge(s_t, 16)
                pool.dma_start(it["tiles"][:], tile_tab[which].rearrange("(o n) -> o n", o=1)).then_inc(s_tl, 16)
                if attention:
                    pool.wait_ge(s_rw, 1)
                    pool.dma_start(row_local.rearrange("(p n) -> p n", p=IP), loc_b[:].rearrange("p q s -> p (q s)")).then_inc(s_tl, 16)
                    pool.dma_start(row_other.rearrange("(p n) -> p n", p=IP), lo_b[:].rearrange("p q s -> p (q s)")).then_inc(s_tl, 16)
                    pool.wait_ge(s_b, 1)
                    for i, q, s in ((0, IQ - 1, CH - 1), (1, 0, 0)):
                        pool.dma_start(edge_tab[i:i + 1, :].rearrange("o p -> p o"), f[:, q, s, 0:1]).then_inc(s_ed, 16)
                    pool.wait_ge(s_ed, 32)
                    pool.dma_start(prev[1:IP, 0:1], edge_tab[0:1, 0:IP - 1].rearrange("o p -> p o")).then_inc(s_ed, 16)
                    pool.dma_start(prev[0:IP - 1, 1:2], edge_tab[1:2, 1:IP].rearrange("o p -> p o")).then_inc(s_ed, 16)
                    pool.wait_ge(s_ed, 64)

            @block.sync
            def _(sp):
                sp.wait_ge(s_tl, 48 if attention else 16)

            @block.tensor
            def _(pe):
                pe.wait_ge(s_rw, 1)
                for b, t in enumerate((loc, oth, wg, hi)):
                    for q in range(IQ):
                        nc.tensor.transpose(bank[b][:, q * IP:(q + 1) * IP], t[:, q, :], ident[0:IP, 0:IP])
                pe.drain().then_inc(s_tr, 1)


        def row_stats(block, name, done=None):
            s_c, s_v, s_q = sem(name + "_c"), sem(name + "_v"), sem(name + "_q")
            st = stats[:].rearrange("p (t s) -> p t s", s=6)

            @block.vector
            def _(dve):
                c = Chain(dve, s_c)
                v = nc.vector
                with dve.Fori(0, NT // 5) as i:
                    for k in range(5):
                        t = i * 5 + k
                        v.bn_stats(stats[:, bass.ds(t * 6, 6)], x_flat[:, bass.ds(t * D, D)])
                c(dve.drain())
                c(v.tensor_tensor(mean[:], st[:, :, 1], st[:, :, 4], ALU.add))
                c(v.tensor_scalar(mean[:], mean[:], 0.5, None, ALU.mult))
                c(v.tensor_tensor(spread[:], st[:, :, 1], st[:, :, 4], ALU.subtract))
                c(v.scalar_tensor_tensor(spread[:], spread[:], 0.25, spread[:], ALU.mult, ALU.mult))
                c(v.tensor_tensor(rstd[:], st[:, :, 2], st[:, :, 5], ALU.add))
                c(v.scalar_tensor_tensor(rstd[:], rstd[:], 1.0 / D, spread[:], ALU.mult, ALU.add))
                dve.drain().then_inc(s_v, 1)
                dve.wait_ge(s_q, 1)
                c(v.reciprocal(rstd[:], rstd[:]))
                if done is not None:
                    c(v.scalar_tensor_tensor(shift[:], mean[:], -1.0, rstd[:], ALU.mult, ALU.mult))
                    dve.drain().then_inc(done, 1)

            @block.scalar
            def _(act):
                act.wait_ge(s_v, 1)
                nc.scalar.activation(rstd[:], rstd[:], ACT.Sqrt, bias=eps[0:TN, :]).then_inc(s_q, 1)

        def project(block, scope, name, srcs, weights, bias, width, func, finish, store, prepare=None, act_ahead=None):
            K = KD * srcs
            s_input, s_turned, s_cols, s_product, s_taken, s_c = (sem(name + k) for k in ("_h", "_tr", "_ht", "_z", "_zc", "_c"))
            s_stored = [sem(name + f"_w{b}") for b in range(2)]
            hbuf = sb(name + "_hbuf", [TN, 2, K * 128], F32, scope)
            h_t = sb(name + "_h_t", [128, 2, K, TN], F32, scope)
            res = sb(name + "_res", [TN, 2, width], F32, scope)
            nb = (K + 3) // 4
            flow = Flow(hbuf=hbuf, res=res, s_turned=s_turned, s_input=s_input, s_taken=s_taken, s_stored=s_stored)

            def product(b):
                return bank[4 + b][0:TN, 0:width]

            if prepare is not None:
                @block.vector
                def _(dve):
                    dve.sem_inc(s_input, 2)
                    prepare(dve, Chain(dve, s_c), flow)

            @block.tensor
            def _(pe):
                pe.sem_inc(s_turned, 2)
                pe.sem_inc(s_product, 2)

                def ahead(n, b, r):
                    pe.wait_ge(s_input, n + 3)
                    pe.wait_ge(s_cols, n + 1)
                    for k in range(K):
                        last = nc.tensor.transpose(bank[2 * b + k // 4][:, (k % 4) * TN:(k % 4 + 1) * TN],
                                                   hbuf[:, b, k * 128:(k + 1) * 128], ident[0:TN, 0:TN])
                    last.then_inc(s_turned, 1)

                def behind(n, b, r):
                    pe.wait_ge(s_cols, n + 3)
                    pe.wait_ge(s_taken, n + 1)
                    for k in range(K):
                        last = nc.tensor.matmul(product(b), h_t[:, b, k, :], weights[:, k, 0:width],
                                                start=(k == 0), stop=(k == K - 1 and bias is None))
                    if bias is not None:
                        last = nc.tensor.matmul(product(b), ones16[:], bias, start=False, stop=True)
                    last.then_inc(s_product, 1)

                skewed(pe, NT, ahead, behind)

            @block.scalar
            def _(act):
                act.sem_inc(s_cols, 2)
                act.sem_inc(s_taken, 2)
                if prepare is None:
                    act.sem_inc(s_input, 2)

                if act_ahead is not None:
                    act_ahead(act, 0, 0, flow)

                def ahead(n, b, r):
                    if act_ahead is not None:
                        act_ahead(act, n + 1, 1 - b, flow)
                    act.wait_ge(s_turned, n + 3)
                    act.wait_ge(s_product, n + 1)
                    for k in range(nb):
                        m = min(4, K - 4 * k)
                        last = nc.scalar.activation(h_t[:, b, 4 * k:4 * k + m, :],
                                                    bank[2 * b + k][:, 0:m * TN].rearrange("p (k n) -> p k n", k=m), func)
                    last.then_inc(s_cols, 1)

                def behind(n, b, r):
                    act.wait_ge(s_product, n + 3)
                    act.wait_ge(s_stored[b], r * 16 + 16)
                    finish(act, n, product(b), res[:, b, :]).then_inc(s_taken, 1)

                skewed(act, NT, ahead, behind)

            @block.sync
            def _(sp):
                for b in range(2):
                    sp.sem_inc(s_stored[b], 16)

                alternate(sp, NT, lambda n, b, r: store(sp, n, b, flow))
                for b in range(2):
                    sp.wait_ge(s_stored[b], 16 + 16 * ((NT + 1 - b) // 2))

        def attention_finish(heads):
            def finish(act, n, product, res):
                nc.scalar.activation(res[:, 0:D], product[:, 0:D], ACT.Copy)
                nc.scalar.activation(s_tab[:, 0:heads * NT].rearrange("p (h t) -> p h t", h=heads)[:, :, bass.ds(n, 1)],
                                     product[:, D:D + heads].unsqueeze(2), ACT.Copy)
                return nc.scalar.activation(d_tab[:, bass.ds(n * heads, heads)], product[:, D + heads:D + 2 * heads], ACT.Copy)
            return finish

        def table_store(table):
            def store(sp, n, b, flow):
                sp.wait_ge(flow.s_taken, n + 3)
                sp.dma_start(table[bass.ds(n * TN, TN), :], flow.res[:, b, 0:D]).then_inc(flow.s_stored[b], 16)
            return store

        def split_tables(block, name, heads):
            s_c = sem(name)

            @block.vector
            def _(dve):
                c = Chain(dve, s_c)
                d4 = d_part[:, 0:NT * 3 * heads].rearrange("p (t m h) -> p m t h", m=3, h=heads)
                for k in range(3):
                    for t, o in ((s_tab[:, 0:heads * NT], s_part[:, k, 0:heads * NT]),
                                 (d_tab[:, 0:heads * NT].rearrange("p (t h) -> p t h", h=heads), d4[:, k])):
                        c(nc.vector.tensor_copy(o, t))
                        if k < 2:
                            c(nc.vector.tensor_tensor(t, t, o, ALU.subtract))

        def edge_softmax(block, scope, name, H):
            s_selected, s_looked, s_summed, s_c = (sem(name + k) for k in ("_sel", "_look", "_sum", "_c"))
            WAYS = 4
            s_rows = [sem(name + f"_row{b}") for b in range(WAYS)]
            rows_l = sb(name + "_rows_l", [128, WAYS, G * CH], BF16, scope)
            rows_o = sb(name + "_rows_o", [128, WAYS, G * CH], BF16, scope)
            sel_l = sb(name + "_sel_l", [128, 2, G * CH], BF16, scope)
            sel_o = sb(name + "_sel_o", [128, 2, G * CH], BF16, scope)
            hot = sb(name + "_hot", [128, 2, G, NT], F32, scope)
            prod = sb(name + "_prod", [128, G, H, NT], F32, scope)
            es = sb(name + "_es", [128, 2, G, H], F32, scope)
            ed = sb(name + "_ed", [128, 2, G, H], F32, scope)
            e_all = sb(name + "_e", [128, H, NI], F32, scope)
            hg = G // 2 if H > 1 else G
            nb = G // hg

            def rows_of(row, n):
                return row.rearrange("(o n) -> o n", o=1)[:, bass.ds(n * (G * CH), G * CH)].to_broadcast([128, G * CH])

            @block.sync
            def _(sp):
                sp.sem_inc(s_selected, WAYS)

                def load(n, b, r):
                    sp.wait_ge(s_selected, n + 1)
                    sp.dma_start(rows_l[:, b, :], rows_of(row_local, n)).then_inc(s_rows[b], 16)
                    sp.dma_start(rows_o[:, b, :], rows_of(row_other, n)).then_inc(s_rows[b], 16)

                staggered(sp, NG, ((load, 0),), ways=WAYS)

            @block.vector
            def _(dve):
                c = Chain(dve, s_c)
                v = nc.vector
                dve.sem_inc(s_summed, 2)

                def masked(n, b, r):
                    dve.wait_ge(s_looked, n + 3)
                    c.wait()
                    for k in range(nb):
                        c.step(v.tensor_tensor(prod[:, k * hg:(k + 1) * hg],
                                               bank[b % 2 * 2 + k][:, 0:hg * H * NT].rearrange("e (g h t) -> e g h t", g=hg, h=H),
                                               hot[:, b % 2, k * hg:(k + 1) * hg].unsqueeze(2).to_broadcast([128, hg, H, NT]), ALU.mult))

                def mark(n, b, r):
                    c.step(v.tensor_tensor(hot[:, b % 2], high[:, bass.ds(n * G, G)].unsqueeze(2).to_broadcast([128, G, NT]),
                                           col[:, 0:NT].unsqueeze(1).to_broadcast([128, G, NT]), ALU.is_equal))

                def source_term(n, b, r):
                    dve.wait_ge(s_summed, n + 1)
                    c.wait(1 if not isinstance(n, int) or n < NG - 1 else 0)
                    c.step(v.tensor_reduce(es[:, b % 2], prod[:], AX.X, ALU.add))

                def select_key(n, b, r):
                    dve.wait_ge(s_rows[b], r * 32 + 32)
                    dve.wait_ge(s_looked, n + 1)
                    v.tensor_scalar(sel_l[:, b % 2, :], rows_l[:, b, :], part[:], None, ALU.is_equal)

                def own_term(n, b, r):
                    c.step(v.tensor_reduce(ed[:, b % 2], bank[4 + b % 2][:, 0:G * 3 * H].rearrange("e (g m h) -> e g h m", m=3, h=H), AX.X, ALU.add))

                def select_other(n, b, r):
                    v.tensor_scalar(sel_o[:, b % 2, :], rows_o[:, b, :], part[:], None, ALU.is_equal).then_inc(s_selected, 1)

                def total(n, b, r):
                    c.wait()
                    v.tensor_tensor(e_all[:, :, bass.ds(n * G, G)], es[:, b % 2].rearrange("e g h -> e h g"),
                                    ed[:, b % 2].rearrange("e g h -> e h g"), ALU.add).then_inc(s_summed, 1)

                staggered(dve, NG, ((masked, 0), (mark, 1), (source_term, 0), (select_key, 2), (own_term, 0), (select_other, 2),
                                    (total, 0)), c, 3 + nb, ways=WAYS)
                c(dve.drain())
                c(v.scalar_tensor_tensor(e_all[:], e_all[:], 0.01, e_all[:], ALU.mult, ALU.max))

            @block.tensor
            def _(pe):
                pe.sem_inc(s_looked, 2)

                def lookups(n, b, tiles):
                    pe.wait_ge(s_selected, n + 1 + WAYS)
                    pe.wait_ge(s_summed, n + 1)
                    for k in range(G):
                        o = bank[b * 2 + k // hg][:, (k % hg) * H * NT:(k % hg + 1) * H * NT]
                        for m in range(3):
                            nc.tensor.matmul(o, sel_o[0:TN, b, k * CH:(k + 1) * CH], s_part[:, m, 0:H * NT],
                                             start=(m == 0), stop=(m == 2))
                    for k in range(G):
                        last = nc.tensor.matmul(bank[4 + b][:, k * 3 * H:(k + 1) * 3 * H], sel_l[0:TN, b, k * CH:(k + 1) * CH],
                                                d_part[:, bass.ds(tiles[k] * (3 * H), 3 * H)], start=True, stop=True)
                    last.then_inc(s_looked, 1)

                with pe.Fori(0, NG // 2) as i:
                    _, tiles = nc.values_load_multi_w_load_instructions(
                        it_d["tiles"][0:1, bass.ds(i * (2 * G), 2 * G)], engines=[mybir.EngineType.PE], min_val=0, max_val=NT - 1,
                        skip_runtime_bounds_check_because="the items' tiles are sums of at most NT marks, less one")
                    for b in range(2):
                        lookups(i * 2 + b, b, tiles[b * G:(b + 1) * G])

            fence(block, name + "_f1")
            L = IQ * CH
            e_t = sb(name + "_e_t", [IP, H, L], F32, scope)
            fwd = sb(name + "_fwd", [IP, H, L], F32, scope)
            bwd = sb(name + "_bwd", [IP, H, L], F32, scope)
            ends = sb(name + "_ends", [IP, 4, H], F32, scope)
            c_row = sb(name + "_c_row", [H, 4, IP], F32, scope)
            c_run = sb(name + "_c_run", [H, 2, IP], F32, scope)
            c_in = sb(name + "_c_in", [H, 2, IP], F32, scope)
            c_col = sb(name + "_c_col", [IP, 2, H], F32, scope)
            s_turned, s_terms, s_ends, s_ends_turned, s_carries, s_carries_turned, s_maxima, s_maxima_turned = (sem(name + f"_s{i}") for i in range(8))

            def scan(c, o, e, same, forward):
                turn = slice(None) if forward else slice(None, None, -1)
                for h in range(H):
                    c.step(nc.vector.tensor_tensor_scan(o[:, h, turn], same[:, turn], e[:, h, turn], -BIG, ALU.add, ALU.max))

            @block.tensor
            def _(pe):
                for h in range(H):
                    for q in range(IQ):
                        nc.tensor.transpose(bank[h][0:IP, q * CH:(q + 1) * CH],
                                            e_all[:, h, :].rearrange("e (p q) -> e q p", q=IQ)[:, q, :], ident[:])
                pe.drain().then_inc(s_turned, 1)
                pe.wait_ge(s_ends, 1)
                for k in range(4):
                    nc.tensor.transpose(bank[4][0:H, k * IP:(k + 1) * IP], ends[:, k, :], ident[0:IP, 0:IP])
                pe.drain().then_inc(s_ends_turned, 1)
                pe.wait_ge(s_carries, 1)
                for k in range(2):
                    nc.tensor.transpose(bank[5][0:IP, k * H:(k + 1) * H], c_in[:, k, :], ident[0:H, 0:H])
                pe.drain().then_inc(s_carries_turned, 1)
                pe.wait_ge(s_maxima, 1)
                for h in range(H):
                    for q in range(IQ):
                        nc.tensor.transpose(bank[h][:, q * IP:(q + 1) * IP], fwd[:, h, q * CH:(q + 1) * CH], ident[0:IP, 0:IP])
                pe.drain().then_inc(s_maxima_turned, 1)

            @block.scalar
            def _(act):
                act.wait_ge(s_turned, 1)
                for h in range(H):
                    nc.scalar.activation(e_t[:, h, :], bank[h][0:IP, :], ACT.Copy)
                act.drain().then_inc(s_terms, 1)

            @block.vector
            def _(dve):
                c = Chain(dve, sem(name + "_c2"))
                v = nc.vector
                dve.wait_ge(s_terms, 1)
                scan(c, fwd, e_t, same_f, True)
                scan(c, bwd, e_t, same_b, False)
                c.wait()
                c(v.tensor_copy(ends[:, 0, :], fwd[:, :, L - 1]))
                c(v.tensor_copy(ends[:, 1, :], bwd[:, :, 0]))
                c(v.tensor_copy(ends[:, 2:4, :], link[:, 2:4].unsqueeze(2).to_broadcast([IP, 2, H])))
                dve.drain().then_inc(s_ends, 1)
                dve.wait_ge(s_ends_turned, 1)
                c(v.tensor_copy(c_row[:], bank[4][0:H, 0:4 * IP].rearrange("h (k p) -> h k p", k=4)))
                c(v.tensor_tensor_scan(c_run[:, 0, :], c_row[:, 2, :], c_row[:, 0, :], -BIG, ALU.add, ALU.max))
                c(v.tensor_tensor_scan(c_run[:, 1, ::-1], c_row[:, 3, ::-1], c_row[:, 1, ::-1], -BIG, ALU.add, ALU.max))
                c(v.memset(c_in[:], -BIG))
                c(v.tensor_copy(c_in[:, 0, 1:IP], c_run[:, 0, 0:IP - 1]))
                c(v.tensor_copy(c_in[:, 1, 0:IP - 1], c_run[:, 1, 1:IP]))
                dve.drain().then_inc(s_carries, 1)
                dve.wait_ge(s_carries_turned, 1)
                for k, at in ((0, 0), (1, L - 1)):
                    c(v.tensor_scalar(c_col[:, k, :], bank[5][0:IP, k * H:(k + 1) * H], link[:, k:k + 1], None, ALU.add))
                    c(v.tensor_tensor(e_t[:, :, at], e_t[:, :, at], c_col[:, k, :], ALU.max))
                scan(c, fwd, e_t, same_f, True)
                scan(c, bwd, e_t, same_b, False)
                c.wait()
                c(v.tensor_tensor(fwd[:], fwd[:], bwd[:], ALU.max))
                dve.drain().then_inc(s_maxima, 1)
                dve.wait_ge(s_maxima_turned, 1)
                for h in range(H):
                    c(v.tensor_tensor(e_all[:, h, :].rearrange("e (p q) -> e q p", q=IQ),
                                      e_all[:, h, :].rearrange("e (p q) -> e q p", q=IQ),
                                      bank[h][:, 0:NI].rearrange("e (q p) -> e q p", q=IQ), ALU.subtract))

            fence(block, name + "_f2")

            @block.scalar
            def _(act):
                nc.scalar.activation(w_all[:, 0:NI * H].rearrange("e (n h) -> e h n", h=H), e_all[:], ACT.Exp)

        def aggregate(name, table, it, W, into, weight=None, heads=1, beside=None):
            RB = TURN if heads == 1 else 2 * TURN
            s_rows = [sem(name + f"_g{k}") for k in range(RB)]
            s_index, s_scaled_act, s_scaled_dve, s_sel, s_product, s_added, s_zeroed, s_turn = (
                sem(name + k) for k in ("_ix", "_half", "_use", "_sel", "_mm", "_add", "_z", "_turn"))
            IXB = 4
            UN = IXB * G
            BANKS = RING if beside is None else RING // 2
            HH = heads // 2
            with ExitStack() as scope:
                ix = sb(name + "_ixb", [128, UN], I32, scope)
                rows = sb(name + "_rowb", [128, RB, D + 1], F32, scope)
                sel = sb(name + "_selb", [128, RING, TN], F32, scope)
                scaled = sb(name + "_scl", [128, RING, W], F32, scope) if heads > 1 else None
                with nc.Block() as block:
                    other = None if beside is None else beside.place(block, scope)

                    @block.gpsimd
                    def _(pool):
                        def turn(i, begin=False):
                            for g in range(IXB):
                                pool.wait_ge(s_index, i * IXB + (g + 1))
                                pool.sem_inc(s_turn, 1)
                                for k in range(g * G, (g + 1) * G):
                                    if k % 4 == 0 and not (begin and k < RB):
                                        used = i * UN + (k + 4 - RB)
                                        if heads == 1:
                                            pool.wait_ge(s_product, used + RING)
                                        else:
                                            pool.wait_ge(s_scaled_dve, used)
                                            pool.wait_ge(s_scaled_act, used)
                                        pool.sem_inc(s_turn, 1)
                                    nc.gpsimd.indirect_dma_start(rows[:, k % RB, 0:D], None, table,
                                                                 bass.IndirectOffsetOnAxis(ap=ix[:, k:k + 1], axis=0)).then_inc(s_rows[k % RB], 16)
                        turn(0, True)
                        with pool.Fori(1, NI // UN) as i:
                            turn(i)

                    @block.scalar
                    def _(act):
                        def indices(i, g, begin=False):
                            if not begin:
                                act.wait_ge(s_product, (i - 1) * UN + ((g + 1) * G + RING))
                            nc.scalar.activation(ix[:, g * G:(g + 1) * G], it["index"][:, bass.ds((i * IXB + g) * G, G)], ACT.Copy).then_inc(s_index, 1)

                        def scale(n, k, r):
                            act.wait_ge(s_rows[k], r * 16 + 16)
                            act.wait_ge(s_product, n + 1)
                            nc.scalar.activation(scaled[:, k % RING, D:W], w_all[:, bass.ds(n * HEADS, HEADS)], ACT.Copy)
                            for h in range(HH):
                                last = nc.scalar.activation(scaled[:, k % RING, h * HID:(h + 1) * HID], rows[:, k, h * HID:(h + 1) * HID],
                                                            ACT.Copy, scale=w_all[:, bass.ds(n * HEADS + h, 1)])
                            last.then_inc(s_scaled_act, 1)

                        if heads == 1:
                            for g in range(IXB):
                                indices(0, g, True)
                            if beside is None:
                                with act.Fori(1, NI // UN) as i:
                                    for g in range(IXB):
                                        indices(i, g)
                            else:
                                other.free(act)

                                def with_tiles(i, begin=False):
                                    m = (i - 1) * 2
                                    indices(i, 0)
                                    if not begin:
                                        other.take(act, m - 1, 1, i - 2)
                                    other.bring(act, m)
                                    indices(i, 1)
                                    other.turned(act, m)
                                    indices(i, 2)
                                    other.take(act, m, 0, i - 1)
                                    other.bring(act, m + 1)
                                    indices(i, 3)
                                    other.turned(act, m + 1)

                                with_tiles(1, True)
                                with act.Fori(2, NI // UN) as i:
                                    with_tiles(i)
                                m = 2 * (NI // UN - 1)
                                other.bring(act, m)
                                other.take(act, m - 1, 1, m // 2 - 1)
                                other.turned(act, m)
                                other.take(act, m, 0, m // 2)
                        else:
                            for g in range(IXB):
                                indices(0, g, True)

                            with act.Fori(0, NI // UN - 1) as i:
                                for g in range(IXB):
                                    for k in range(g * G, (g + 1) * G):
                                        scale(i * UN + k, k % RB, i * (UN // RB) + k // RB)
                                    if g >= 1:
                                        indices(i + 1, g - 1)
                                indices(i + 1, IXB - 1)
                            i = NI // UN - 1
                            for k in range(UN):
                                scale(i * UN + k, k % RB, i * (UN // RB) + k // RB)

                    @block.vector
                    def _(dve):
                        nc.vector.memset(into, 0.0)
                        nc.vector.memset(rows[:, :, D:D + 1], 1.0)
                        dve.drain().then_inc(s_zeroed, 1)
                        dve.wait_ge(s_zeroed, 1)
                        dve.sem_inc(s_product, RING)
                        dve.sem_inc(s_added, BANKS)

                        def make(n, k, r):
                            dve.wait_ge(s_product, n + 1)
                            o = sel[:, k % RING, :]
                            if heads == 1:
                                nc.vector.tensor_scalar(o, col[:, 0:TN], it["local"][:, bass.ds(n, 1)],
                                                        weight[:, bass.ds(n, 1)], ALU.is_equal, ALU.mult).then_inc(s_sel, 1)
                            else:
                                nc.vector.tensor_scalar(o, col[:, 0:TN], it["local"][:, bass.ds(n, 1)],
                                                        None, ALU.is_equal).then_inc(s_sel, 1)
                                dve.wait_ge(s_rows[k], r * 16 + 16)
                                wv = w_all[:, bass.ds(n * HEADS + HH, HEADS - HH)]
                                nc.vector.tensor_tensor(scaled[:, k % RING, HH * HID:D].rearrange("e (h o) -> e h o", o=HID),
                                                        rows[:, k, HH * HID:D].rearrange("e (h o) -> e h o", o=HID),
                                                        wv.unsqueeze(2).to_broadcast([128, HEADS - HH, HID]), ALU.mult).then_inc(s_scaled_dve, 1)

                        def tiles_of(n):
                            return nc.values_load_multi_w_load_instructions(
                                it["tiles"][0:1, bass.ds(n, TURN)], engines=[mybir.EngineType.DVE], min_val=0, max_val=NT - 1,
                                skip_runtime_bounds_check_because="the items' tiles are sums of at most NT marks, less one")[1]

                        def add(n, k, t):
                            dve.wait_ge(s_product, n + (1 + RING))
                            dve.wait_ge(s_added, n + BANKS)
                            o = into[:, bass.ds(t * W, W)]
                            nc.vector.tensor_tensor(o, o, bank[k % BANKS][0:TN, 0:W], ALU.add).then_inc(s_added, 1)

                        for k in range(LEAD):
                            make(k, k, 0)
                        turns = NI // RB
                        with dve.Fori(0, turns - 1) as i:
                            for k in range(RB):
                                if k % TURN == 0:
                                    tiles = tiles_of(i * RB + k)
                                make(i * RB + (k + LEAD), (k + LEAD) % RB, i + (k + LEAD) // RB)
                                add(i * RB + k, k, tiles[k % TURN])
                        at = (turns - 1) * RB
                        for k in range(RB):
                            if k % TURN == 0:
                                tiles = tiles_of(at + k)
                            if k + LEAD < RB:
                                make(at + k + LEAD, k + LEAD, turns - 1)
                            add(at + k, k, tiles[k % TURN])

                    @block.tensor
                    def _(pe):
                        def product(i, k):
                            n = i * RB + k
                            o = bank[k % BANKS][0:TN, :]
                            pe.wait_ge(s_sel, n + 1)
                            pe.wait_ge(s_added, n + 1)
                            if heads == 1:
                                pe.wait_ge(s_rows[k], i * 16 + 16)
                                nc.tensor.matmul(o[:, 0:W], sel[:, k % RING, :], rows[:, k, 0:W], start=True, stop=True).then_inc(s_product, 1)
                            else:
                                pe.wait_ge(s_scaled_dve, n + 1)
                                pe.wait_ge(s_scaled_act, n + 1)
                                nc.tensor.matmul(o[:, 0:W], sel[:, k % RING, :], scaled[:, k % RING, :], start=True, stop=True).then_inc(s_product, 1)

                        def turn(i, begin=False, end=False):
                            for k in range(RB):
                                product(i, k)
                                if other is not None and 2 <= k < 2 + other.steps and not begin:
                                    other.multiply(pe, i - 1, k - 2)
                                if other is not None and k == RB - 6 and not end:
                                    other.transpose(pe, i)

                        turns = NI // RB
                        if other is None:
                            with pe.Fori(0, turns) as i:
                                turn(i)
                        else:
                            other.begin(pe)
                            turn(0, begin=True)
                            with pe.Fori(1, turns - 1) as i:
                                turn(i)
                            turn(turns - 1, end=True)
                end_stage()

        ROUNDS = EC // (2 * SH)
        part1, part2 = 7, 12

        def norm_step(act, n, b, flow):
            if isinstance(n, int) and n >= NT:
                return
            if isinstance(n, int) and n == 0:
                act.wait_ge(s_norm, 1)
            act.wait_ge(flow.s_turned, n + 1)
            nc.scalar.activation(flow.hbuf[:, b, :], x_flat[:, bass.ds(n * D, D)], ACT.Relu, scale=rstd[:, bass.ds(n, 1)],
                                 bias=shift[:, bass.ds(n, 1)]).then_inc(flow.s_input, 1)

        with ExitStack() as scope:
            with nc.Block() as block:
                s_norm = sem("norm")
                row_stats(block, "st1", s_norm)
                with ExitStack() as inner:
                    project(block, inner, "pr1", 1, w_aug[0], None, D + 2 * HEADS, ACT.Copy, attention_finish(HEADS),
                            table_store(z_tab), act_ahead=norm_step)
                    items(block, inner, "id", 1, rec_dst, cnt_d, it_d, True)

                @block.gpsimd
                def _(pool):
                    scatter("sc1", pool, rec_s, rec_src, 0, part1)

                fence(block, "f3")
                split_tables(block, "sp1", HEADS)
                fence(block, "f4")
                with ExitStack() as inner:
                    edge_softmax(block, inner, "es1", HEADS)
            end_stage()

        W = D + HEADS
        aggregate("ag1", z_tab, it_d, W, acc[:], heads=HEADS)

        with ExitStack() as scope:
            inv = sb("inv", [TN, NT, HEADS], F32, scope)
            up = sb("up", [TN, 2, D], F32, scope)
            neg = sb("neg", [TN, 2, D], F32, scope)
            ex = sb("ex", [TN, 2, D], F32, scope)
            s_mn, s_ex = sem("s_mn"), sem("s_ex")

            def prep_elu(dve, c, flow):
                v = nc.vector
                c(v.tensor_scalar(inv[:], acc[:].rearrange("p (t w) -> p t w", w=W)[:, :, D:W], 1e-30, None, ALU.max))
                c(v.reciprocal(inv[:], inv[:]))

                def ahead(n, b, r):
                    dve.wait_ge(flow.s_input, n + 1)
                    c(v.tensor_tensor(up[:, b, :].rearrange("p (h o) -> p h o", h=HEADS),
                                      acc[:, bass.ds(n * W, D)].rearrange("p (h o) -> p h o", h=HEADS),
                                      inv[:].rearrange("p t h -> p (t h)")[:, bass.ds(n * HEADS, HEADS)].unsqueeze(2).to_broadcast([TN, HEADS, HID]), ALU.mult))
                    v.tensor_scalar(neg[:, b, :], up[:, b, :], 0.0, None, ALU.min).then_inc(s_mn, 1)
                    c.step(v.tensor_scalar(up[:, b, :], up[:, b, :], 0.0, -1.0, ALU.max, ALU.add))

                def behind(n, b, r):
                    dve.wait_ge(flow.s_turned, n + 1)
                    dve.wait_ge(s_ex, n + 1)
                    c.wait(0 if isinstance(n, int) and n == NT - 1 else 2)
                    v.tensor_tensor(flow.hbuf[:, b, :], up[:, b, :], ex[:, b, :], ALU.add).then_inc(flow.s_input, 1)

                skewed(dve, NT, ahead, behind, c, 2)

            def exp_step(act, n, b, flow):
                if isinstance(n, int) and n >= NT:
                    return
                act.wait_ge(s_mn, n + 1)
                nc.scalar.activation(ex[:, b, :], neg[:, b, :], ACT.Exp).then_inc(s_ex, 1)

            with nc.Block() as block:
                @block.gpsimd
                def _(pool):
                    scatter("sc2", pool, rec_s, rec_src, part1, part2)

                with ExitStack() as inner:
                    project(block, inner, "pr2", 1, w_aug[1], None, D + 2, ACT.Copy, attention_finish(1), table_store(z2_tab),
                            prepare=prep_elu, act_ahead=exp_step)
                fence(block, "f5")
                split_tables(block, "sp2", 1)
                fence(block, "f6")
                with ExitStack() as inner:
                    edge_softmax(block, inner, "es2", 1)
            end_stage()

        W_ = D + 1
        aggregate("ag2", z2_tab, it_d, W_, acc[:, 0:NT * W_], weight=w_all)

        hb = sb("hb", [TN, NT, D])
        hb_flat = hb[:].rearrange("p t d -> p (t d)")
        a_out = sb("a_out", [TN, NT * D])
        sq = a_out[:].rearrange("p (t d) -> p t d", d=D)
        vec = sb("vec", [TN, 4, D])
        w_io = sb("w_io", [128, KD, 2 * D])
        w_g = sb("w_g", [128, 3 * KD, 2 * D])
        b_all = sb("b_all", [1, 4 * D])
        b_parts = sb("b_parts", [1, 3, 4 * D], BF16)
        b_rows = sb("b_rows", [3, 4 * D], BF16)
        ones16 = sb("ones16", [3, TN], BF16)
        b_io, b_g = b_rows[:, 0:2 * D], b_rows[:, 2 * D:4 * D]
        s_n, s_a = sem("bn_n"), sem("bn_a")
        PARTS = 5
        PT = NT // PARTS
        s_rc, s_c, s_p, s_p2, s_v, s_q, s_w = (sem("bn" + k) for k in ("_rc", "_c", "_p", "_p2", "_v", "_q", "_w"))
        with nc.Block() as block:
            @block.gpsimd
            def _(pool):
                scatter("sc3", pool, rec_s, rec_src, part2, ROUNDS)

            @block.sync
            def _(sp):
                for to, of in ((vec[:, 0, :], gamma.rearrange("(o d) -> o d", o=1).to_broadcast([TN, D])),
                               (vec[:, 1, :], beta.rearrange("(o d) -> o d", o=1).to_broadcast([TN, D])),
                               (w_io[:, :, 0:D], W_in.rearrange("(k p) n -> p k n", p=128)),
                               (w_io[:, :, D:2 * D], W_out.rearrange("(k p) n -> p k n", p=128)),
                               (w_g[:, 0:2 * KD, :], W_x2i.rearrange("(k p) n -> p k n", p=128)),
                               (w_g[:, 2 * KD:3 * KD, :], W_h2h.rearrange("(k p) n -> p k n", p=128)),
                               (b_all[:, 0:D], b_in.rearrange("(o d) -> o d", o=1)),
                               (b_all[:, D:2 * D], b_out.rearrange("(o d) -> o d", o=1)),
                               (b_all[:, 2 * D:4 * D], b_x2i.rearrange("(o d) -> o d", o=1))):
                    sp.dma_start(to, of).then_inc(s_w, 16)
                sp.wait_ge(s_w, 16 * 9)
                sp.wait_ge(s_v, 1)
                for k in range(3):
                    sp.dma_start(b_rows[k:k + 1, :], b_parts[:, k, :]).then_inc(s_w, 16)
                sp.wait_ge(s_w, 16 * 12)

            @block.vector
            def _(dve):
                c = Chain(dve, s_rc)
                a3 = acc[:, 0:NT * W_].rearrange("p (t w) -> p t w", w=W_)
                c(nc.vector.tensor_scalar(spread[:], a3[:, :, D], 1e-30, None, ALU.max))
                c(nc.vector.reciprocal(spread[:], spread[:]))
                with dve.Fori(0, NT // 5) as i:
                    for k in range(5):
                        t = i * 5 + k
                        xt = x_flat[:, bass.ds(t * D, D)]
                        nc.vector.scalar_tensor_tensor(xt, acc[:, bass.ds(t * W_, D)], spread[:, bass.ds(t, 1)], xt, ALU.mult, ALU.add)
                c(dve.drain())

            row_stats(block, "st2")

            @block.vector
            def _(dve):
                c = Chain(dve, s_c)
                v = nc.vector

                def tall(k, n):
                    return vec[:, k:k + 1, :].to_broadcast([TN, n, D])

                with dve.Fori(0, PARTS) as i:
                    for k in range(PT):
                        t = i * PT + k
                        v.tensor_scalar(hb_flat[:, bass.ds(t * D, D)], x_flat[:, bass.ds(t * D, D)], mean[:, bass.ds(t, 1)],
                                        rstd[:, bass.ds(t, 1)], ALU.subtract, ALU.mult)
                    dve.drain().then_inc(s_n, 1)
                dve.wait_ge(s_p, 1)
                c(v.tensor_scalar(vec[:, 2, :], bank[0][0:TN, 0:D], 1.0 / N, None, ALU.mult))
                for i in range(PARTS):
                    o = hb[:, i * PT:(i + 1) * PT, :]
                    v.tensor_tensor(o, o, tall(2, PT), ALU.subtract).then_inc(s_n, 1)
                dve.wait_ge(s_w, 16 * 9)
                v.memset(ones16[:], 1.0)
                for k in range(3):
                    c(v.tensor_copy(b_parts[:, k, :], b_all[:]))
                    if k < 2:
                        c(v.tensor_tensor(b_all[:], b_all[:], b_parts[:, k, :], ALU.subtract))
                dve.drain().then_inc(s_v, 1)
                dve.wait_ge(s_p2, 1)
                c(v.tensor_scalar(vec[:, 3, :], bank[1][0:TN, 0:D], 1.0 / N, None, ALU.mult))
                dve.drain().then_inc(s_v, 1)
                dve.wait_ge(s_q, 1)
                c(v.reciprocal(vec[:, 3, :], vec[:, 3, :]))
                c(v.tensor_tensor(vec[:, 3, :], vec[:, 3, :], vec[:, 0, :], ALU.mult))

            @block.scalar
            def _(act):
                for i in range(PARTS):
                    o = hb[:, i * PT:(i + 1) * PT, :]
                    act.wait_ge(s_n, i + 1)
                    nc.scalar.activation(o, o, ACT.Relu).then_inc(s_a, 1)
                for i in range(PARTS):
                    act.wait_ge(s_n, PARTS + i + 1)
                    nc.scalar.activation(sq[:, i * PT:(i + 1) * PT, :], hb[:, i * PT:(i + 1) * PT, :], ACT.Square).then_inc(s_a, 1)
                act.wait_ge(s_v, 2)
                nc.scalar.activation(vec[:, 3, :], vec[:, 3, :], ACT.Sqrt, bias=eps[0:TN, :]).then_inc(s_q, 1)

            @block.tensor
            def _(pe):
                for j, (t, done) in enumerate(((hb[:], s_p), (sq, s_p2))):
                    for i in range(PARTS):
                        pe.wait_ge(s_a, j * PARTS + i + 1)
                        for k in range(i * PT, (i + 1) * PT):
                            last = nc.tensor.matmul(bank[j][0:TN, 0:D], ones[0:TN, 0:TN], t[:, k, :], start=(k == 0), stop=(k == NT - 1))
                    last.then_inc(done, 1)

            fence(block, "f7")

            s_turn = sem("scaled_turn")

            def prep_scaled(dve, c, flow):
                def step(n, b, r):
                    h = hb_flat[:, bass.ds(n * D, D)]
                    c(nc.vector.tensor_tensor(h, h, vec[:, 3, :], ALU.mult))
                    c(nc.vector.tensor_tensor(h, h, vec[:, 1, :], ALU.add))
                    dve.wait_ge(flow.s_turned, n + 1)
                    dve.sem_inc(s_turn, 1)
                    nc.vector.tensor_copy(flow.hbuf[:, b, :], h).then_inc(flow.s_input, 1)
                alternate(dve, NT, step, c, 2)

            def io_finish(act, n, product, res):
                return nc.scalar.activation(res, product, ACT.Copy)

            with ExitStack() as inner:
                project(block, inner, "fp", 1, w_io, b_io[:, 0:D], D, ACT.Copy, io_finish, table_store(fin_tab), prepare=prep_scaled)
                items(block, inner, "is", 0, rec_src, cnt_s, it_s, False)
        end_stage()
        class Beside:

            def __init__(self, name, srcs, weights, bias, width, table):
                self.name, self.srcs, self.weights, self.bias, self.width, self.table = name, srcs, weights, bias, width, table
                self.K = KD * len(srcs)
                self.steps = self.K + 1

            def place(self, block, scope):
                name = self.name
                self.rows = sb(name + "_rows", [TN, self.K * 128], F32, scope)
                self.cols = sb(name + "_cols", [128, self.K, TN], F32, scope)
                self.res = sb(name + "_res", [TN, 2, self.width], F32, scope)
                self.s_input, self.s_turned, self.s_cols, self.s_product, self.s_taken = (
                    sem(name + k) for k in ("_in", "_tr", "_cols", "_prod", "_res"))
                self.s_stored = [sem(name + f"_w{b}") for b in range(2)]

                @block.sync
                def _(sp):
                    for b in range(2):
                        sp.sem_inc(self.s_stored[b], 16)

                    def step(m, b, r):
                        sp.wait_ge(self.s_taken, m + 2)
                        sp.dma_start(self.table[bass.ds(m * TN, TN), :], self.res[:, b, :]).then_inc(self.s_stored[b], 16)

                    alternate(sp, NT, step)
                    for b in range(2):
                        sp.wait_ge(self.s_stored[b], 16 + 16 * ((NT + 1 - b) // 2))
                return self

            def free(self, act):
                act.sem_inc(self.s_cols, 1)
                act.sem_inc(self.s_taken, 1)

            def bring(self, act, m):
                act.wait_ge(self.s_turned, m + 1)
                for i, of in enumerate(self.srcs):
                    last = nc.scalar.activation(self.rows[:, i * D:(i + 1) * D], of[:, bass.ds(m * D, D)], ACT.Copy)
                last.then_inc(self.s_input, 1)

            def turned(self, act, m):
                act.wait_ge(self.s_turned, m + 2)
                act.wait_ge(self.s_product, m + 1)
                nc.scalar.activation(self.cols[:], bank[6][:, 0:self.K * TN].rearrange("p (k n) -> p k n", k=self.K), ACT.Copy).then_inc(self.s_cols, 1)

            def take(self, act, m, b, r):
                act.wait_ge(self.s_product, m + 2)
                act.wait_ge(self.s_stored[b], r * 16 + 16)
                nc.scalar.activation(self.res[:, b, :], bank[7][0:TN, 0:self.width], ACT.Copy).then_inc(self.s_taken, 1)

            def begin(self, pe):
                pe.sem_inc(self.s_turned, 1)
                pe.sem_inc(self.s_product, 1)

            def transpose(self, pe, m):
                pe.wait_ge(self.s_input, m + 1)
                pe.wait_ge(self.s_cols, m + 1)
                for k in range(self.K):
                    last = nc.tensor.transpose(bank[6][:, k * TN:(k + 1) * TN], self.rows[:, k * 128:(k + 1) * 128], ident[0:TN, 0:TN])
                last.then_inc(self.s_turned, 1)

            def multiply(self, pe, m, step):
                if step == 0:
                    pe.wait_ge(self.s_cols, m + 2)
                    pe.wait_ge(self.s_taken, m + 1)
                    nc.tensor.matmul(bank[7][0:TN, 0:self.width], ones16[:], self.bias, start=True, stop=False)
                    return
                k = step - 1
                last = nc.tensor.matmul(bank[7][0:TN, 0:self.width], self.cols[:, k, :], self.weights[k], start=False, stop=(k == self.K - 1))
                if k == self.K - 1:
                    last.then_inc(self.s_product, 1)

        aggregate("ag3", fin_tab, it_d, D, acc[:, 0:NT * D], weight=it_d["weight"],
                  beside=Beside("fout", [hb_flat], [w_io[:, k, D:2 * D] for k in range(KD)], b_io[:, D:2 * D], D, fout_tab))

        gate_tab = dram("gate_tab", (N, 2 * D))
        aggregate("ag4", fout_tab, it_s, D, a_out[:], weight=it_s["weight"], 
                  beside=Beside("gates", [acc[:, 0:NT * D], hb_flat], [w_g[:, k, :] for k in (0, 1, 2 * KD, 2 * KD + 1)],
                                b_g, 2 * D, gate_tab))

        with ExitStack() as scope:
            rows = sb("gru_rows", [TN, 2, D], F32, scope)
            cols = sb("gru_cols", [128, 2, KD, TN], F32, scope)
            base = sb("gru_base", [TN, 2, 2 * D], F32, scope)
            total = sb("gru_total", [TN, 2, 2 * D], F32, scope)
            gate = sb("gru_gate", [TN, 2, 2 * D], F32, scope)
            outb = sb("gru_outb", [TN, 2, D], F32, scope)
            s_input, s_turned, s_cols, s_product, s_total, s_gate, s_state, s_out, s_c = (sem("gru" + k) for k in (
                "_in", "_tr", "_cols", "_prod", "_sum", "_gate", "_fin", "_out", "_c"))
            s_loaded, s_stored = ([sem(f"gru_{k}{b}") for b in range(2)] for k in ("load", "store"))
            with nc.Block() as block:
                @block.sync
                def _(sp):
                    for b in range(2):
                        sp.sem_inc(s_stored[b], 16)

                    def load(n, b, r):
                        sp.wait_ge(s_total, n + 1)
                        sp.dma_start(base[:, b, :], gate_tab[bass.ds(n * TN, TN), :]).then_inc(s_loaded[b], 16)

                    def store(n, b, r):
                        sp.wait_ge(s_out, n + 1)
                        sp.dma_start(out[bass.ds(n * TN, TN), :], outb[:, b, :]).then_inc(s_stored[b], 16)

                    staggered(sp, NT, ((load, 3), (store, 0)))
                    for b in range(2):
                        sp.wait_ge(s_stored[b], 16 + 16 * ((NT + 1 - b) // 2))

                @block.gpsimd
                def _(pool):
                    def residual(n, b, r):
                        pool.wait_ge(s_state, n + 3)
                        nc.gpsimd.tensor_tensor(outb[:, b, :], outb[:, b, :], x_flat[:, bass.ds(n * D, D)], ALU.add).then_inc(s_out, 1)

                    alternate(pool, NT, residual)

                @block.tensor
                def _(pe):
                    pe.sem_inc(s_turned, 2)
                    pe.sem_inc(s_product, 2)

                    def turn(n, b, r):
                        pe.wait_ge(s_input, n + 1)
                        pe.wait_ge(s_cols, n + 1)
                        for k in range(KD):
                            last = nc.tensor.transpose(bank[b][:, k * TN:(k + 1) * TN], rows[:, b, k * 128:(k + 1) * 128], ident[0:TN, 0:TN])
                        last.then_inc(s_turned, 1)

                    def product(n, b, r):
                        pe.wait_ge(s_cols, n + 3)
                        pe.wait_ge(s_total, n + 1)
                        for k in range(KD):
                            last = nc.tensor.matmul(bank[2 + b][0:TN, :], cols[:, b, k, :], w_g[:, KD + k, :], start=(k == 0), stop=(k == KD - 1))
                        last.then_inc(s_product, 1)

                    skewed(pe, NT, turn, product)

                @block.scalar
                def _(act):
                    act.sem_inc(s_gate, 2)

                    def gates(n, b, r):
                        act.wait_ge(s_total, n + 3)
                        act.wait_ge(s_state, n + 1)
                        nc.scalar.activation(gate[:, b, 0:D], total[:, b, 0:D], ACT.Sigmoid)
                        nc.scalar.activation(gate[:, b, D:2 * D], total[:, b, D:2 * D], ACT.Tanh).then_inc(s_gate, 1)

                    def bring(n, b, r):
                        act.wait_ge(s_turned, n + 1)
                        nc.scalar.activation(rows[:, b, :], a_out[:, bass.ds(n * D, D)], ACT.Copy).then_inc(s_input, 1)

                    staggered(act, NT, ((gates, 0), (bring, 3)))

                @block.vector
                def _(dve):
                    dve.sem_inc(s_total, 2)
                    dve.sem_inc(s_state, 2)
                    dve.sem_inc(s_cols, 2)
                    c = Chain(dve, s_c)
                    v = nc.vector

                    def turned(n, b, r):
                        dve.wait_ge(s_turned, n + 3)
                        dve.wait_ge(s_product, n + 1)
                        v.tensor_copy(cols[:, b], bank[b][:, 0:KD * TN].rearrange("p (k n) -> p k n", k=KD)).then_inc(s_cols, 1)

                    def totals(n, b, r):
                        dve.wait_ge(s_product, n + 3)
                        dve.wait_ge(s_loaded[b], r * 16 + 16)
                        dve.wait_ge(s_gate, n + 1)
                        v.tensor_tensor(total[:, b, :], base[:, b, :], bank[2 + b][0:TN, :], ALU.add).then_inc(s_total, 1)

                    def state(n, b, r):
                        dve.wait_ge(s_gate, n + 3)
                        dve.wait_ge(s_stored[b], r * 16 + 16)
                        o, keep, new = outb[:, b, :], gate[:, b, 0:D], gate[:, b, D:2 * D]
                        c(v.tensor_tensor(o, hb_flat[:, bass.ds(n * D, D)], new, ALU.subtract))
                        c(v.tensor_tensor(o, o, keep, ALU.mult))
                        v.tensor_tensor(o, o, new, ALU.add).then_inc(s_state, 1)

                    staggered(dve, NT, ((turned, 2), (totals, 1), (state, 0)), c, 2)
            end_stage()


_INS = ["x", "src", "dst", "edge_weight", "edge_weight_n2", "L0_gnn_W1", "L0_gnn_a1", "L0_gnn_W2", "L0_gnn_a2",
        "L1_gnn_gamma", "L1_gnn_beta", "L1_gnn_W_in", "L1_gnn_b_in", "L1_gnn_W_out", "L1_gnn_b_out",
        "L1_gnn_W_x2i", "L1_gnn_b_x2i", "L1_gnn_W_h2h"]


def kernel(**inputs):
    import numpy as np
    import concourse.bacc as bacc
    from concourse.bass_utils import run_bass_kernel_spmd

    nc = bacc.Bacc("TRN2", target_bir_lowering=False, num_devices=1)
    arrays, args = {}, []
    for name in _INS:
        a = np.ascontiguousarray(inputs[name])
        arrays[f"in_{name}"] = a
        args.append(nc.dram_tensor(f"in_{name}", a.shape, mybir.dt.from_np(a.dtype), kind="ExternalInput").ap())
    out = nc.dram_tensor("out", (N, D), F32, kind="ExternalOutput").ap()
    build(nc, *args, out)
    r = run_bass_kernel_spmd(nc, [arrays], core_ids=[0])
    return r.results[0]["out"]
```
